# Optimizing a Trainium2 kernel written in Bass

```python
import numpy as np
import jax
import jax.numpy as jnp

def _softmax(x, axis=-1):
    return jax.nn.softmax(x, axis=axis)

def _gelu(x):
    return jax.nn.gelu(x, approximate=True)

def _silu(x):
    return jax.nn.silu(x)

def _sigmoid(x):
    return jax.nn.sigmoid(x)

def _layernorm(x, axis=-1, eps=1e-05):
    m = jnp.mean(x, axis=axis, keepdims=True)
    v = jnp.var(x, axis=axis, keepdims=True)
    return (x - m) / jnp.sqrt(v + eps)

def _scatter_add(tgt, idx, src, axis=0):
    return tgt.at[idx].add(src)

def _segment_sum(src, seg, n):
    return jax.ops.segment_sum(src, seg, n)
kernel_name = 'mk_gnn_resnorm_d4_gnn_r8_acb6c2'

def setup_inputs(seed: int=0):
    np.random.seed(seed)
    _w = jnp.asarray

    def _rec_inputs():
        import jax
        import jax.numpy as jnp
        _gk = jax.random.key(seed)
        x = -0.0003019 + 1 * jax.random.normal(jax.random.fold_in(_gk, 1), (1250, 1024), jnp.float32)
        src = jax.random.randint(jax.random.fold_in(_gk, 2), (40000,), 0, 1250, jnp.int32)
        dst = jnp.minimum((1250 * jax.random.uniform(jax.random.fold_in(_gk, 3), (40000,)) ** 2.0).astype(jnp.int32), 9999)
        _o = jnp.argsort(dst, stable=True)
        src = src[_o]
        dst = dst[_o]
        edge_weight = -0.000130211 + 0.031236 * jax.random.normal(jax.random.fold_in(_gk, 13), (40000,), jnp.float32)
        return (x, src, dst, edge_weight)
    x, src, dst, edge_weight = _rec_inputs()

    def _L0_gnn_setup():
        import jax, jax.numpy as jnp
        import numpy as np
        N = 2500
        E = 40000
        IN = 1024
        HID = 256
        H = 4
        D = HID // H
        OUT = 1024
        EPS = 1e-06
        NEG_SLOPE = 0.2
        key = jax.random.key(seed)
        ks = jax.random.split(key, 8)
        x = jax.random.normal(ks[0], (N, IN), dtype=jnp.float32)
        edge_index = jax.random.randint(ks[1], (2, E), 0, N, dtype=jnp.int64)
        s = 0.02
        return {'x': x, 'edge_index': edge_index, 'rms_w': jnp.ones((IN,), dtype=jnp.float32), 'W_down': jax.random.normal(ks[2], (IN, HID), dtype=jnp.float32) * s, 'Wl': jax.random.normal(ks[3], (HID, HID), dtype=jnp.float32) * s, 'Wr': jax.random.normal(ks[4], (HID, HID), dtype=jnp.float32) * s, 'att': jax.random.normal(ks[5], (H, D), dtype=jnp.float32) * s, 'W_up': jax.random.normal(ks[6], (HID, OUT), dtype=jnp.float32) * s}
    _L0_gnn_all = _L0_gnn_setup()
    _L0_gnn_in = {k: v for k, v in _L0_gnn_all.items() if k in ('rms_w', 'W_down', 'Wl', 'Wr', 'att', 'W_up')}
    del _L0_gnn_all

    def _L1_gnn_setup():
        import jax, jax.numpy as jnp
        import numpy as np
        N_NODES = 3125
        N_EDGES = 50000
        D = 1024

        def _sage_layer(h, edge_src, edge_dst, deg_inv, W_self, W_neigh, b):
            msg = h[edge_src]
            agg = jax.ops.segment_sum(msg, edge_dst, num_segments=h.shape[0])
            mean = agg * deg_inv[:, None]
            return h @ W_self + mean @ W_neigh + b
        key = jax.random.key(seed)
        ks = jax.random.split(key, 8)
        s = 1.0 / np.sqrt(D)
        return {'x': jax.random.normal(ks[0], (N_NODES, D), dtype=jnp.float32), 'edge_src': jax.random.randint(ks[1], (N_EDGES,), 0, N_NODES, dtype=jnp.int32), 'edge_dst': jax.random.randint(ks[2], (N_EDGES,), 0, N_NODES, dtype=jnp.int32), 'W_self0': jax.random.normal(ks[3], (D, D), dtype=jnp.float32) * s, 'W_neigh0': jax.random.normal(ks[4], (D, D), dtype=jnp.float32) * s, 'b0': jnp.zeros((D,), dtype=jnp.float32), 'W_self1': jax.random.normal(ks[5], (D, D), dtype=jnp.float32) * s, 'W_neigh1': jax.random.normal(ks[6], (D, D), dtype=jnp.float32) * s, 'b1': jnp.zeros((D,), dtype=jnp.float32)}
    _L1_gnn_all = _L1_gnn_setup()
    _L1_gnn_in = {k: v for k, v in _L1_gnn_all.items() if k in ('W_self0', 'W_neigh0', 'b0', 'W_self1', 'W_neigh1', 'b1')}
    del _L1_gnn_all

    def _L2_gnn_setup():
        import jax, jax.numpy as jnp
        import numpy as np
        INDIM = 1024
        OUTDIM = 1024
        NNZ = 8192
        N = 6250
        key = jax.random.key(seed)
        k1, k2, k3, k4, k5 = jax.random.split(key, 5)
        x = jax.random.normal(k1, (N, INDIM), dtype=jnp.float32)
        stdv = np.sqrt(6.0 / (INDIM + OUTDIM))
        nnz_weight = jax.random.uniform(k2, (NNZ,), dtype=jnp.float32, minval=-stdv, maxval=stdv)
        bias = jax.random.normal(k3, (OUTDIM,), dtype=jnp.float32) * 0.02
        row = jax.random.randint(k4, (NNZ,), 0, OUTDIM, dtype=jnp.int64)
        col = jax.random.randint(k5, (NNZ,), 0, INDIM, dtype=jnp.int64)
        edge_index = jnp.stack([row, col])
        return {'x': x, 'nnz_weight': nnz_weight, 'bias': bias, 'edge_index': edge_index}
    _L2_gnn_all = _L2_gnn_setup()
    _L2_gnn_in = {k: v for k, v in _L2_gnn_all.items() if k in ('bias',)}
    del _L2_gnn_all

    def _L3_gnn_setup():
        import math
        import jax, jax.numpy as jnp
        import numpy as np
        N_NODES = 625
        N_EDGES = 20000
        D_IN = 1024
        D_OUT = 1024
        BN_EPS = 1e-05

        def _positional_encoding(n, d):
            pos = jnp.arange(n, dtype=jnp.float32)[:, None]
            div = jnp.exp(jnp.arange(0, d, 2, dtype=jnp.float32) * (-math.log(10000.0) / d))
            ang = pos * div
            pe = jnp.stack([jnp.sin(ang), jnp.cos(ang)], axis=-1).reshape(n, d)
            return pe

        def _gcn_conv(x, W, b, src, dst, dinv):
            xw = x @ W
            norm = (dinv[src] * dinv[dst])[:, None]
            agg = jax.ops.segment_sum(xw[src] * norm, dst, num_segments=x.shape[0])
            agg = agg + xw * (dinv * dinv)[:, None]
            return agg + b
        key = jax.random.key(seed)
        ks = jax.random.split(key, 8)
        x = jax.random.normal(ks[0], (N_NODES, D_IN), dtype=jnp.float32)
        src = jax.random.randint(ks[1], (N_EDGES,), 0, N_NODES, dtype=jnp.int32)
        dst = jax.random.randint(ks[2], (N_EDGES,), 0, N_NODES, dtype=jnp.int32)
        s1 = 1.0 / math.sqrt(D_IN)
        s2 = 1.0 / math.sqrt(D_OUT)
        W1 = jax.random.uniform(ks[3], (D_IN, D_OUT), jnp.float32, -s1, s1)
        b1 = jnp.zeros((D_OUT,), jnp.float32)
        gamma = jnp.ones((D_OUT,), jnp.float32)
        beta = jnp.zeros((D_OUT,), jnp.float32)
        W2 = jax.random.uniform(ks[4], (D_OUT, D_OUT), jnp.float32, -s2, s2)
        b2 = jnp.zeros((D_OUT,), jnp.float32)
        return {'x': x, 'src': src, 'dst': dst, 'W1': W1, 'b1': b1, 'gamma': gamma, 'beta': beta, 'W2': W2, 'b2': b2}
    _L3_gnn_all = _L3_gnn_setup()
    _L3_gnn_in = {k: v for k, v in _L3_gnn_all.items() if k in ('W1', 'b1', 'gamma', 'beta', 'W2', 'b2')}
    del _L3_gnn_all
    return {'x': x, 'src': src, 'dst': dst, 'edge_weight': edge_weight, 'L0_gnn_rms_w': _L0_gnn_in['rms_w'], 'L0_gnn_W_down': _L0_gnn_in['W_down'], 'L0_gnn_Wl': _L0_gnn_in['Wl'], 'L0_gnn_Wr': _L0_gnn_in['Wr'], 'L0_gnn_att': _L0_gnn_in['att'], 'L0_gnn_W_up': _L0_gnn_in['W_up'], 'L1_gnn_W_self0': _L1_gnn_in['W_self0'], 'L1_gnn_W_neigh0': _L1_gnn_in['W_neigh0'], 'L1_gnn_b0': _L1_gnn_in['b0'], 'L1_gnn_W_self1': _L1_gnn_in['W_self1'], 'L1_gnn_W_neigh1': _L1_gnn_in['W_neigh1'], 'L1_gnn_b1': _L1_gnn_in['b1'], 'L2_gnn_bias': _L2_gnn_in['bias'], 'L3_gnn_W1': _L3_gnn_in['W1'], 'L3_gnn_b1': _L3_gnn_in['b1'], 'L3_gnn_gamma': _L3_gnn_in['gamma'], 'L3_gnn_beta': _L3_gnn_in['beta'], 'L3_gnn_W2': _L3_gnn_in['W2'], 'L3_gnn_b2': _L3_gnn_in['b2']}

def reference(x, src, dst, edge_weight, L0_gnn_rms_w, L0_gnn_W_down, L0_gnn_Wl, L0_gnn_Wr, L0_gnn_att, L0_gnn_W_up, L1_gnn_W_self0, L1_gnn_W_neigh0, L1_gnn_b0, L1_gnn_W_self1, L1_gnn_W_neigh1, L1_gnn_b1, L2_gnn_bias, L3_gnn_W1, L3_gnn_b1, L3_gnn_gamma, L3_gnn_beta, L3_gnn_W2, L3_gnn_b2):
    import jax
    import jax.numpy as jnp

    def _L0_gnn_ref(x, edge_index, rms_w, W_down, Wl, Wr, att, W_up):
        import jax, jax.numpy as jnp
        import numpy as np
        N = 2500
        E = 40000
        IN = 1024
        HID = 256
        H = 4
        D = HID // H
        OUT = 1024
        EPS = 1e-06
        NEG_SLOPE = 0.2
        n = x.shape[0]
        ms = jnp.mean(jnp.square(x), axis=-1, keepdims=True)
        x = x * jax.lax.rsqrt(ms + EPS) * rms_w
        x = x @ W_down
        loop = jnp.arange(n, dtype=edge_index.dtype)
        src = jnp.concatenate([edge_index[0], loop])
        dst = jnp.concatenate([edge_index[1], loop])
        xl = (x @ Wl).reshape(n, H, D)
        xr = (x @ Wr).reshape(n, H, D)
        msg = xl[src] + xr[dst]
        act = jnp.where(msg > 0, msg, NEG_SLOPE * msg)
        e = jnp.einsum('ehd,hd->eh', act, att)
        m = jax.ops.segment_max(e, dst, num_segments=n)
        p = jnp.exp(e - m[dst])
        denom = jax.ops.segment_sum(p, dst, num_segments=n)
        alpha = p / (denom[dst] + 1e-16)
        out = jax.ops.segment_sum(alpha[..., None] * xl[src], dst, num_segments=n)
        out = out.reshape(n, HID)
        return out @ W_up

    def _L1_gnn_ref(x, edge_src, edge_dst, W_self0, W_neigh0, b0, W_self1, W_neigh1, b1):
        import jax, jax.numpy as jnp
        import numpy as np
        N_NODES = 3125
        N_EDGES = 50000
        D = 1024

        def _sage_layer(h, edge_src, edge_dst, deg_inv, W_self, W_neigh, b):
            msg = h[edge_src]
            agg = jax.ops.segment_sum(msg, edge_dst, num_segments=h.shape[0])
            mean = agg * deg_inv[:, None]
            return h @ W_self + mean @ W_neigh + b
        N = x.shape[0]
        deg = jax.ops.segment_sum(jnp.ones_like(edge_dst, dtype=x.dtype), edge_dst, num_segments=N)
        deg_inv = 1.0 / jnp.maximum(deg, 1.0)
        h = jax.nn.relu(_sage_layer(x, edge_src, edge_dst, deg_inv, W_self0, W_neigh0, b0))
        out = _sage_layer(h, edge_src, edge_dst, deg_inv, W_self1, W_neigh1, b1)
        return out

    def _L2_gnn_ref(x, nnz_weight, bias, edge_index):
        import jax, jax.numpy as jnp
        import numpy as np
        INDIM = 1024
        OUTDIM = 1024
        NNZ = 8192
        N = 6250
        row, col = (edge_index[0], edge_index[1])
        W = jnp.zeros((OUTDIM, INDIM), dtype=nnz_weight.dtype).at[row, col].add(nnz_weight)
        return x @ W.T + bias

    def _L3_gnn_ref(x, src, dst, W1, b1, gamma, beta, W2, b2):
        import math
        import jax, jax.numpy as jnp
        import numpy as np
        N_NODES = 625
        N_EDGES = 20000
        D_IN = 1024
        D_OUT = 1024
        BN_EPS = 1e-05

        def _positional_encoding(n, d):
            pos = jnp.arange(n, dtype=jnp.float32)[:, None]
            div = jnp.exp(jnp.arange(0, d, 2, dtype=jnp.float32) * (-math.log(10000.0) / d))
            ang = pos * div
            pe = jnp.stack([jnp.sin(ang), jnp.cos(ang)], axis=-1).reshape(n, d)
            return pe

        def _gcn_conv(x, W, b, src, dst, dinv):
            xw = x @ W
            norm = (dinv[src] * dinv[dst])[:, None]
            agg = jax.ops.segment_sum(xw[src] * norm, dst, num_segments=x.shape[0])
            agg = agg + xw * (dinv * dinv)[:, None]
            return agg + b
        n = x.shape[0]
        x = x + _positional_encoding(n, x.shape[1])
        deg = jax.ops.segment_sum(jnp.ones_like(dst, dtype=x.dtype), dst, num_segments=n) + 1.0
        dinv = deg ** (-0.5)
        h = _gcn_conv(x, W1, b1, src, dst, dinv)
        mu = h.mean(axis=0)
        var = h.var(axis=0)
        h = (h - mu) * jax.lax.rsqrt(var + BN_EPS) * gamma + beta
        h = jax.nn.relu(h)
        h = _gcn_conv(h, W2, b2, src, dst, dinv)
        return jax.nn.relu(h)
    edge_index = jnp.stack([src, dst])
    x = _layernorm(x + _L0_gnn_ref(x, edge_index, L0_gnn_rms_w, L0_gnn_W_down, L0_gnn_Wl, L0_gnn_Wr, L0_gnn_att, L0_gnn_W_up), axis=-1)
    x = _layernorm(x + _L1_gnn_ref(x, src, dst, L1_gnn_W_self0, L1_gnn_W_neigh0, L1_gnn_b0, L1_gnn_W_self1, L1_gnn_W_neigh1, L1_gnn_b1), axis=-1)
    x = _layernorm(x + _L2_gnn_ref(x, edge_weight, L2_gnn_bias, edge_index), axis=-1)
    x = _layernorm(x + _L3_gnn_ref(x, src, dst, L3_gnn_W1, L3_gnn_b1, L3_gnn_gamma, L3_gnn_beta, L3_gnn_W2, L3_gnn_b2), axis=-1)
    return x

_drawn_inputs = setup_inputs


def setup_inputs(seed=0):
    import zlib

    import numpy as np

    out = dict(_drawn_inputs(seed))
    spreads = {'L0_gnn_rms_w': (1.0, 0.6),
     'L1_gnn_b0': (0.0, 0.1),
     'L1_gnn_b1': (0.0, 0.1),
     'L3_gnn_b1': (0.0, 0.8),
     'L3_gnn_gamma': (1.0, 0.2),
     'L3_gnn_beta': (0.0, 0.34),
     'L3_gnn_b2': (0.0, 0.1)}
    factors = {'L0_gnn_W_down': 4.321,
     'L0_gnn_Wl': 4.333,
     'L0_gnn_Wr': 8.0,
     'L0_gnn_att': 8.0,
     'L0_gnn_W_up': 4.324,
     'L2_gnn_bias': 2.849}
    for name, (base, spread) in spreads.items():
        noise = np.random.default_rng([zlib.crc32(name.encode()), seed]).standard_normal(out[name].shape)
        drawn = base * np.exp(spread * noise) if base else spread * noise
        out[name] = jnp.asarray(drawn.astype(out[name].dtype))
    for name, factor in factors.items():
        out[name] = (out[name] * factor).astype(out[name].dtype)
    return out
```

```python
from contextlib import ExitStack

import concourse.bass as bass
from concourse import mybir

F32 = mybir.dt.float32
F32R = mybir.dt.float32r
BF16 = mybir.dt.bfloat16
F16 = mybir.dt.float16
I32 = mybir.dt.int32
ALU = mybir.AluOpType
ACT = mybir.ActivationFunctionType
AX = mybir.AxisListType

P = 128
N_NODES = 1250
N_EDGES = 40000
D = 1024
HID = 256
HEADS = 4
HD = HID // HEADS
HW = HD + 1
XW = HEADS * HW
NT = -(-N_NODES // P)
NPAD = NT * P
KT = D // P

EP = 125
EC = N_EDGES // EP
CH = 4
GE = CH * P
NG = (N_EDGES + NT * (GE - 1)) // GE
NG += NG % 2
NC = NG * CH
NO_DST = 200.0

LN_EPS = 1e-5
BIG = 1e38


def identity(pool, t, n, filled, made):
    pool.memset(t, 0.0).then_inc(filled, 1)
    pool.wait_ge(filled, 1)
    pool.affine_select(out=t, in_=t, compare_op=ALU.not_equal, fill=1.0, base=0,
                       pattern=[[-1, n]], channel_multiplier=1).then_inc(made, 1)


def prepare_phase(nc, sem, x, src, dst, edge_weight, rms_w, w_down, wl, wr, att,
                  edge_tab, xl_tab, self_tab, xr_tab, tile_tab):
    with ExitStack() as ctx:
        def sb(name, shape, dt):
            return ctx.enter_context(nc.sbuf_tensor("pr_" + name, shape, dt))

        def ps(name, shape):
            return ctx.enter_context(nc.psum_tensor("pr_" + name, shape, F32))

        src_i = sb("src_i", [EP, EC], I32)
        dst_i = sb("dst_i", [EP, EC], I32)
        wgt = sb("wgt", [EP, EC], F32)
        bucket_i = sb("bucket_i", [EP, EC], I32)
        local_i = sb("local_i", [EP, EC], I32)
        bucket = sb("bucket", [EP, EC], F32)
        mask = sb("mask", [EP, NT, EC], F32)
        rank = sb("rank", [EP, NT, EC], F32)
        zeros = sb("zeros", [EP, EC], F32)
        total = sb("total", [EP, NT], F32)
        before = sb("before", [EP, P], F32)
        ones = sb("ones", [P, P], F32)
        count_f = sb("count_f", [P, NT], F32)
        count_i = sb("count_i", [P, NT], I32)
        groups = sb("groups", [P, NT], F32)
        zeros10 = sb("zeros10", [P, NT], F32)
        group_end = sb("group_end", [P, NT], F32)
        base = sb("base", [EP, NT], F32)
        slot = sb("slot", [EP, EC], F32)
        part = sb("part", [EP, EC], F32)
        slot_i = sb("slot_i", [EP, EC], I32)
        record = sb("record", [EP, EC, 4], F32)
        unused = sb("unused", [P, NC, 4], F32)
        iota_g = sb("iota_g", [1, NG], F32)
        tile_f = sb("tile_f", [1, NG], F32)
        tile_i = sb("tile_i", [1, NG], I32)
        SC = 8
        slot_st = sb("slot_st", [EP, 2, SC], I32)
        rec_st = sb("rec_st", [EP, 2, SC * 4], F32)
        ident = sb("ident", [P, P], F32)
        xin = sb("xin", [P, 2, D], F32)
        sq = sb("sq", [P, D], F32)
        ssq = sb("ssq", [P, 2], F32)
        ms = sb("ms", [P, 1], F32)
        rms = sb("rms", [P, 1], F32)
        rinv = sb("rinv", [P, 1], F32)
        xT = sb("xT", [P, D], F32)
        wd = sb("wd", [P, KT, HID], F32)
        rw = sb("rw", [P, KT], F32)
        wlr = sb("wlr", [P, 2, 2 * HID], F32)
        xd = sb("xd", [P, HID], F32)
        xdT = sb("xdT", [P, HID], F32)
        xl = sb("xl", [P, 2, XW], F32)
        xr = sb("xr", [P, 2, HID], F32)
        att_b = sb("att_b", [P, HID], F32)
        msg = sb("msg", [P, HID], F32)
        act_s = sb("act_s", [P, HID], F32)
        prod = sb("prod", [P, HID], F32)
        e_self = sb("e_self", [P, NT, HEADS], F32)

        tp = ps("tp", [P, D])
        pd = ps("pd", [P, HID])
        pt = ps("pt", [P, HID])
        plr = ps("plr", [P, 2 * HID])
        pe = ps("pe", [P, 2 * 16])

        started = sem("pr_started")
        edges_in = sem("pr_edges_in")
        consts_in = sem("pr_consts_in")
        filled = sem("pr_filled")
        idents = sem("pr_idents")
        dve = sem("pr_dve")
        totals = sem("pr_totals")
        prefixes = sem("pr_prefixes")
        slots_ready = sem("pr_slots_ready")
        unused_ready = sem("pr_unused_ready")
        unused_out = sem("pr_unused_out")
        tiles_ready = sem("pr_tiles_ready")
        staged = sem("pr_staged")
        scattered = [sem(f"pr_scattered{k}") for k in range(2)]
        x_in = [sem(f"pr_x_in{k}") for k in range(2)]
        x_used = sem("pr_x_used")
        squared = sem("pr_squared")
        x_turned = sem("pr_x_turned")
        xT_ready = sem("pr_xT_ready")
        wd_ready = sem("pr_wd_ready")
        down = sem("pr_down")
        ms_ready = sem("pr_ms_ready")
        rms_ready = sem("pr_rms_ready")
        xd_ready = sem("pr_xd_ready")
        xd_turned = sem("pr_xd_turned")
        xdT_ready = sem("pr_xdT_ready")
        lr = sem("pr_lr")
        xl_ready = sem("pr_xl_ready")
        xr_ready = sem("pr_xr_ready")
        self_msg = sem("pr_self_msg")
        self_act = sem("pr_self_act")
        self_ready = sem("pr_self_ready")
        xl_ones = sem("pr_xl_ones")
        tabs_out = [sem(f"pr_tabs_out{k}") for k in range(2)]
        last_out = sem("pr_last_out")

        block = ctx.enter_context(nc.Block())

        @block.sync
        def _(eng):
            eng.dma_start(dst_i[:, :], dst.rearrange("(p c) -> p c", p=EP)).then_inc(edges_in, 16)
            eng.dma_start(src_i[:, :], src.rearrange("(p c) -> p c", p=EP)).then_inc(edges_in, 16)
            eng.dma_start(wgt[:, :], edge_weight.rearrange("(p c) -> p c", p=EP)).then_inc(edges_in, 16)
            eng.dma_start(wd[:, :, :], w_down.rearrange("(k p) n -> p k n", p=P)).then_inc(consts_in, 16)
            eng.dma_start(rw[:, :], rms_w.rearrange("(k p) -> p k", p=P),
                          allow_slow_non_contiguous=True).then_inc(consts_in, 16)
            eng.dma_start(wlr[:, :, 0:HID], wl.rearrange("(k p) n -> p k n", p=P)).then_inc(consts_in, 16)
            eng.dma_start(wlr[:, :, HID:2 * HID], wr.rearrange("(k p) n -> p k n", p=P)).then_inc(consts_in, 16)
            eng.dma_start(att_b[:, :], att.rearrange("h d -> (h d)").partition_broadcast(P)).then_inc(consts_in, 16)
            eng.wait_ge(unused_ready, 1)
            eng.dma_start(edge_tab.rearrange("(p c) w -> p c w", p=P), unused[:, :, :]).then_inc(unused_out, 16)
            eng.wait_ge(started, 3)
            with eng.Fori(0, NT // 2) as j:
                for k in range(2):
                    i = 2 * j + k
                    eng.wait_ge(started, 3)
                    eng.wait_ge(x_used, i + 1)
                    eng.dma_start(xin[:, k, :], x[bass.ds(i * P, P), :]).then_inc(x_in[k], 16)
            eng.wait_ge(tiles_ready, 1)
            eng.dma_start(tile_tab, tile_i[:, :]).then_inc(last_out, 16)
            eng.wait_ge(self_ready, NT)
            eng.dma_start(self_tab, e_self[:, :, :]).then_inc(last_out, 16)
            eng.wait_ge(last_out, 32)

        @block.gpsimd
        def _(eng):
            eng.sem_inc(x_used, 2)
            eng.sem_inc(started, 1)
            eng.memset(unused[:, :, :], 0.0).then_inc(filled, 1)
            eng.memset(ident[:, :], 0.0).then_inc(filled, 1)
            eng.memset(before[:, :], 1.0).then_inc(filled, 1)
            eng.memset(ones[:, :], 1.0).then_inc(filled, 1)
            eng.wait_ge(filled, 4)
            eng.memset(unused[:, :, 1], NO_DST).then_inc(unused_ready, 1)
            eng.affine_select(out=ident[:, :], in_=ident[:, :], compare_op=ALU.not_equal, fill=1.0, base=0,
                              pattern=[[-1, P]], channel_multiplier=1).then_inc(idents, 1)
            eng.affine_select(out=before[:, :], in_=before[:, :], compare_op=ALU.is_gt, fill=0.0, base=0,
                              pattern=[[1, P]], channel_multiplier=-1).then_inc(idents, 1)
            eng.iota(iota_g[:, :], [[1, NG]], base=0, channel_multiplier=0,
                     allow_small_or_imprecise_dtypes=True).then_inc(idents, 1)
            eng.memset(xl[:, :, :], 1.0).then_inc(xl_ones, 1)
            eng.wait_ge(slots_ready, 1)
            eng.wait_ge(unused_out, 16)
            for k in range(2):
                eng.tensor_copy(slot_st[:, k, :], slot_i[:, k * SC:(k + 1) * SC]).then_inc(staged, 1)
                eng.tensor_copy(rec_st[:, k, :], record[:, k * SC:(k + 1) * SC, :].rearrange("p c w -> p (c w)"))\
                   .then_inc(staged, 1)
                eng.wait_ge(staged, 2 * k + 2)
                for s in range(SC):
                    eng.indirect_dma_start(edge_tab, bass.IndirectOffsetOnAxis(ap=slot_st[:, k, s:s + 1], axis=0),
                                           rec_st[:, k, s * 4:s * 4 + 4], None).then_inc(scattered[k], 16)
            with eng.Fori(1, EC // (2 * SC)) as j:
                for k in range(2):
                    i = 2 * j + k
                    eng.wait_ge(unused_out, 16)
                    eng.wait_ge(scattered[k], 16 * SC * j)
                    eng.tensor_copy(slot_st[:, k, :], slot_i[:, bass.ds(i * SC, SC)]).then_inc(staged, 1)
                    eng.tensor_copy(rec_st[:, k, :], record[:, bass.ds(i * SC, SC), :].rearrange("p c w -> p (c w)"))\
                       .then_inc(staged, 1)
                    due = eng.to_reg(i * 2 + 2)
                    eng.wait_ge(unused_out, 16)
                    eng.wait_ge(staged, due)
                    for s in range(SC):
                        eng.indirect_dma_start(edge_tab, bass.IndirectOffsetOnAxis(ap=slot_st[:, k, s:s + 1], axis=0),
                                               rec_st[:, k, s * 4:s * 4 + 4], None).then_inc(scattered[k], 16)
            for k in range(2):
                eng.wait_ge(scattered[k], 16 * EC // 2)

        @block.scalar
        def _(eng):
            eng.sem_inc(started, 1)
            eng.sem_inc(rms_ready, 1)
            eng.wait_ge(started, 3)
            with eng.Fori(0, NT // 2) as j:
                for k in range(2):
                    i = 2 * j + k
                    eng.wait_ge(started, 3)
                    eng.wait_ge(x_in[k], 16 * j + 16)
                    eng.wait_ge(ms_ready, i + 1)
                    eng.activation(sq[:, :], xin[:, k, :], ACT.Square, accum_out=ssq[:, 0:1]).then_inc(squared, 1)
                    eng.wait_ge(started, 3)
                    eng.wait_ge(x_turned, i + 1)
                    eng.activation(xT[:, :], tp[:, :], ACT.Copy).then_inc(xT_ready, 1)
                    eng.wait_ge(started, 3)
                    eng.wait_ge(ms_ready, i + 2)
                    eng.activation(rms[:, :], ms[:, :], ACT.Sqrt).then_inc(rms_ready, 1)
                    eng.wait_ge(started, 3)
                    eng.wait_ge(xr_ready, i + 1)
                    eng.dma_start(xl_tab[bass.ds(i * P, P), :], xl[:, k, :]).then_inc(tabs_out[k], 16)
                    eng.dma_start(xr_tab[bass.ds(i * P, P), :], xr[:, k, :]).then_inc(tabs_out[k], 16)
            for k in range(2):
                eng.wait_ge(tabs_out[k], 32 * (NT // 2) + 32)

        @block.tensor
        def _(eng):
            eng.sem_inc(started, 1)
            eng.wait_ge(idents, 3)
            eng.wait_ge(totals, 1)
            eng.matmul(pe[:, 0:NT], before[:, :], total[:, :], start=True, stop=True).then_inc(prefixes, 1)
            eng.matmul(pe[:, 16:16 + NT], ones[0:EP, :], total[:, :], start=True, stop=True).then_inc(prefixes, 1)
            eng.wait_ge(wd_ready, KT)
            with eng.Fori(0, NT // 2) as j:
                for k in range(2):
                    i = 2 * j + k
                    eng.wait_ge(started, 3)
                    eng.wait_ge(squared, i + 1)
                    for t in range(KT):
                        mm = eng.transpose(tp[:, t * P:(t + 1) * P], xin[:, k, t * P:(t + 1) * P], ident[:, :])
                    mm.then_inc(x_turned, 1)
                    eng.wait_ge(started, 3)
                    eng.wait_ge(xT_ready, i + 1)
                    for t in range(KT):
                        mm = eng.matmul(pd[:, :], xT[:, t * P:(t + 1) * P], wd[:, t, :],
                                        start=(t == 0), stop=(t == KT - 1))
                        if t == 0:
                            mm.then_inc(x_used, 1)
                    mm.then_inc(down, 1)
                    eng.wait_ge(started, 3)
                    eng.wait_ge(xd_ready, i + 1)
                    for t in range(2):
                        mm = eng.transpose(pt[:, t * P:(t + 1) * P], xd[:, t * P:(t + 1) * P], ident[:, :])
                    mm.then_inc(xd_turned, 1)
                    eng.wait_ge(started, 3)
                    eng.wait_ge(xdT_ready, i + 1)
                    for t in range(2):
                        mm = eng.matmul(plr[:, :], xdT[:, t * P:(t + 1) * P], wlr[:, t, :],
                                        start=(t == 0), stop=(t == 1))
                    mm.then_inc(lr, 1)

        @block.vector
        def _(eng):
            eng.sem_inc(ms_ready, 1)
            eng.sem_inc(tabs_out[0], 32)
            eng.sem_inc(tabs_out[1], 32)
            n = 0

            def step(ins):
                nonlocal n
                n += 1
                ins.then_inc(dve, 1)
                eng.wait_ge(dve, n)

            eng.wait_ge(edges_in, 48)
            step(eng.tensor_scalar(bucket_i[:, :], dst_i[:, :], 7, None, ALU.logical_shift_right))
            step(eng.tensor_scalar(local_i[:, :], dst_i[:, :], P - 1, None, ALU.bitwise_and))
            step(eng.tensor_copy(bucket[:, :], bucket_i[:, :]))
            step(eng.tensor_copy(record[:, :, 0], src_i[:, :]))
            step(eng.tensor_copy(record[:, :, 1], local_i[:, :]))
            step(eng.tensor_copy(record[:, :, 2], wgt[:, :]))
            step(eng.memset(record[:, :, 3], 0.0))
            step(eng.memset(zeros[:, :], 0.0))
            step(eng.memset(zeros10[:, :], 0.0))
            for b in range(NT):
                step(eng.tensor_scalar(mask[:, b, :], bucket[:, :], float(b), None, ALU.is_equal))
                step(eng.tensor_tensor_scan(rank[:, b, :], mask[:, b, :], zeros[:, :], 0.0, ALU.add, ALU.add))
            eng.tensor_copy(total[:, :], rank[:, :, EC - 1]).then_inc(totals, 1)
            eng.wait_ge(prefixes, 2)
            step(eng.tensor_scalar(count_f[:, :], pe[:, 16:16 + NT], float(GE - 1), None, ALU.add))
            step(eng.tensor_copy(count_i[:, :], count_f[:, :]))
            step(eng.tensor_scalar(count_i[:, :], count_i[:, :], GE.bit_length() - 1, None, ALU.logical_shift_right))
            step(eng.tensor_copy(groups[:, :], count_i[:, :]))
            step(eng.tensor_tensor_scan(group_end[:, :], groups[:, :], zeros10[:, :], 0.0, ALU.add, ALU.add))
            step(eng.tensor_tensor(groups[:, :], group_end[:, :], groups[:, :], ALU.subtract))
            step(eng.tensor_scalar(base[:, :], groups[0:EP, :], float(GE), -1.0, ALU.mult, ALU.add))
            step(eng.tensor_tensor(base[:, :], base[:, :], pe[0:EP, 0:NT], ALU.add))
            for b in range(NT):
                o = slot if b == 0 else part
                step(eng.scalar_tensor_tensor(out=o[:, :], in0=rank[:, b, :], scalar=base[:, b:b + 1],
                                              in1=mask[:, b, :], op0=ALU.add, op1=ALU.mult))
                if b:
                    step(eng.tensor_tensor(slot[:, :], slot[:, :], part[:, :], ALU.add))
            eng.tensor_copy(slot_i[:, :], slot[:, :]).then_inc(slots_ready, 1)
            step(eng.memset(tile_f[:, :], 0.0))
            eng.wait_ge(idents, 3)
            for b in range(NT - 1):
                step(eng.scalar_tensor_tensor(out=tile_f[:, :], in0=iota_g[:, :], scalar=group_end[0:1, b:b + 1],
                                              in1=tile_f[:, :], op0=ALU.is_ge, op1=ALU.add))
            eng.tensor_copy(tile_i[:, :], tile_f[:, :]).then_inc(tiles_ready, 1)

            eng.wait_ge(consts_in, 80)
            for t in range(KT):
                eng.tensor_scalar(wd[:, t, :], wd[:, t, :], rw[:, t:t + 1], None, ALU.mult).then_inc(wd_ready, 1)
            eng.wait_ge(xl_ones, 1)
            with eng.Fori(0, NT // 2) as j:
                for k in range(2):
                    i = 2 * j + k
                    eng.wait_ge(xl_ones, 1)
                    eng.wait_ge(squared, i + 1)
                    eng.wait_ge(rms_ready, i + 1)
                    eng.tensor_scalar(ms[:, :], ssq[:, 0:1], 1.0 / D, 1e-6, ALU.mult, ALU.add).then_inc(ms_ready, 1)
                    eng.wait_ge(xl_ones, 1)
                    eng.wait_ge(rms_ready, i + 2)
                    eng.reciprocal(rinv[:, :], rms[:, :]).then_inc(dve, 1)
                    eng.wait_ge(dve, n + 3 * i + 1)
                    eng.wait_ge(down, i + 1)
                    eng.tensor_scalar(xd[:, :], pd[:, :], rinv[:, 0:1], None, ALU.mult).then_inc(xd_ready, 1)
                    eng.wait_ge(xl_ones, 1)
                    eng.wait_ge(xd_turned, i + 1)
                    eng.tensor_copy(xdT[:, :], pt[:, :]).then_inc(xdT_ready, 1)
                    eng.wait_ge(xl_ones, 1)
                    eng.wait_ge(lr, i + 1)
                    eng.wait_ge(tabs_out[k], 32 * j + 32)
                    eng.tensor_copy(xl[:, k, :].rearrange("p (h w) -> p h w", h=HEADS)[:, :, 0:HD],
                                    plr[:, 0:HID].rearrange("p (h d) -> p h d", h=HEADS)).then_inc(dve, 1)
                    eng.tensor_copy(xr[:, k, :], plr[:, HID:2 * HID]).then_inc(xr_ready, 1)
                    eng.wait_ge(xl_ones, 1)
                    eng.wait_ge(dve, n + 3 * i + 2)
                    eng.wait_ge(xr_ready, i + 1)
                    eng.tensor_tensor(msg[:, :].rearrange("p (h d) -> p h d", h=HEADS),
                                      xl[:, k, :].rearrange("p (h w) -> p h w", h=HEADS)[:, :, 0:HD],
                                      xr[:, k, :].rearrange("p (h d) -> p h d", h=HEADS), ALU.add)\
                       .then_inc(self_msg, 1)
                    eng.wait_ge(xl_ones, 1)
                    eng.wait_ge(self_msg, i + 1)
                    eng.scalar_tensor_tensor(out=act_s[:, :], in0=msg[:, :], scalar=0.2, in1=msg[:, :],
                                             op0=ALU.mult, op1=ALU.max).then_inc(self_act, 1)
                    eng.wait_ge(xl_ones, 1)
                    eng.wait_ge(self_act, i + 1)
                    eng.tensor_tensor(prod[:, :], act_s[:, :], att_b[:, :], ALU.mult).then_inc(dve, 1)
                    eng.wait_ge(xl_ones, 1)
                    eng.wait_ge(dve, n + 3 * i + 3)
                    eng.tensor_reduce(e_self[:, bass.ds(i, 1), :].rearrange("p a h -> p (a h)"),
                                      prod[:, :].rearrange("p (h d) -> p h d", h=HEADS), AX.X, ALU.add)\
                       .then_inc(self_ready, 1)


def edge_phase(nc, sem, edge_tab, xl_tab, self_tab, xr_tab, tile_tab, att, adj_tab, wt_tab, o_tab,
               deg_inv, deg_rsqrt):
    with ExitStack() as ctx:
        def sb(name, shape, dt):
            return ctx.enter_context(nc.sbuf_tensor("ed_" + name, shape, dt))

        def ps(name, shape):
            return ctx.enter_context(nc.psum_tensor("ed_" + name, shape, F32))

        slots = sb("slots", [P, NC, 4], F32)
        src_f = sb("src_f", [P, NC], F32)
        src_i = sb("src_i", [P, NC], I32)
        loc = sb("loc", [P, NC], F32)
        w_rest = sb("w_rest", [P, NC], F32)
        w_b = sb("w_b", [P, NC], BF16)
        w_part = sb("w_part", [P, 3, NC], F32)
        tiles = sb("tiles", [1, NG], I32)
        iota_n = sb("iota_n", [P, NPAD], F16)
        ident = sb("ident", [P, P], F32)
        ident_r = sb("ident_r", [P, P], F32R)
        att_b = sb("att_b", [P, HID], F32)
        src_st = sb("src_st", [P, 2, CH], I32)
        gat = sb("gat", [P, 2, NPAD], F32)
        hot_s = sb("hot_s", [P, 2, CH, NPAD], BF16)
        hot_b = sb("hot_b", [P, 2, CH, 4, P], BF16)
        hot_f = sb("hot_f", [P, 2, CH, P], F32)
        hot_t = sb("hot_t", [P, CH, P], F32R)
        bound = sb("bound", [P, CH, P], F32)
        xr_hi = sb("xr_hi", [P, NT, HID], F32R)
        xr_lo = sb("xr_lo", [P, NT, HID], F32R)
        work = sb("work", [P, 2, NPAD], F32)
        score = sb("score", [P, CH * HEADS], F32)
        score_hi = sb("score_hi", [P, CH * HEADS], F32R)
        score_lo = sb("score_lo", [P, CH * HEADS], F32R)
        masked = sb("masked", [P, CH * P], F32)
        group_max = sb("group_max", [P, HEADS], F32)
        new_max = sb("new_max", [P, HEADS], F32)
        shift = sb("shift", [P, HEADS], F32)
        fade = sb("fade", [P, HEADS], F32)
        max_hi = sb("max_hi", [P, HEADS], F32R)
        max_lo = sb("max_lo", [P, HEADS], F32R)
        expo = sb("expo", [P, CH * HEADS], F32)
        prob = sb("prob", [P, CH * HEADS], F32)
        seg_max = sb("seg_max", [P, NT * HEADS], F32)
        seg_sum = sb("seg_sum", [P, NT, XW], F32)
        adj = sb("adj", [P, NT, NPAD], F32)
        wt = sb("wt", [P, NT, D], F32)

        p_adj = ps("p_adj", [P, 3 * 512])
        p_wt = ps("p_wt", [P, D])
        bank_x = ps("bank_x", [P, 512])
        bank_y = ps("bank_y", [P, 512])
        bank_z = ps("bank_z", [P, 512])

        tabs_in = sem("ed_tabs_in")
        filled = sem("ed_filled")
        consts = sem("ed_consts")
        dve = sem("ed_dve")
        ready = sem("ed_ready")
        tiles_in = sem("ed_tiles_in")
        staged = sem("ed_staged")
        gathered = [sem(f"ed_gathered{k}") for k in range(2)]
        hots = sem("ed_hots")
        turned = sem("ed_turned")
        turned_out = sem("ed_turned_out")
        xr_done = sem("ed_xr_done")
        msg_ready = sem("ed_msg_ready")
        act_ready = sem("ed_act_ready")
        score_ready = sem("ed_score_ready")
        spread = sem("ed_spread")
        head_max = sem("ed_head_max")
        shift_ready = sem("ed_shift_ready")
        fade_ready = sem("ed_fade_ready")
        max_ready = sem("ed_max_ready")
        max_back = sem("ed_max_back")
        expo_ready = sem("ed_expo_ready")
        prob_ready = sem("ed_prob_ready")
        weighted = sem("ed_weighted")
        summed = sem("ed_summed")
        sums_added = sem("ed_sums_added")
        counted = sem("ed_counted")
        counts_added = sem("ed_counts_added")
        loop_done = sem("ed_loop_done")
        adj_st_ready = sem("ed_adj_st_ready")
        adj_turned = sem("ed_adj_turned")
        adj_t_ready = sem("ed_adj_t_ready")
        adj_out = [sem(f"ed_adj_out{k}") for k in range(2)]
        deg_done = sem("ed_deg_done")
        root = sem("ed_root")
        o_ready = sem("ed_o_ready")
        last_out = sem("ed_last_out")

        deg = sb("deg", [P, NT], F32)
        deg1 = sb("deg1", [P, NT], F32)
        droot = sb("droot", [P, NT], F32)
        den = sb("den", [P, NT, HEADS], F32)
        xlg = gat[:, :, 0:CH * XW].rearrange("p k (c w) -> p k c w", c=CH)
        msg = work[:, 0, 0:CH * HID].rearrange("p (c d) -> p c d", c=CH)
        act_m = work[:, 1, 0:CH * HID].rearrange("p (c d) -> p c d", c=CH)
        adj_st = work
        adj_t = gat

        block = ctx.enter_context(nc.Block())

        @block.sync
        def _(eng):
            eng.dma_start(slots[:, :, :].rearrange("p (g c) w -> p g (c w)", c=CH),
                          edge_tab.rearrange("(g p c) w -> p g (c w)", p=P, c=CH)).then_inc(tabs_in, 16)
            eng.dma_start(seg_max[:, :], self_tab.rearrange("p t h -> p (t h)")).then_inc(tabs_in, 16)
            eng.dma_start(seg_sum[:, :, :], xl_tab.rearrange("(t p) w -> p t w", p=P)).then_inc(tabs_in, 16)
            eng.dma_start(adj[:, 0:2, :].rearrange("p a n -> p (a n)").rearrange("p (t n) -> p t n", t=NT),
                          xr_tab.rearrange("(t p) n -> p t n", p=P)).then_inc(tabs_in, 16)
            eng.dma_start(att_b[:, :], att.rearrange("h d -> (h d)").partition_broadcast(P)).then_inc(tabs_in, 16)
            eng.dma_start(tiles[:, :], tile_tab).then_inc(tiles_in, 16)
            eng.wait_ge(counts_added, NG + 1)
            for t in range(D // P):
                eng.dma_start(wt_tab[t * P:(t + 1) * P, :], wt[:, t, :]).then_inc(last_out, 16)
            with eng.Fori(0, NT // 2) as j:
                for k in range(2):
                    i = 2 * j + k
                    eng.wait_ge(tiles_in, 16)
                    eng.wait_ge(adj_t_ready, i + 2)
                    eng.dma_start(adj_tab[bass.ds(i * P, P), :], adj_t[:, k, :]).then_inc(adj_out[k], 16)
            eng.wait_ge(o_ready, 1)
            for h in range(HEADS):
                eng.dma_start(o_tab.rearrange("(t p) (h d) -> p t h d", p=P, h=HEADS)[:, :, h, :],
                              seg_sum[:, :, h * HW:h * HW + HD]).then_inc(last_out, 16)
            for k in range(2):
                eng.wait_ge(adj_out[k], 16 * (NT // 2) + 16)
            eng.wait_ge(last_out, 16 * (D // P + HEADS))

        @block.gpsimd
        def _(eng):
            eng.memset(ident[:, :], 0.0).then_inc(filled, 1)
            eng.iota(iota_n[:, :], [[1, NPAD]], base=0, channel_multiplier=0,
                     allow_small_or_imprecise_dtypes=True).then_inc(consts, 1)
            eng.wait_ge(filled, 1)
            eng.affine_select(out=ident[:, :], in_=ident[:, :], compare_op=ALU.not_equal, fill=1.0, base=0,
                              pattern=[[-1, P]], channel_multiplier=1).then_inc(consts, 1)
            eng.memset(wt[:, :, :], 0.0).then_inc(consts, 1)
            eng.wait_ge(ready, 1)
            with eng.Fori(0, NG // 2) as j:
                for k in range(2):
                    g = 2 * j + k
                    eng.wait_ge(ready, 1)
                    eng.wait_ge(summed, g + 1)
                    eng.tensor_copy(src_st[:, k, :], src_i[:, bass.ds(g * CH, CH)]).then_inc(staged, 1)
                    due = eng.to_reg(g + 1)
                    eng.wait_ge(ready, 1)
                    eng.wait_ge(staged, due)
                    for c in range(CH):
                        eng.indirect_dma_start(xlg[:, k, c, :], None, xl_tab,
                                               bass.IndirectOffsetOnAxis(ap=src_st[:, k, c:c + 1], axis=0))\
                           .then_inc(gathered[k], 16)

        def hot(eng, g, k, c):
            at = g * CH + c
            eng.wait_ge(ready, 1)
            eng.wait_ge(counted, at + 1)
            eng.tensor_scalar(hot_s[:, k, c, :], iota_n[:, :], src_f[:, bass.ds(at, 1)], None, ALU.is_equal)\
               .then_inc(hots, 1)
            eng.tensor_scalar(hot_f[:, k, c, :], iota_n[:, 0:P], loc[:, bass.ds(at, 1)], None, ALU.is_equal)\
               .then_inc(hots, 1)
            eng.tensor_scalar(hot_b[:, k, c, 0, :], iota_n[:, 0:P], loc[:, bass.ds(at, 1)], None, ALU.is_equal)\
               .then_inc(hots, 1)
            for q in range(3):
                eng.tensor_scalar(hot_b[:, k, c, 1 + q, :], iota_n[:, 0:P], loc[:, bass.ds(at, 1)],
                                  w_part[:, q, bass.ds(at, 1)], ALU.is_equal, ALU.mult).then_inc(hots, 1)

        HOTS = 6

        @block.scalar
        def _(eng):
            eng.wait_ge(consts, 3)
            eng.activation(ident_r[:, :], ident[:, :], ACT.Copy).then_inc(consts, 1)

            def turn_out(g):
                eng.wait_ge(ready, 1)
                eng.wait_ge(turned, g + 1)
                eng.activation(hot_t[:, :, :], bank_x[:, :].rearrange("p (c e) -> p c e", c=CH), ACT.Copy)\
                   .then_inc(turned_out, 1)
                eng.activation(bound[:, :, :], bank_x[:, :].rearrange("p (c e) -> p c e", c=CH), ACT.Copy,
                               scale=BIG, bias=-BIG).then_inc(turned_out, 1)

            def body(g, k, last=False):
                eng.wait_ge(ready, 1)
                eng.wait_ge(shift_ready, g + 1)
                eng.activation(fade[:, :], shift[:, :], ACT.Exp).then_inc(fade_ready, 1)
                eng.wait_ge(ready, 1)
                eng.wait_ge(expo_ready, g + 1)
                eng.activation(prob[:, :], expo[:, :], ACT.Exp).then_inc(prob_ready, 1)
                if not last:
                    turn_out(g + 1)

            turn_out(0)
            with eng.Fori(0, NG // 2 - 1) as j:
                for k in range(2):
                    body(2 * j + k, k)
            body(NG - 2, 0)
            body(NG - 1, 1, last=True)
            eng.wait_ge(deg_done, 4)
            eng.activation(droot[:, :], deg1[:, :], ACT.Sqrt).then_inc(root, 1)
            with eng.Fori(0, NT // 2) as j:
                for k in range(2):
                    i = 2 * j + k
                    eng.wait_ge(counts_added, NG + 1)
                    eng.wait_ge(adj_turned, i + 1)
                    eng.activation(adj_st[:, k, :], adj[:, bass.ds(i, 1), :].rearrange("p a n -> p (a n)"),
                                   ACT.Copy).then_inc(adj_st_ready, 1)

        @block.tensor
        def _(eng):
            eng.sem_inc(counted, 2 * CH)
            eng.sem_inc(adj_turned, 2)
            eng.sem_inc(summed, 2)

            def turn(g, k):
                eng.wait_ge(ready, 1)
                eng.wait_ge(hots, HOTS * CH * (g + 1))
                for c in range(CH):
                    mm = eng.transpose(bank_x[:, c * P:(c + 1) * P], hot_f[:, k, c, :], ident[:, :])
                mm.then_inc(turned, 1)

            def counts(g, k, c):
                if c == 0:
                    eng.wait_ge(ready, 1)
                    eng.wait_ge(counts_added, g + 1)
                for n0, n1 in ((0, 512), (512, 1024), (1024, N_NODES)):
                    eng.matmul(p_adj[:, n0:n1], hot_b[:, k, c, 0, :], hot_s[:, k, c, n0:n1],
                               start=(c == 0), stop=(c == CH - 1))
                for n0 in (0, 512):
                    for q in range(3):
                        mm = eng.matmul(p_wt[:, n0:n0 + 512], hot_b[:, k, c, 1 + q, :], hot_s[:, k, c, n0:n0 + 512],
                                        start=(c == 0 and q == 0), stop=(c == CH - 1 and q == 2))
                mm.then_inc(counted, 1)

            def spread_head(g, h):
                bank = (bank_x, bank_y, bank_z, bank_x)[h]
                for c in range(CH):
                    for q, part in enumerate((score_hi, score_lo)):
                        mm = eng.matmul(bank[:, c * P:(c + 1) * P],
                                        part[:, c * HEADS + h:c * HEADS + h + 1].broadcast_to([P, P]),
                                        ident_r[:, :], start=(q == 0), stop=(q == 1))
                mm.then_inc(spread, 1)

            def body(g, k, last=False):
                t = eng.value_load(tiles[0:1, bass.ds(g, 1)], min_val=0, max_val=NT - 1)
                eng.wait_ge(ready, 1)
                eng.wait_ge(turned_out, 2 * g + 2)
                eng.wait_ge(sums_added, g + 1)
                for c in range(CH):
                    bank = (bank_y, bank_z)[c // 2]
                    for q, part in enumerate((xr_hi, xr_lo)):
                        mm = eng.matmul(bank[:, (c % 2) * HID:(c % 2 + 1) * HID], hot_t[:, c, :],
                                        part[:, bass.ds(t, 1), :].rearrange("p a n -> p (a n)"),
                                        start=(q == 0), stop=(q == 1))
                    if c % 2 == 1:
                        mm.then_inc(xr_done, 1)
                counts(g, k, 0)
                eng.wait_ge(ready, 1)
                eng.wait_ge(score_ready, g + 1)
                for h in range(3):
                    spread_head(g, h)
                counts(g, k, 1)
                eng.wait_ge(ready, 1)
                eng.wait_ge(head_max, HEADS * g + 1)
                spread_head(g, 3)
                counts(g, k, 2)
                eng.wait_ge(ready, 1)
                eng.wait_ge(max_ready, g + 1)
                for c in range(CH):
                    for q, part in enumerate((max_hi, max_lo)):
                        mm = eng.matmul(bank_z[:, c * HEADS:(c + 1) * HEADS], hot_t[:, c, :], part[:, :],
                                        start=(q == 0), stop=(q == 1))
                mm.then_inc(max_back, 1)
                counts(g, k, 3)
                if not last:
                    turn(g + 1, 1 - k)
                eng.wait_ge(ready, 1)
                eng.wait_ge(weighted, g + 1)
                for c in range(CH):
                    mm = eng.matmul(bank_y[:, 0:XW], hot_f[:, k, c, :], xlg[:, k, c, :],
                                    start=(c == 0), stop=(c == CH - 1))
                mm.then_inc(summed, 1)

            eng.wait_ge(consts, 4)
            eng.wait_ge(tiles_in, 16)
            turn(0, 0)
            with eng.Fori(0, NG // 2 - 1) as j:
                for k in range(2):
                    body(2 * j + k, k)
            body(NG - 2, 0)
            body(NG - 1, 1, last=True)
            with eng.Fori(0, NT // 2) as j:
                for k in range(2):
                    i = 2 * j + k
                    eng.wait_ge(counts_added, NG + 1)
                    eng.wait_ge(adj_st_ready, i + 1)
                    eng.wait_ge(adj_t_ready, i + 1)
                    for s in range(NT):
                        mm = eng.transpose(p_adj[:, s * P:(s + 1) * P], adj_st[:, k, s * P:(s + 1) * P], ident[:, :])
                    mm.then_inc(adj_turned, 1)

        @block.vector
        def _(eng):
            eng.sem_inc(counts_added, 1)
            eng.sem_inc(sums_added, 1)
            n = 0

            def step(ins):
                nonlocal n
                n += 1
                ins.then_inc(dve, 1)
                eng.wait_ge(dve, n)

            eng.wait_ge(tabs_in, 80)
            eng.wait_ge(tiles_in, 16)
            eng.wait_ge(consts, 4)
            step(eng.tensor_copy(src_f[:, :], slots[:, :, 0]))
            step(eng.tensor_copy(src_i[:, :], slots[:, :, 0]))
            step(eng.tensor_copy(loc[:, :], slots[:, :, 1]))
            step(eng.tensor_copy(w_rest[:, :], slots[:, :, 2]))
            for q in range(3):
                step(eng.tensor_copy(w_b[:, :], w_rest[:, :]))
                step(eng.tensor_copy(w_part[:, q, :], w_b[:, :]))
                step(eng.tensor_tensor(w_rest[:, :], w_rest[:, :], w_part[:, q, :], ALU.subtract))
            landed = adj[:, 0:2, :].rearrange("p a n -> p (a n)").rearrange("p (t n) -> p t n", t=NT)
            step(eng.tensor_copy(xr_hi[:, :, :], landed))
            step(eng.tensor_tensor(xr_lo[:, :, :], landed, xr_hi[:, :, :].bitcast(F32), ALU.subtract))
            step(eng.memset(adj[:, :, :], 0.0))
            eng.sem_inc(ready, 1)
            for c in range(CH):
                hot(eng, 0, 0, c)
            at0 = n
            STEPS = 9

            def body(r, k, last=False):
                g = 2 * r + k
                t = eng.value_load(tiles[0:1, bass.ds(g, 1)], min_val=0, max_val=NT - 1)
                m = 0

                def chain(ins):
                    nonlocal m
                    m += 1
                    ins.then_inc(dve, 1)
                    eng.wait_ge(ready, 1)
                    eng.wait_ge(dve, at0 + STEPS * g + m)

                eng.wait_ge(gathered[k], 16 * CH * (r + 1))
                for b, bank in enumerate((bank_y, bank_z)):
                    eng.wait_ge(ready, 1)
                    eng.wait_ge(xr_done, 2 * g + b + 1)
                    eng.tensor_tensor(msg[:, 2 * b:2 * b + 2, :].rearrange("p c (h d) -> p (c h) d", h=HEADS),
                                      xlg[:, k, 2 * b:2 * b + 2, :].rearrange("p c (h w) -> p (c h) w", h=HEADS)[:, :, 0:HD],
                                      bank[:, :].rearrange("p (c d) -> p c d", d=HD), ALU.add).then_inc(msg_ready, 1)
                if not last:
                    hot(eng, g + 1, 1 - k, 0)
                eng.wait_ge(ready, 1)
                eng.wait_ge(msg_ready, 2 * g + 2)
                eng.scalar_tensor_tensor(out=work[:, 1, 0:CH * HID], in0=work[:, 0, 0:CH * HID], scalar=0.2,
                                         in1=work[:, 0, 0:CH * HID], op0=ALU.mult, op1=ALU.max).then_inc(act_ready, 1)
                eng.wait_ge(ready, 1)
                eng.wait_ge(act_ready, g + 1)
                chain(eng.tensor_tensor(act_m[:, :, :], act_m[:, :, :], att_b[:, :].unsqueeze(1).broadcast_to([P, CH, HID]),
                                        ALU.mult))
                chain(eng.tensor_reduce(score[:, :], act_m[:, :, :].rearrange("p c (h d) -> p (c h) d", h=HEADS),
                                        AX.X, ALU.add))
                chain(eng.tensor_copy(score_hi[:, :], score[:, :]))
                eng.tensor_tensor(score_lo[:, :], score[:, :], score_hi[:, :].bitcast(F32), ALU.subtract)\
                   .then_inc(score_ready, 1)
                if not last:
                    hot(eng, g + 1, 1 - k, 1)
                for h in range(HEADS):
                    bank = (bank_x, bank_y, bank_z, bank_x)[h]
                    due = eng.to_reg(g * HEADS + (h + 1)) if not isinstance(g, int) else g * HEADS + h + 1
                    before = g * HEADS + h
                    before = eng.to_reg(before) if h and not isinstance(g, int) else before
                    eng.wait_ge(ready, 1)
                    eng.wait_ge(spread, due)
                    if h:
                        eng.wait_ge(head_max, before)
                    eng.tensor_tensor_reduce(masked[:, :], bank[:, :], bound[:, :, :].rearrange("p c e -> p (c e)"),
                                             1.0, -BIG, ALU.add, ALU.max, group_max[:, h:h + 1]).then_inc(head_max, 1)
                run_max = seg_max[:, bass.ds(t * HEADS, HEADS)]
                eng.wait_ge(ready, 1)
                eng.wait_ge(head_max, HEADS * g + HEADS)
                chain(eng.tensor_tensor(new_max[:, :], run_max, group_max[:, :], ALU.max))
                eng.tensor_tensor(shift[:, :], run_max, new_max[:, :], ALU.subtract).then_inc(shift_ready, 1)
                eng.wait_ge(ready, 1)
                eng.wait_ge(shift_ready, g + 1)
                chain(eng.tensor_scalar(run_max, new_max[:, :], 1.0, None, ALU.mult))
                chain(eng.tensor_copy(max_hi[:, :], new_max[:, :]))
                eng.tensor_tensor(max_lo[:, :], new_max[:, :], max_hi[:, :].bitcast(F32), ALU.subtract)\
                   .then_inc(max_ready, 1)
                if not last:
                    hot(eng, g + 1, 1 - k, 2)
                eng.wait_ge(ready, 1)
                eng.wait_ge(max_back, g + 1)
                chain(eng.tensor_tensor(expo[:, :], score[:, :], bank_z[:, 0:CH * HEADS], ALU.subtract))
                eng.tensor_scalar(expo[:, :], expo[:, :], 0.0, None, ALU.min).then_inc(expo_ready, 1)
                if not last:
                    hot(eng, g + 1, 1 - k, 3)
                eng.wait_ge(ready, 1)
                eng.wait_ge(prob_ready, g + 1)
                rows = xlg[:, k, :, :].rearrange("p c (h w) -> p (c h) w", h=HEADS)
                eng.tensor_tensor(rows, rows, prob[:, :].unsqueeze(2).broadcast_to([P, CH * HEADS, HW]), ALU.mult)\
                   .then_inc(weighted, 1)
                run_adj = adj[:, bass.ds(t, 1), 0:N_NODES].rearrange("p a n -> p (a n)")
                run_wt = wt[:, bass.ds(t, 1), :].rearrange("p a n -> p (a n)")
                eng.wait_ge(ready, 1)
                eng.wait_ge(counted, CH * g + CH + 2 * CH)
                eng.wait_ge(counts_added, g + 1)
                chain(eng.tensor_tensor(run_adj, run_adj, p_adj[:, 0:N_NODES], ALU.add))
                eng.tensor_tensor(run_wt, run_wt, p_wt[:, :], ALU.add).then_inc(counts_added, 1)
                run_sum = seg_sum[:, bass.ds(t, 1), :].rearrange("p a (h w) -> p (a h) w", h=HEADS)
                eng.wait_ge(ready, 1)
                eng.wait_ge(fade_ready, g + 1)
                eng.wait_ge(sums_added, g + 1)
                chain(eng.tensor_tensor(run_sum, run_sum, fade[:, :].unsqueeze(2).broadcast_to([P, HEADS, HW]), ALU.mult))
                eng.wait_ge(ready, 1)
                eng.wait_ge(summed, g + 3)
                eng.tensor_tensor(run_sum, run_sum, bank_y[:, 0:XW].rearrange("p (h w) -> p h w", h=HEADS), ALU.add)\
                   .then_inc(sums_added, 1)
                return m

            with eng.Fori(0, NG // 2 - 1) as j:
                for k in range(2):
                    used = body(j, k)
            body(NG // 2 - 1, 0)
            body(NG // 2 - 1, 1, last=True)
            assert used == STEPS, used

            n = at0 + STEPS * NG
            eng.wait_ge(sums_added, NG + 1)
            eng.wait_ge(counts_added, NG + 1)
            sums = seg_sum[:, :, :].rearrange("p t (h w) -> p t h w", h=HEADS)
            step(eng.tensor_scalar(den[:, :, :], sums[:, :, :, HD], 1e-16, None, ALU.add))
            step(eng.reciprocal(den[:, :, :], den[:, :, :]))
            for t in range(NT):
                rows = seg_sum[:, t, :].rearrange("p (h w) -> p h w", h=HEADS)
                step(eng.tensor_tensor(rows, rows, den[:, t, :].unsqueeze(2).broadcast_to([P, HEADS, HW]), ALU.mult))
            eng.sem_inc(o_ready, 1)
            for t in range(NT):
                step(eng.tensor_reduce(deg[:, t:t + 1], adj[:, t, :], AX.X, ALU.add))
            step(eng.tensor_scalar(deg1[:, :], deg[:, :], 1.0, None, ALU.max))
            step(eng.reciprocal(deg_inv[:, :], deg1[:, :]))
            step(eng.tensor_scalar(deg1[:, :], deg[:, :], 1.0, None, ALU.add))
            eng.sem_inc(deg_done, 4)
            eng.wait_ge(root, 1)
            step(eng.reciprocal(deg_rsqrt[:, :], droot[:, :]))
            eng.sem_inc(adj_t_ready, 1)
            eng.sem_inc(adj_out[0], 16)
            eng.sem_inc(adj_out[1], 16)
            with eng.Fori(0, NT // 2) as j:
                for k in range(2):
                    i = 2 * j + k
                    eng.wait_ge(counts_added, NG + 1)
                    eng.wait_ge(adj_turned, i + 3)
                    eng.wait_ge(adj_out[k], 16 * j + 16)
                    eng.tensor_scalar(adj_t[:, k, :], p_adj[:, 0:NPAD], 1.0, None, ALU.mult).then_inc(adj_t_ready, 1)


def dense_phase(nc, sem, tag, sources, resident=None, scale=None, add_first=None, bias=None, relu=False,
                add=None, norm=False, out=None, add_after=None, out_after=None):
    S = len(sources)
    kts = [right.shape[0] // P for _, _, right in sources]
    KTS = sum(kts)
    KM = max(kts)
    rows = [r for r in (add_first, add, add_after) if r is not None]
    R = len(rows)

    with ExitStack() as ctx:
        def sb(name, shape, dt=F32):
            return ctx.enter_context(nc.sbuf_tensor(tag + name, shape, dt))

        right_hi = sb("right_hi", [P, KTS, D], F32R)
        right_lo = sb("right_lo", [P, KTS, D], F32R)
        right_in = sb("right_in", [P, 2, D])
        left_in = sb("left_in", [P, 2, KM * P]) if sources[0][0] != "held" else None
        left_hi = sb("left_hi", [P, 2, KM * P], F32R)
        left_lo = sb("left_lo", [P, 2, KM * P], F32R)
        ident = sb("ident", [P, P])
        y = sb("y", [P, 2, D])
        row_in = sb("row_in", [P, 2, R, D]) if R else None
        y2 = sb("y2", [P, 2, D]) if out_after is not None else None
        bias_b = sb("bias_b", [P, D]) if bias is not None else None
        stats = sb("stats", [P, 2, 6])
        mean_var = sb("mean_var", [P, 2])
        var_eps = sb("var_eps", [P, 1])
        std = sb("std", [P, 1])
        rstd = sb("rstd", [P, 1])
        turn = ctx.enter_context(nc.psum_tensor(tag + "turn", [P, 2, D], F32))
        acc = ctx.enter_context(nc.psum_tensor(tag + "acc", [P, 2, D], F32))

        started = sem(tag + "started")
        filled = sem(tag + "filled")
        ident_ready = sem(tag + "ident_ready")
        bias_in = sem(tag + "bias_in")
        right_landed = [sem(tag + f"right_landed{k}") for k in range(2)]
        right_hi_ready = sem(tag + "right_hi_ready")
        right_lo_ready = sem(tag + "right_lo_ready")
        left_landed = [sem(tag + f"left_landed{k}") for k in range(2)]
        turned = sem(tag + "turned")
        hi_ready = sem(tag + "hi_ready")
        lo_ready = sem(tag + "lo_ready")
        multiplied = sem(tag + "multiplied")
        row_landed = [sem(tag + f"row_landed{k}") for k in range(2)]
        chain = sem(tag + "chain")
        eps_added = sem(tag + "eps_added")
        rooted = sem(tag + "rooted")
        y_ready = sem(tag + "y_ready")
        y2_ready = sem(tag + "y2_ready")
        y_left = [sem(tag + f"y_left{k}") for k in range(2)]
        y2_left = [sem(tag + f"y2_left{k}") for k in range(2)]

        OPS = (add_first is not None) + (bias is not None or scale is not None) + relu + (add is not None)
        LINKS = OPS + 4 if norm else OPS - 1

        block = ctx.enter_context(nc.Block())

        @block.sync
        def _(eng):
            eng.sem_inc(started, 1)
            if bias is not None:
                eng.dma_start(bias_b[:, :], bias.partition_broadcast(P)).then_inc(bias_in, 16)
            n = 0

            def load_left(i, k, s, q):
                kind, left, _ = sources[s]
                kt = kts[s]
                eng.dma_start(left_in[:, q, 0:kt * P], left[bass.ds(i * P, P), :]).then_inc(left_landed[q], 16)

            for s, (_, _, right) in enumerate(sources):
                for t in range(kts[s]):
                    if n >= 2:
                        eng.wait_ge(right_lo_ready, n - 1)
                        eng.wait_ge(right_hi_ready, n - 1)
                    eng.dma_start(right_in[:, n % 2, :], right[t * P:(t + 1) * P, :]).then_inc(right_landed[n % 2], 16)
                    n += 1
            eng.wait_ge(started, 5)

            def store(i, k):
                n = N_NODES - (NT - 1) * P if out.shape[0] != NPAD and i is NT - 1 else P
                eng.dma_start(out[bass.ds(i * P, n), :], y[0:n, k, :]).then_inc(y_left[k], 16)
                if out_after is not None:
                    eng.dma_start(out_after[bass.ds(i * P, P), :], y2[:, k, :]).then_inc(y2_left[k], 16)

            def body(i, k, first=False):
                for s in range(S):
                    if sources[s][0] != "held":
                        q = (k * S + s) % 2
                        eng.wait_ge(started, 5)
                        if sources[s][0] == "rows":
                            eng.wait_ge(turned, S * i + s + 1)
                        else:
                            eng.wait_ge(lo_ready, S * i + s + 1)
                            eng.wait_ge(hi_ready, S * i + s + 1)
                        eng.dma_start(left_in[:, q, 0:kts[s] * P], sources[s][1][bass.ds(i * P, P), :])\
                           .then_inc(left_landed[q], 16)
                eng.wait_ge(started, 5)
                eng.wait_ge(y_ready, i + 1)
                if out_after is not None:
                    eng.wait_ge(y2_ready, i + 1)
                if not first:
                    store(i - 2, k)
                for r in range(R):
                    eng.dma_start(row_in[:, k, r, :], rows[r][bass.ds(i * P, P), :]).then_inc(row_landed[k], 16)

            for k in range(2):
                body(k, k, first=True)
            with eng.Fori(1, NT // 2) as j:
                for k in range(2):
                    body(2 * j + k, k)
            for i in (NT - 2, NT - 1):
                eng.wait_ge(y_ready, i + 3)
                if out_after is not None:
                    eng.wait_ge(y2_ready, i + 3)
                store(i, i % 2)
            for k in range(2):
                eng.wait_ge(y_left[k], 16 * (NT // 2) + 16)
                if out_after is not None:
                    eng.wait_ge(y2_left[k], 16 * (NT // 2) + 16)

        @block.gpsimd
        def _(eng):
            eng.sem_inc(started, 1)
            eng.memset(ident[:, :], 0.0).then_inc(filled, 1)
            eng.wait_ge(filled, 1)
            eng.affine_select(out=ident[:, :], in_=ident[:, :], compare_op=ALU.not_equal, fill=1.0, base=0,
                              pattern=[[-1, P]], channel_multiplier=1).then_inc(ident_ready, 1)

        @block.scalar
        def _(eng):
            eng.sem_inc(started, 1)
            eng.sem_inc(hi_ready, 2)
            for n in range(KTS):
                eng.wait_ge(right_landed[n % 2], 16 * (n // 2) + 16)
                eng.activation(right_hi[:, n, :], right_in[:, n % 2, :], ACT.Copy).then_inc(right_hi_ready, 1)

            def high(i, j, k, s):
                kind, kt, q = sources[s][0], kts[s], (k * S + s) % 2
                eng.wait_ge(started, 5)
                eng.wait_ge(multiplied, S * i + s + 1)
                if kind == "rows":
                    eng.wait_ge(turned, S * i + s + 3)
                    eng.activation(left_hi[:, q, 0:kt * P], turn[:, q, 0:kt * P], ACT.Copy).then_inc(hi_ready, 1)
                elif kind == "turned":
                    eng.wait_ge(left_landed[q], 16 * j + 16)
                    eng.activation(left_hi[:, q, 0:kt * P], left_in[:, q, 0:kt * P], ACT.Copy).then_inc(hi_ready, 1)
                else:
                    eng.activation(left_hi[:, q, :].rearrange("p (t n) -> p t n", t=kt),
                                   resident[:, :, bass.ds(i * P, P)], ACT.Copy).then_inc(hi_ready, 1)

            for s in range(S):
                high(0, 0, 0, s)
            with eng.Fori(0, NT // 2 - 1) as j:
                for k in range(2):
                    i = 2 * j + k
                    for s in range(S):
                        high(i + 1, (j, j + 1)[k], 1 - k, s)
                    if norm:
                        eng.wait_ge(started, 5)
                        eng.wait_ge(eps_added, i + 1)
                        eng.activation(std[:, :], var_eps[:, :], ACT.Sqrt).then_inc(rooted, 1)
            for i in (NT - 2, NT - 1):
                if i < NT - 1:
                    for s in range(S):
                        high(NT - 1, NT // 2 - 1, 1, s)
                if norm:
                    eng.wait_ge(eps_added, i + 1)
                    eng.activation(std[:, :], var_eps[:, :], ACT.Sqrt).then_inc(rooted, 1)

        @block.tensor
        def _(eng):
            eng.sem_inc(started, 1)
            eng.sem_inc(turned, 2)
            eng.sem_inc(multiplied, 2)
            eng.wait_ge(ident_ready, 1)

            def transposes(i, j, k, s):
                if sources[s][0] != "rows":
                    return
                q = (k * S + s) % 2
                eng.wait_ge(started, 5)
                eng.wait_ge(left_landed[q], 16 * (j + 1) if S == 1 else 16 * (i + 1))
                eng.wait_ge(hi_ready, S * i + s + 1)
                eng.wait_ge(lo_ready, S * i + s + 1)
                for t in range(kts[s]):
                    mm = eng.transpose(turn[:, q, t * P:(t + 1) * P], left_in[:, q, t * P:(t + 1) * P], ident[:, :])
                mm.then_inc(turned, 1)

            def products(i, k, s):
                q = (k * S + s) % 2
                first = sum(kts[:s])
                eng.wait_ge(started, 5)
                eng.wait_ge(hi_ready, S * i + s + 3)
                eng.wait_ge(lo_ready, S * i + s + 3)
                if s == 0:
                    eng.wait_ge(y_ready, i + 1)
                for n0 in (0, 512):
                    for t in range(kts[s]):
                        for a, b in ((left_hi, right_hi), (left_hi, right_lo), (left_lo, right_hi)):
                            mm = eng.matmul(acc[:, k, n0:n0 + 512], a[:, q, t * P:(t + 1) * P],
                                            b[:, first + t, n0:n0 + 512],
                                            start=(s == 0 and t == 0 and a is left_hi and b is right_hi),
                                            stop=(s == S - 1 and t == kts[s] - 1 and a is left_lo),
                                            skip_group_check=True)
                mm.then_inc(multiplied, 1)

            for s in range(S):
                transposes(0, 0, 0, s)
            eng.wait_ge(right_hi_ready, KTS)
            eng.wait_ge(right_lo_ready, KTS)
            with eng.Fori(0, NT // 2 - 1) as j:
                for k in range(2):
                    i = 2 * j + k
                    if S == 1:
                        transposes(i + 1, (j, j + 1)[k], 1 - k, 0)
                        products(i, k, 0)
                    else:
                        for s in range(S):
                            products(i, k, s)
                            transposes(i + 1, (j, j + 1)[k], 1 - k, s)
            if S == 1:
                transposes(NT - 1, NT // 2 - 1, 1, 0)
                products(NT - 2, 0, 0)
                products(NT - 1, 1, 0)
            else:
                for s in range(S):
                    products(NT - 2, 0, s)
                    transposes(NT - 1, NT // 2 - 1, 1, s)
                for s in range(S):
                    products(NT - 1, 1, s)

        @block.vector
        def _(eng):
            eng.sem_inc(started, 1)
            eng.sem_inc(lo_ready, 2)
            eng.sem_inc(y_ready, 2)
            eng.sem_inc(y_left[0], 16)
            eng.sem_inc(y_left[1], 16)
            if out_after is not None:
                eng.sem_inc(y2_ready, 2)
                eng.sem_inc(y2_left[0], 16)
                eng.sem_inc(y2_left[1], 16)
            for n in range(KTS):
                eng.wait_ge(right_hi_ready, n + 1)
                eng.tensor_tensor(right_lo[:, n, :], right_in[:, n % 2, :], right_hi[:, n, :].bitcast(F32), ALU.subtract)\
                   .then_inc(right_lo_ready, 1)

            def low(i, k, s):
                kind, kt, q = sources[s][0], kts[s], (k * S + s) % 2
                whole = {"rows": turn, "turned": left_in}.get(kind)
                eng.wait_ge(started, 5)
                eng.wait_ge(hi_ready, S * i + s + 3)
                if whole is not None:
                    eng.tensor_tensor(left_lo[:, q, 0:kt * P], whole[:, q, 0:kt * P],
                                      left_hi[:, q, 0:kt * P].bitcast(F32), ALU.subtract).then_inc(lo_ready, 1)
                else:
                    eng.tensor_tensor(left_lo[:, q, :].rearrange("p (t n) -> p t n", t=kt),
                                      resident[:, :, bass.ds(i * P, P)],
                                      left_hi[:, q, :].rearrange("p (t n) -> p t n", t=kt).bitcast(F32),
                                      ALU.subtract).then_inc(lo_ready, 1)

            def epilogue(i, j, k):
                m = 0
                yk = y[:, k, :]
                cur = acc[:, k, :]
                r = 0

                def link(ins):
                    nonlocal m
                    m += 1
                    if m > LINKS:
                        ins.then_inc(y_ready, 1)
                        return
                    ins.then_inc(chain, 1)
                    due = eng.to_reg(i * LINKS + m) if not isinstance(i, int) else i * LINKS + m
                    eng.wait_ge(started, 5)
                    eng.wait_ge(chain, due)

                eng.wait_ge(started, 5)
                eng.wait_ge(multiplied, S * i + S + 2)
                eng.wait_ge(y_left[k], 16 * j + 16)
                if R:
                    eng.wait_ge(row_landed[k], 16 * R * (j + 1))
                if bias is not None:
                    eng.wait_ge(bias_in, 16)
                if add_first is not None:
                    link(eng.tensor_tensor(yk, cur, row_in[:, k, r, :], ALU.add))
                    cur, r = yk, r + 1
                if scale is not None and bias is not None:
                    link(eng.scalar_tensor_tensor(out=yk, in0=cur, scalar=scale[:, bass.ds(i, 1)], in1=bias_b[:, :],
                                                  op0=ALU.mult, op1=ALU.add))
                    cur = yk
                elif scale is not None:
                    link(eng.tensor_scalar(yk, cur, scale[:, bass.ds(i, 1)], None, ALU.mult))
                    cur = yk
                elif bias is not None:
                    link(eng.tensor_tensor(yk, cur, bias_b[:, :], ALU.add))
                    cur = yk
                if relu:
                    link(eng.tensor_scalar(yk, cur, 0.0, None, ALU.max))
                if add is not None:
                    link(eng.tensor_tensor(yk, cur, row_in[:, k, r, :], ALU.add))
                    cur, r = yk, r + 1
                if norm:
                    eng.bn_stats(stats[:, 0, :], yk[:, 0:512]).then_inc(chain, 1)
                    link(eng.bn_stats(stats[:, 1, :], yk[:, 512:1024]))
                    m += 1
                    due = eng.to_reg(i * LINKS + m) if not isinstance(i, int) else i * LINKS + m
                    eng.wait_ge(started, 5)
                    eng.wait_ge(chain, due)
                    link(eng.bn_aggr(mean_var[:, :], stats[:, :, :].rearrange("p a b -> p (a b)")))
                    eng.tensor_scalar(var_eps[:, :], mean_var[:, 1:2], LN_EPS, None, ALU.add).then_inc(eps_added, 1)
                    eng.wait_ge(started, 5)
                    eng.wait_ge(rooted, i + 1)
                    link(eng.reciprocal(rstd[:, :], std[:, :]))
                    eng.tensor_scalar(yk, yk, mean_var[:, 0:1], rstd[:, 0:1], ALU.subtract, ALU.mult).then_inc(y_ready, 1)
                assert m == OPS + 4 * norm
                if out_after is not None:
                    eng.wait_ge(started, 5)
                    eng.wait_ge(y_ready, i + 3)
                    eng.wait_ge(y2_left[k], 16 * j + 16)
                    eng.tensor_tensor(y2[:, k, :], yk, row_in[:, k, r, :], ALU.add).then_inc(y2_ready, 1)

            for s in range(S):
                low(0, 0, s)
            with eng.Fori(0, NT // 2 - 1) as j:
                for k in range(2):
                    i = 2 * j + k
                    for s in range(S):
                        low(i + 1, 1 - k, s)
                    epilogue(i, j, k)
            for s in range(S):
                low(NT - 1, 1, s)
            epilogue(NT - 2, NT // 2 - 1, 0)
            epilogue(NT - 1, NT // 2 - 1, 1)


def batch_norm_phase(nc, sem, g_tab, gamma, beta, held):
    with ExitStack() as ctx:
        def sb(name, shape):
            return ctx.enter_context(nc.sbuf_tensor("bn_" + name, shape, F32))

        g_in = sb("g_in", [P, NT, D])
        ident = sb("ident", [P, P])
        gam = sb("gam", [P, KT])
        bet = sb("bet", [P, KT])
        PIECE = -(-N_NODES // 3)
        stats = sb("stats", [P, KT, 3, 6])
        mean_var = sb("mean_var", [P, KT, 2])
        var_eps = sb("var_eps", [P, KT])
        std = sb("std", [P, KT])
        factor = sb("factor", [P, KT])
        offset = sb("offset", [P, KT])
        turn = ctx.enter_context(nc.psum_tensor("bn_turn", [P, 2, 3 * 512], F32))

        loaded = [sem(f"bn_loaded{i}") for i in range(NT)]
        consts_in = sem("bn_consts_in")
        filled = sem("bn_filled")
        ident_ready = sem("bn_ident_ready")
        turned = sem("bn_turned")
        copied = sem("bn_copied")
        stated = sem("bn_stated")
        var_ready = sem("bn_var_ready")
        rooted = sem("bn_rooted")
        chain = sem("bn_chain")
        affine_ready = sem("bn_affine_ready")
        normed = sem("bn_normed")

        block = ctx.enter_context(nc.Block())

        @block.sync
        def _(eng):
            for i in range(NT):
                eng.dma_start(g_in[:, i, :], g_tab[i * P:(i + 1) * P, :]).then_inc(loaded[i], 16)
            eng.dma_start(gam[:, :], gamma.rearrange("(k p) -> p k", p=P),
                          allow_slow_non_contiguous=True).then_inc(consts_in, 16)
            eng.dma_start(bet[:, :], beta.rearrange("(k p) -> p k", p=P),
                          allow_slow_non_contiguous=True).then_inc(consts_in, 16)

        @block.gpsimd
        def _(eng):
            eng.memset(ident[:, :], 0.0).then_inc(filled, 1)
            eng.wait_ge(filled, 1)
            eng.affine_select(out=ident[:, :], in_=ident[:, :], compare_op=ALU.not_equal, fill=1.0, base=0,
                              pattern=[[-1, P]], channel_multiplier=1).then_inc(ident_ready, 1)

        @block.tensor
        def _(eng):
            eng.wait_ge(ident_ready, 1)
            for i in range(NT):
                eng.wait_ge(loaded[i], 16)
            for t in range(KT):
                if t >= 2:
                    eng.wait_ge(copied, t - 1)
                for i in range(NT):
                    mm = eng.transpose(turn[:, t % 2, i * P:(i + 1) * P], g_in[:, i, t * P:(t + 1) * P], ident[:, :])
                mm.then_inc(turned, 1)

        @block.scalar
        def _(eng):
            for t in range(KT):
                eng.wait_ge(turned, t + 1)
                eng.activation(held[:, t, :], turn[:, t % 2, 0:NPAD], ACT.Copy).then_inc(copied, 1)
            eng.wait_ge(var_ready, 1)
            eng.activation(std[:, :], var_eps[:, :], ACT.Sqrt).then_inc(rooted, 1)
            eng.wait_ge(affine_ready, 1)
            for t in range(KT):
                eng.activation(held[:, t, :], held[:, t, :], ACT.Relu, scale=factor[:, t:t + 1],
                               bias=offset[:, t:t + 1]).then_inc(normed, 1)
            eng.wait_ge(normed, KT)

        @block.vector
        def _(eng):
            for t in range(KT):
                eng.wait_ge(copied, t + 1)
                for q in range(3):
                    eng.bn_stats(stats[:, t, q, :], held[:, t, q * PIECE:min((q + 1) * PIECE, N_NODES)])\
                       .then_inc(stated, 1)
                eng.wait_ge(stated, 3 * t + 3)
                eng.bn_aggr(mean_var[:, t, :], stats[:, t, :, :].rearrange("p q s -> p (q s)")).then_inc(chain, 1)
            eng.wait_ge(chain, KT)
            eng.tensor_scalar(var_eps[:, :], mean_var[:, :, 1], LN_EPS, None, ALU.add).then_inc(var_ready, 1)
            eng.wait_ge(rooted, 1)
            eng.reciprocal(factor[:, :], std[:, :]).then_inc(chain, 1)
            eng.wait_ge(consts_in, 32)
            eng.wait_ge(chain, KT + 1)
            eng.tensor_tensor(factor[:, :], factor[:, :], gam[:, :], ALU.mult).then_inc(chain, 1)
            eng.wait_ge(chain, KT + 2)
            eng.tensor_tensor(offset[:, :], mean_var[:, :, 0], factor[:, :], ALU.mult).then_inc(chain, 1)
            eng.wait_ge(chain, KT + 3)
            eng.tensor_tensor(offset[:, :], bet[:, :], offset[:, :], ALU.subtract).then_inc(affine_ready, 1)


def build(nc, stop, x, src, dst, edge_weight, positions, rms_w, w_down, wl, wr, att, w_up,
          w_self0, w_neigh0, b0, w_self1, w_neigh1, b1, sparse_bias, w1, c1, gamma, beta, w2, c2, out):
    taken = []

    def sem(name):
        taken.append(nc.alloc_semaphore(name=name))
        return taken[-1]

    def phase(f, *args, **kwargs):
        f(nc, sem, *args, **kwargs)
        nc.clear_and_free_semaphores(taken)
        nc.all_engine_barrier()
        taken.clear()

    with ExitStack() as ctx:
        def scratch(name, shape, dt=F32):
            return nc.dram_tensor(name, shape, dt, kind="Internal").ap()

        edge_tab = scratch("edge_tab", [NC * P, 4])
        xl_tab = scratch("xl_tab", [NPAD, XW])
        xr_tab = scratch("xr_tab", [NPAD, HID])
        self_tab = scratch("self_tab", [P, NT, HEADS])
        tile_tab = scratch("tile_tab", [1, NG], I32)
        adj_tab = scratch("adj_tab", [NPAD, NPAD])
        wt_tab = scratch("wt_tab", [D, D])
        o_tab = scratch("o_tab", [NPAD, HID])
        rows = {n: scratch(n, [NPAD, D]) for n in ("x1", "mean1", "h1", "mean2", "x2", "x3", "x3p", "s1", "g1", "s2")}
        deg_inv = ctx.enter_context(nc.sbuf_tensor("deg_inv", [P, NT], F32))
        deg_rsqrt = ctx.enter_context(nc.sbuf_tensor("deg_rsqrt", [P, NT], F32))

        phase(prepare_phase, x, src, dst, edge_weight, rms_w, w_down, wl, wr, att,
                      edge_tab, xl_tab, self_tab, xr_tab, tile_tab)
        phase(edge_phase, edge_tab, xl_tab, self_tab, xr_tab, tile_tab, att, adj_tab, wt_tab, o_tab,
                   deg_inv, deg_rsqrt)

        phase(dense_phase, "up_", [("rows", o_tab, w_up)], add=x, norm=True, out=out if stop == 1 else rows["x1"])
        if stop == 1:
            return
        phase(dense_phase, "m1_", [("turned", adj_tab, rows["x1"])], scale=deg_inv, out=rows["mean1"])
        phase(dense_phase, "h1_", [("rows", rows["x1"], w_self0), ("rows", rows["mean1"], w_neigh0)],
                    bias=b0, relu=True, out=rows["h1"])
        phase(dense_phase, "m2_", [("turned", adj_tab, rows["h1"])], scale=deg_inv, out=rows["mean2"])
        phase(dense_phase, "x2_", [("rows", rows["h1"], w_self1), ("rows", rows["mean2"], w_neigh1)],
                    bias=b1, add=rows["x1"], norm=True, out=out if stop == 2 else rows["x2"])
        if stop == 2:
            return
        phase(dense_phase, "x3_", [("rows", rows["x2"], wt_tab)], bias=sparse_bias, add=rows["x2"], norm=True,
                    out=out if stop == 3 else rows["x3"], add_after=positions, out_after=rows["x3p"])
        if stop == 3:
            return
        phase(dense_phase, "s1_", [("rows", rows["x3p"], w1)], scale=deg_rsqrt, out=rows["s1"])
        phase(dense_phase, "g1_", [("turned", adj_tab, rows["s1"])], add_first=rows["s1"], scale=deg_rsqrt,
                    bias=c1, out=rows["g1"])
        with nc.sbuf_tensor("held", [P, KT, NPAD], F32) as held:
            phase(batch_norm_phase, rows["g1"], gamma, beta, held)
            phase(dense_phase, "s2_", [("held", None, w2)], resident=held, scale=deg_rsqrt, out=rows["s2"])
        phase(dense_phase, "g2_", [("turned", adj_tab, rows["s2"])], add_first=rows["s2"], scale=deg_rsqrt,
                    bias=c2, relu=True, add=rows["x3"], norm=True, out=out)


_INS = ["x", "src", "dst", "edge_weight", "positions", "L0_gnn_rms_w", "L0_gnn_W_down", "L0_gnn_Wl", "L0_gnn_Wr",
        "L0_gnn_att", "L0_gnn_W_up", "L1_gnn_W_self0", "L1_gnn_W_neigh0", "L1_gnn_b0", "L1_gnn_W_self1",
        "L1_gnn_W_neigh1", "L1_gnn_b1", "L2_gnn_bias", "L3_gnn_W1", "L3_gnn_b1", "L3_gnn_gamma", "L3_gnn_beta",
        "L3_gnn_W2", "L3_gnn_b2"]
STOP = 4


def kernel(**inputs):
    import numpy as _np
    import concourse.bacc as _bacc
    from concourse import mybir as _mybir
    from concourse.bass_utils import run_bass_kernel_spmd as _run

    pos = _np.arange(N_NODES, dtype=_np.float32)[:, None]
    div = _np.exp(_np.arange(0, D, 2, dtype=_np.float32) * _np.float32(-_np.log(10000.0) / D))
    ang = (pos * div).astype(_np.float32)
    positions = _np.zeros((NPAD, D), _np.float32)
    positions[:N_NODES] = _np.stack([_np.sin(ang), _np.cos(ang)], axis=-1).reshape(N_NODES, D)

    nc = _bacc.Bacc("TRN2", target_bir_lowering=False, num_devices=1)
    arrays, args = {}, []
    for name in _INS:
        if name == "positions":
            a = positions
        else:
            a = _np.ascontiguousarray(inputs[name])
        if name == "x":
            a = _np.pad(a, ((0, NPAD - N_NODES), (0, 0)))
        arrays[f"in_{name}_dram"] = a
        args.append(nc.dram_tensor(f"in_{name}_dram", a.shape, _mybir.dt.from_np(a.dtype), kind="ExternalInput").ap())
    args.append(nc.dram_tensor("out_0_dram", (N_NODES, D), _mybir.dt.float32, kind="ExternalOutput").ap())
    build(nc, STOP, *args)
    r = _run(nc, [arrays], core_ids=[0])
    return r.results[0]["out_0_dram"]
```

```python
from contextlib import ExitStack

import concourse.bass as bass
from concourse import mybir

F32 = mybir.dt.float32
F32R = mybir.dt.float32r
BF16 = mybir.dt.bfloat16
F16 = mybir.dt.float16
I32 = mybir.dt.int32
ALU = mybir.AluOpType
ACT = mybir.ActivationFunctionType
AX = mybir.AxisListType

P = 128
N_NODES = 1250
N_EDGES = 40000
D = 1024
HID = 256
HEADS = 4
HD = HID // HEADS
HW = HD + 1
XW = HEADS * HW
NT = -(-N_NODES // P)
NPAD = NT * P
KT = D // P

EP = 125
EC = N_EDGES // EP
CH = 4
GE = CH * P
NG = (N_EDGES + NT * (GE - 1)) // GE
U = 4
NG += -NG % U
NC = NG * CH
NO_DST = 200.0

LN_EPS = 1e-5
BIG = 1e38


def identity(pool, t, n, filled, made):
    pool.memset(t, 0.0).then_inc(filled, 1)
    pool.wait_ge(filled, 1)
    pool.affine_select(out=t, in_=t, compare_op=ALU.not_equal, fill=1.0, base=0,
                       pattern=[[-1, n]], channel_multiplier=1).then_inc(made, 1)


def prepare_phase(nc, sem, x, src, dst, edge_weight, rms_w, w_down, wl, wr, att,
                  edge_tab, xl_tab, self_tab, xr_tab, tile_tab):
    with ExitStack() as ctx:
        def sb(name, shape, dt):
            return ctx.enter_context(nc.sbuf_tensor("pr_" + name, shape, dt))

        def ps(name, shape):
            return ctx.enter_context(nc.psum_tensor("pr_" + name, shape, F32))

        src_i = sb("src_i", [EP, EC], I32)
        dst_i = sb("dst_i", [EP, EC], I32)
        wgt = sb("wgt", [EP, EC], F32)
        bucket_i = sb("bucket_i", [EP, EC], I32)
        local_i = sb("local_i", [EP, EC], I32)
        bucket = sb("bucket", [EP, EC], F32)
        mask = sb("mask", [EP, NT, EC], F32)
        rank = sb("rank", [EP, NT, EC], F32)
        zeros = sb("zeros", [EP, EC], F32)
        total = sb("total", [EP, NT], F32)
        before = sb("before", [EP, P], F32)
        ones = sb("ones", [P, P], F32)
        count_f = sb("count_f", [P, NT], F32)
        count_i = sb("count_i", [P, NT], I32)
        groups = sb("groups", [P, NT], F32)
        zeros10 = sb("zeros10", [P, NT], F32)
        group_end = sb("group_end", [P, NT], F32)
        base = sb("base", [EP, NT], F32)
        slot = sb("slot", [EP, EC], F32)
        part = sb("part", [EP, EC], F32)
        slot_i = sb("slot_i", [EP, EC], I32)
        record = sb("record", [EP, EC, 4], F32)
        unused = sb("unused", [P, NC, 4], F32)
        iota_g = sb("iota_g", [1, NG], F32)
        tile_f = sb("tile_f", [1, NG], F32)
        tile_i = sb("tile_i", [1, NG], I32)
        SC = 8
        slot_st = sb("slot_st", [EP, 2, SC], I32)
        rec_st = sb("rec_st", [EP, 2, SC * 4], F32)
        ident = sb("ident", [P, P], F32)
        xin = sb("xin", [P, 2, D], F32)
        sq = sb("sq", [P, D], F32)
        ssq = sb("ssq", [P, 2], F32)
        ms = sb("ms", [P, 1], F32)
        rms = sb("rms", [P, 1], F32)
        rinv = sb("rinv", [P, 1], F32)
        xT = sb("xT", [P, D], F32)
        wd = sb("wd", [P, KT, HID], F32)
        rw = sb("rw", [P, KT], F32)
        wlr = sb("wlr", [P, 2, 2 * HID], F32)
        xd = sb("xd", [P, HID], F32)
        xdT = sb("xdT", [P, HID], F32)
        xl = sb("xl", [P, 2, XW], F32)
        xr = sb("xr", [P, 2, HID], F32)
        att_b = sb("att_b", [P, HID], F32)
        msg = sb("msg", [P, HID], F32)
        act_s = sb("act_s", [P, HID], F32)
        prod = sb("prod", [P, HID], F32)
        e_self = sb("e_self", [P, NT, HEADS], F32)

        tp = ps("tp", [P, D])
        pd = ps("pd", [P, HID])
        pt = ps("pt", [P, HID])
        plr = ps("plr", [P, 2 * HID])
        pe = ps("pe", [P, 2 * 16])

        started = sem("pr_started")
        edges_in = sem("pr_edges_in")
        consts_in = sem("pr_consts_in")
        filled = sem("pr_filled")
        idents = sem("pr_idents")
        dve = sem("pr_dve")
        totals = sem("pr_totals")
        prefixes = sem("pr_prefixes")
        slots_ready = sem("pr_slots_ready")
        unused_ready = sem("pr_unused_ready")
        unused_out = sem("pr_unused_out")
        tiles_ready = sem("pr_tiles_ready")
        staged = sem("pr_staged")
        scattered = [sem(f"pr_scattered{k}") for k in range(2)]
        x_in = [sem(f"pr_x_in{k}") for k in range(2)]
        x_used = sem("pr_x_used")
        squared = sem("pr_squared")
        x_turned = sem("pr_x_turned")
        xT_ready = sem("pr_xT_ready")
        wd_ready = sem("pr_wd_ready")
        down = sem("pr_down")
        ms_ready = sem("pr_ms_ready")
        rms_ready = sem("pr_rms_ready")
        xd_ready = sem("pr_xd_ready")
        xd_turned = sem("pr_xd_turned")
        xdT_ready = sem("pr_xdT_ready")
        lr = sem("pr_lr")
        xl_ready = sem("pr_xl_ready")
        xr_ready = sem("pr_xr_ready")
        self_msg = sem("pr_self_msg")
        self_act = sem("pr_self_act")
        self_ready = sem("pr_self_ready")
        xl_ones = sem("pr_xl_ones")
        tabs_out = [sem(f"pr_tabs_out{k}") for k in range(2)]
        last_out = sem("pr_last_out")

        block = ctx.enter_context(nc.Block())

        @block.sync
        def _(eng):
            eng.dma_start(dst_i[:, :], dst.rearrange("(p c) -> p c", p=EP)).then_inc(edges_in, 16)
            eng.dma_start(src_i[:, :], src.rearrange("(p c) -> p c", p=EP)).then_inc(edges_in, 16)
            eng.dma_start(wgt[:, :], edge_weight.rearrange("(p c) -> p c", p=EP)).then_inc(edges_in, 16)
            eng.dma_start(wd[:, :, :], w_down.rearrange("(k p) n -> p k n", p=P)).then_inc(consts_in, 16)
            eng.dma_start(rw[:, :], rms_w.rearrange("(k p) -> p k", p=P),
                          allow_slow_non_contiguous=True).then_inc(consts_in, 16)
            eng.dma_start(wlr[:, :, 0:HID], wl.rearrange("(k p) n -> p k n", p=P)).then_inc(consts_in, 16)
            eng.dma_start(wlr[:, :, HID:2 * HID], wr.rearrange("(k p) n -> p k n", p=P)).then_inc(consts_in, 16)
            eng.dma_start(att_b[:, :], att.rearrange("h d -> (h d)").partition_broadcast(P)).then_inc(consts_in, 16)
            eng.wait_ge(unused_ready, 1)
            eng.dma_start(edge_tab.rearrange("(p c) w -> p c w", p=P), unused[:, :, :]).then_inc(unused_out, 16)
            eng.wait_ge(started, 3)
            with eng.Fori(0, NT // 2) as j:
                for k in range(2):
                    i = 2 * j + k
                    eng.wait_ge(started, 3)
                    eng.wait_ge(x_used, i + 1)
                    eng.dma_start(xin[:, k, :], x[bass.ds(i * P, P), :]).then_inc(x_in[k], 16)
            eng.wait_ge(tiles_ready, 1)
            eng.dma_start(tile_tab, tile_i[:, :]).then_inc(last_out, 16)
            eng.wait_ge(self_ready, NT)
            eng.dma_start(self_tab, e_self[:, :, :]).then_inc(last_out, 16)
            eng.wait_ge(last_out, 32)

        @block.gpsimd
        def _(eng):
            eng.sem_inc(x_used, 2)
            eng.sem_inc(started, 1)
            eng.memset(unused[:, :, :], 0.0).then_inc(filled, 1)
            eng.memset(ident[:, :], 0.0).then_inc(filled, 1)
            eng.memset(before[:, :], 1.0).then_inc(filled, 1)
            eng.memset(ones[:, :], 1.0).then_inc(filled, 1)
            eng.wait_ge(filled, 4)
            eng.memset(unused[:, :, 1], NO_DST).then_inc(unused_ready, 1)
            eng.affine_select(out=ident[:, :], in_=ident[:, :], compare_op=ALU.not_equal, fill=1.0, base=0,
                              pattern=[[-1, P]], channel_multiplier=1).then_inc(idents, 1)
            eng.affine_select(out=before[:, :], in_=before[:, :], compare_op=ALU.is_gt, fill=0.0, base=0,
                              pattern=[[1, P]], channel_multiplier=-1).then_inc(idents, 1)
            eng.iota(iota_g[:, :], [[1, NG]], base=0, channel_multiplier=0,
                     allow_small_or_imprecise_dtypes=True).then_inc(idents, 1)
            eng.memset(xl[:, :, :], 1.0).then_inc(xl_ones, 1)
            eng.wait_ge(slots_ready, 1)
            eng.wait_ge(unused_out, 16)
            for k in range(2):
                eng.tensor_copy(slot_st[:, k, :], slot_i[:, k * SC:(k + 1) * SC]).then_inc(staged, 1)
                eng.tensor_copy(rec_st[:, k, :], record[:, k * SC:(k + 1) * SC, :].rearrange("p c w -> p (c w)"))\
                   .then_inc(staged, 1)
                eng.wait_ge(staged, 2 * k + 2)
                for s in range(SC):
                    eng.indirect_dma_start(edge_tab, bass.IndirectOffsetOnAxis(ap=slot_st[:, k, s:s + 1], axis=0),
                                           rec_st[:, k, s * 4:s * 4 + 4], None).then_inc(scattered[k], 16)
            with eng.Fori(1, EC // (2 * SC)) as j:
                for k in range(2):
                    i = 2 * j + k
                    eng.wait_ge(unused_out, 16)
                    eng.wait_ge(scattered[k], 16 * SC * j)
                    eng.tensor_copy(slot_st[:, k, :], slot_i[:, bass.ds(i * SC, SC)]).then_inc(staged, 1)
                    eng.tensor_copy(rec_st[:, k, :], record[:, bass.ds(i * SC, SC), :].rearrange("p c w -> p (c w)"))\
                       .then_inc(staged, 1)
                    due = eng.to_reg(i * 2 + 2)
                    eng.wait_ge(unused_out, 16)
                    eng.wait_ge(staged, due)
                    for s in range(SC):
                        eng.indirect_dma_start(edge_tab, bass.IndirectOffsetOnAxis(ap=slot_st[:, k, s:s + 1], axis=0),
                                               rec_st[:, k, s * 4:s * 4 + 4], None).then_inc(scattered[k], 16)
            for k in range(2):
                eng.wait_ge(scattered[k], 16 * EC // 2)

        @block.scalar
        def _(eng):
            eng.sem_inc(started, 1)
            eng.sem_inc(rms_ready, 1)
            eng.wait_ge(started, 3)
            with eng.Fori(0, NT // 2) as j:
                for k in range(2):
                    i = 2 * j + k
                    eng.wait_ge(started, 3)
                    eng.wait_ge(x_in[k], 16 * j + 16)
                    eng.wait_ge(ms_ready, i + 1)
                    eng.activation(sq[:, :], xin[:, k, :], ACT.Square, accum_out=ssq[:, 0:1]).then_inc(squared, 1)
                    eng.wait_ge(started, 3)
                    eng.wait_ge(x_turned, i + 1)
                    eng.activation(xT[:, :], tp[:, :], ACT.Copy).then_inc(xT_ready, 1)
                    eng.wait_ge(started, 3)
                    eng.wait_ge(ms_ready, i + 2)
                    eng.activation(rms[:, :], ms[:, :], ACT.Sqrt).then_inc(rms_ready, 1)
                    eng.wait_ge(started, 3)
                    eng.wait_ge(xr_ready, i + 1)
                    eng.dma_start(xl_tab[bass.ds(i * P, P), :], xl[:, k, :]).then_inc(tabs_out[k], 16)
                    eng.dma_start(xr_tab[bass.ds(i * P, P), :], xr[:, k, :]).then_inc(tabs_out[k], 16)
            for k in range(2):
                eng.wait_ge(tabs_out[k], 32 * (NT // 2) + 32)

        @block.tensor
        def _(eng):
            eng.sem_inc(started, 1)
            eng.wait_ge(idents, 3)
            eng.wait_ge(totals, 1)
            eng.matmul(pe[:, 0:NT], before[:, :], total[:, :], start=True, stop=True).then_inc(prefixes, 1)
            eng.matmul(pe[:, 16:16 + NT], ones[0:EP, :], total[:, :], start=True, stop=True).then_inc(prefixes, 1)
            eng.wait_ge(wd_ready, KT)
            with eng.Fori(0, NT // 2) as j:
                for k in range(2):
                    i = 2 * j + k
                    eng.wait_ge(started, 3)
                    eng.wait_ge(squared, i + 1)
                    for t in range(KT):
                        mm = eng.transpose(tp[:, t * P:(t + 1) * P], xin[:, k, t * P:(t + 1) * P], ident[:, :])
                    mm.then_inc(x_turned, 1)
                    eng.wait_ge(started, 3)
                    eng.wait_ge(xT_ready, i + 1)
                    for t in range(KT):
                        mm = eng.matmul(pd[:, :], xT[:, t * P:(t + 1) * P], wd[:, t, :],
                                        start=(t == 0), stop=(t == KT - 1))
                        if t == 0:
                            mm.then_inc(x_used, 1)
                    mm.then_inc(down, 1)
                    eng.wait_ge(started, 3)
                    eng.wait_ge(xd_ready, i + 1)
                    for t in range(2):
                        mm = eng.transpose(pt[:, t * P:(t + 1) * P], xd[:, t * P:(t + 1) * P], ident[:, :])
                    mm.then_inc(xd_turned, 1)
                    eng.wait_ge(started, 3)
                    eng.wait_ge(xdT_ready, i + 1)
                    for t in range(2):
                        mm = eng.matmul(plr[:, :], xdT[:, t * P:(t + 1) * P], wlr[:, t, :],
                                        start=(t == 0), stop=(t == 1))
                    mm.then_inc(lr, 1)

        @block.vector
        def _(eng):
            eng.sem_inc(ms_ready, 1)
            eng.sem_inc(tabs_out[0], 32)
            eng.sem_inc(tabs_out[1], 32)
            n = 0

            def step(ins):
                nonlocal n
                n += 1
                ins.then_inc(dve, 1)
                eng.wait_ge(dve, n)

            eng.wait_ge(edges_in, 48)
            step(eng.tensor_scalar(bucket_i[:, :], dst_i[:, :], 7, None, ALU.logical_shift_right))
            step(eng.tensor_scalar(local_i[:, :], dst_i[:, :], P - 1, None, ALU.bitwise_and))
            step(eng.tensor_copy(bucket[:, :], bucket_i[:, :]))
            step(eng.tensor_copy(record[:, :, 0], src_i[:, :]))
            step(eng.tensor_copy(record[:, :, 1], local_i[:, :]))
            step(eng.tensor_copy(record[:, :, 2], wgt[:, :]))
            step(eng.memset(record[:, :, 3], 0.0))
            step(eng.memset(zeros[:, :], 0.0))
            step(eng.memset(zeros10[:, :], 0.0))
            for b in range(NT):
                step(eng.tensor_scalar(mask[:, b, :], bucket[:, :], float(b), None, ALU.is_equal))
                step(eng.tensor_tensor_scan(rank[:, b, :], mask[:, b, :], zeros[:, :], 0.0, ALU.add, ALU.add))
            eng.tensor_copy(total[:, :], rank[:, :, EC - 1]).then_inc(totals, 1)
            eng.wait_ge(prefixes, 2)
            step(eng.tensor_scalar(count_f[:, :], pe[:, 16:16 + NT], float(GE - 1), None, ALU.add))
            step(eng.tensor_copy(count_i[:, :], count_f[:, :]))
            step(eng.tensor_scalar(count_i[:, :], count_i[:, :], GE.bit_length() - 1, None, ALU.logical_shift_right))
            step(eng.tensor_copy(groups[:, :], count_i[:, :]))
            step(eng.tensor_tensor_scan(group_end[:, :], groups[:, :], zeros10[:, :], 0.0, ALU.add, ALU.add))
            step(eng.tensor_tensor(groups[:, :], group_end[:, :], groups[:, :], ALU.subtract))
            step(eng.tensor_scalar(base[:, :], groups[0:EP, :], float(GE), -1.0, ALU.mult, ALU.add))
            step(eng.tensor_tensor(base[:, :], base[:, :], pe[0:EP, 0:NT], ALU.add))
            for b in range(NT):
                o = slot if b == 0 else part
                step(eng.scalar_tensor_tensor(out=o[:, :], in0=rank[:, b, :], scalar=base[:, b:b + 1],
                                              in1=mask[:, b, :], op0=ALU.add, op1=ALU.mult))
                if b:
                    step(eng.tensor_tensor(slot[:, :], slot[:, :], part[:, :], ALU.add))
            eng.tensor_copy(slot_i[:, :], slot[:, :]).then_inc(slots_ready, 1)
            step(eng.memset(tile_f[:, :], 0.0))
            eng.wait_ge(idents, 3)
            for b in range(NT - 1):
                step(eng.scalar_tensor_tensor(out=tile_f[:, :], in0=iota_g[:, :], scalar=group_end[0:1, b:b + 1],
                                              in1=tile_f[:, :], op0=ALU.is_ge, op1=ALU.add))
            eng.tensor_copy(tile_i[:, :], tile_f[:, :]).then_inc(tiles_ready, 1)

            eng.wait_ge(consts_in, 80)
            for t in range(KT):
                eng.tensor_scalar(wd[:, t, :], wd[:, t, :], rw[:, t:t + 1], None, ALU.mult).then_inc(wd_ready, 1)
            eng.wait_ge(xl_ones, 1)
            with eng.Fori(0, NT // 2) as j:
                for k in range(2):
                    i = 2 * j + k
                    eng.wait_ge(xl_ones, 1)
                    eng.wait_ge(squared, i + 1)
                    eng.wait_ge(rms_ready, i + 1)
                    eng.tensor_scalar(ms[:, :], ssq[:, 0:1], 1.0 / D, 1e-6, ALU.mult, ALU.add).then_inc(ms_ready, 1)
                    eng.wait_ge(xl_ones, 1)
                    eng.wait_ge(rms_ready, i + 2)
                    eng.reciprocal(rinv[:, :], rms[:, :]).then_inc(dve, 1)
                    eng.wait_ge(dve, n + 3 * i + 1)
                    eng.wait_ge(down, i + 1)
                    eng.tensor_scalar(xd[:, :], pd[:, :], rinv[:, 0:1], None, ALU.mult).then_inc(xd_ready, 1)
                    eng.wait_ge(xl_ones, 1)
                    eng.wait_ge(xd_turned, i + 1)
                    eng.tensor_copy(xdT[:, :], pt[:, :]).then_inc(xdT_ready, 1)
                    eng.wait_ge(xl_ones, 1)
                    eng.wait_ge(lr, i + 1)
                    eng.wait_ge(tabs_out[k], 32 * j + 32)
                    eng.tensor_copy(xl[:, k, :].rearrange("p (h w) -> p h w", h=HEADS)[:, :, 0:HD],
                                    plr[:, 0:HID].rearrange("p (h d) -> p h d", h=HEADS)).then_inc(dve, 1)
                    eng.tensor_copy(xr[:, k, :], plr[:, HID:2 * HID]).then_inc(xr_ready, 1)
                    eng.wait_ge(xl_ones, 1)
                    eng.wait_ge(dve, n + 3 * i + 2)
                    eng.wait_ge(xr_ready, i + 1)
                    eng.tensor_tensor(msg[:, :].rearrange("p (h d) -> p h d", h=HEADS),
                                      xl[:, k, :].rearrange("p (h w) -> p h w", h=HEADS)[:, :, 0:HD],
                                      xr[:, k, :].rearrange("p (h d) -> p h d", h=HEADS), ALU.add)\
                       .then_inc(self_msg, 1)
                    eng.wait_ge(xl_ones, 1)
                    eng.wait_ge(self_msg, i + 1)
                    eng.scalar_tensor_tensor(out=act_s[:, :], in0=msg[:, :], scalar=0.2, in1=msg[:, :],
                                             op0=ALU.mult, op1=ALU.max).then_inc(self_act, 1)
                    eng.wait_ge(xl_ones, 1)
                    eng.wait_ge(self_act, i + 1)
                    eng.tensor_tensor(prod[:, :], act_s[:, :], att_b[:, :], ALU.mult).then_inc(dve, 1)
                    eng.wait_ge(xl_ones, 1)
                    eng.wait_ge(dve, n + 3 * i + 3)
                    eng.tensor_reduce(e_self[:, bass.ds(i, 1), :].rearrange("p a h -> p (a h)"),
                                      prod[:, :].rearrange("p (h d) -> p h d", h=HEADS), AX.X, ALU.add)\
                       .then_inc(self_ready, 1)


def edge_phase(nc, sem, edge_tab, xl_tab, self_tab, xr_tab, tile_tab, att, adj_tab, wt_tab, o_tab,
               deg_inv, deg_rsqrt):
    with ExitStack() as ctx:
        def sb(name, shape, dt):
            return ctx.enter_context(nc.sbuf_tensor("ed_" + name, shape, dt))

        def ps(name, shape):
            return ctx.enter_context(nc.psum_tensor("ed_" + name, shape, F32))

        src_f = sb("src_f", [P, NC], F32)
        src_i = sb("src_i", [P, NC], I32)
        loc = sb("loc", [P, NC], F32)
        w_b = sb("w_b", [P, NC], BF16)
        w_part = sb("w_part", [P, 3, NC], F32)
        tiles = sb("tiles", [1, NG], I32)
        iota_n = sb("iota_n", [P, NPAD], F16)
        ident = sb("ident", [P, P], F32)
        ident_r = sb("ident_r", [P, P], F32R)
        att_b = sb("att_b", [P, HID], F32)
        src_st = sb("src_st", [P, U, CH], I32)
        gat = sb("gat", [P, U * CH * XW], F32)
        hot_s = sb("hot_s", [P, 2, CH, NPAD], BF16)
        hot_b = sb("hot_b", [P, 2, CH, 4, P], BF16)
        hot_f = sb("hot_f", [P, U, CH, P], F32)
        hot_t = sb("hot_t", [P, 2, CH, P], F32R)
        bound = sb("bound", [P, 2, CH, P], F32)
        xr_hi = sb("xr_hi", [P, NT, HID], F32R)
        xr_lo = sb("xr_lo", [P, NT, HID], F32R)
        work = sb("work", [P, 2, NPAD], F32)
        score = sb("score", [P, 2, CH * HEADS], F32)
        score_r = sb("score_r", [P, 2, CH * HEADS], F32R)
        masked = sb("masked", [P, CH * P], F32)
        group_max = sb("group_max", [P, HEADS], F32)
        new_max = sb("new_max", [P, HEADS], F32)
        shift = sb("shift", [P, HEADS], F32)
        fade = sb("fade", [P, HEADS], F32)
        max_r = sb("max_r", [P, HEADS], F32R)
        expo = sb("expo", [P, CH * HEADS], F32)
        prob = sb("prob", [P, CH * HEADS], F32)
        seg_max = sb("seg_max", [P, NT * HEADS], F32)
        seg_max_r = sb("seg_max_r", [P, NT * HEADS], F32R)
        self_prob = sb("self_prob", [P, NT * HEADS], F32)
        seg_sum = sb("seg_sum", [P, NT, XW], F32)
        adj = sb("adj", [P, NT, NPAD], F32)
        wt = sb("wt", [P, NT, D], F32)

        p_adj = ps("p_adj", [P, 3 * 512])
        p_wt = ps("p_wt", [P, D])
        bank_x = ps("bank_x", [P, 512])
        bank_y = ps("bank_y", [P, 512])
        bank_z = ps("bank_z", [P, 512])

        tabs_in = sem("ed_tabs_in")
        filled = sem("ed_filled")
        consts = sem("ed_consts")
        dve = sem("ed_dve")
        ready = sem("ed_ready")
        tiles_in = sem("ed_tiles_in")
        staged = sem("ed_staged")
        gathered = [sem(f"ed_gathered{u}") for u in range(U)]
        hots = sem("ed_hots")
        turned = sem("ed_turned")
        turned_out = sem("ed_turned_out")
        self_ready = sem("ed_self_ready")
        xr_done = sem("ed_xr_done")
        xr_ready = sem("ed_xr_ready")
        msg_ready = sem("ed_msg_ready")
        relu_ready = sem("ed_relu_ready")
        act_added = sem("ed_act_added")
        act_scaled = sem("ed_act_scaled")
        local_hots = sem("ed_local_hots")
        parts_ready = sem("ed_parts_ready")
        wt_cleared = sem("ed_wt_cleared")
        score_ready = sem("ed_score_ready")
        spread = sem("ed_spread")
        head_max = sem("ed_head_max")
        shift_ready = sem("ed_shift_ready")
        fade_ready = sem("ed_fade_ready")
        max_ready = sem("ed_max_ready")
        max_back = sem("ed_max_back")
        expo_ready = sem("ed_expo_ready")
        prob_ready = sem("ed_prob_ready")
        weighted = sem("ed_weighted")
        summed = sem("ed_summed")
        sums_added = sem("ed_sums_added")
        counted = sem("ed_counted")
        counts_added = sem("ed_counts_added")
        loop_done = sem("ed_loop_done")
        adj_st_ready = sem("ed_adj_st_ready")
        adj_turned = sem("ed_adj_turned")
        adj_t_ready = sem("ed_adj_t_ready")
        adj_out = [sem(f"ed_adj_out{k}") for k in range(2)]
        deg_done = sem("ed_deg_done")
        root = sem("ed_root")
        o_ready = sem("ed_o_ready")
        last_out = sem("ed_last_out")

        deg = sb("deg", [P, NT], F32)
        deg1 = sb("deg1", [P, NT], F32)
        droot = sb("droot", [P, NT], F32)
        den = sb("den", [P, NT, HEADS], F32)
        xlg = gat[:, :].rearrange("p (u c w) -> p u c w", u=U, c=CH)
        msg = work[:, 0, 0:CH * HID]
        act_m = work[:, 1, 0:CH * HID]
        w_rest = masked[:, 0:NC]
        slots = wt[:, :, :].rearrange("p t n -> p (t n)")[:, 0:NC * 4].rearrange("p (c w) -> p c w", w=4)
        adj_st = work
        adj_t = gat[:, 0:2 * NPAD].rearrange("p (k n) -> p k n", k=2)

        block = ctx.enter_context(nc.Block())

        @block.sync
        def _(eng):
            eng.dma_start(wt[:, :, :].rearrange("p t n -> p (t n)")[:, 0:NC * 4].rearrange("p (g w) -> p g w", w=4 * CH),
                          edge_tab.rearrange("(g p c) w -> p g (c w)", p=P, c=CH)).then_inc(tabs_in, 16)
            eng.dma_start(seg_max[:, :], self_tab.rearrange("p t h -> p (t h)")).then_inc(tabs_in, 16)
            eng.dma_start(seg_sum[:, :, :], xl_tab.rearrange("(t p) w -> p t w", p=P)).then_inc(tabs_in, 16)
            eng.dma_start(adj[:, 0:2, :].rearrange("p a n -> p (a n)").rearrange("p (t n) -> p t n", t=NT),
                          xr_tab.rearrange("(t p) n -> p t n", p=P)).then_inc(tabs_in, 16)
            eng.dma_start(att_b[:, :], att.rearrange("h d -> (h d)").partition_broadcast(P)).then_inc(tabs_in, 16)
            eng.dma_start(tiles[:, :], tile_tab).then_inc(tiles_in, 16)
            eng.wait_ge(counts_added, NG + 1)
            for t in range(D // P):
                eng.dma_start(wt_tab[t * P:(t + 1) * P, :], wt[:, t, :]).then_inc(last_out, 16)
            with eng.Fori(0, NT // 2) as j:
                for k in range(2):
                    i = 2 * j + k
                    eng.wait_ge(tiles_in, 16)
                    eng.wait_ge(adj_t_ready, i + 2)
                    eng.dma_start(adj_tab[bass.ds(i * P, P), :], adj_t[:, k, :]).then_inc(adj_out[k], 16)
            eng.wait_ge(o_ready, 1)
            for h in range(HEADS):
                eng.dma_start(o_tab.rearrange("(t p) (h d) -> p t h d", p=P, h=HEADS)[:, :, h, :],
                              seg_sum[:, :, h * HW:h * HW + HD]).then_inc(last_out, 16)
            for k in range(2):
                eng.wait_ge(adj_out[k], 16 * (NT // 2) + 16)
            eng.wait_ge(last_out, 16 * (D // P + HEADS))

        @block.gpsimd
        def _(eng):
            eng.memset(ident[:, :], 0.0).then_inc(filled, 1)
            eng.iota(iota_n[:, :], [[1, NPAD]], base=0, channel_multiplier=0,
                     allow_small_or_imprecise_dtypes=True).then_inc(consts, 1)
            eng.wait_ge(filled, 1)
            eng.affine_select(out=ident[:, :], in_=ident[:, :], compare_op=ALU.not_equal, fill=1.0, base=0,
                              pattern=[[-1, P]], channel_multiplier=1).then_inc(consts, 1)
            eng.wait_ge(ready, 1)
            eng.memset(wt[:, :, :], 0.0).then_inc(wt_cleared, 1)

            def gather(g, u):
                eng.wait_ge(ready, 1)
                eng.tensor_copy(src_st[:, u, :], src_i[:, bass.ds(g * CH, CH)]).then_inc(staged, 1)
                due = eng.to_reg(g + 1) if not isinstance(g, int) else g + 1
                eng.wait_ge(ready, 1)
                eng.wait_ge(staged, due)
                for c in range(CH):
                    eng.indirect_dma_start(xlg[:, u, c, :], None, xl_tab,
                                           bass.IndirectOffsetOnAxis(ap=src_st[:, u, c:c + 1], axis=0))\
                       .then_inc(gathered[u], 16)

            def weigh(g):
                eng.wait_ge(ready, 1)
                eng.wait_ge(relu_ready, g + 1)
                eng.tensor_tensor(act_m, msg, act_m, ALU.add).then_inc(act_added, 1)
                eng.wait_ge(ready, 1)
                eng.wait_ge(act_added, g + 1)
                eng.tensor_tensor(act_m.rearrange("p (c d) -> p c d", c=CH), act_m.rearrange("p (c d) -> p c d", c=CH),
                                  att_b[:, :].unsqueeze(1).broadcast_to([P, CH, HID]), ALU.mult).then_inc(act_scaled, 1)

            for g in range(3):
                gather(g, g)
            weigh(0)

            def body(g, u):
                if not isinstance(g, int) or g + 1 < NG:
                    weigh(g + 1)
                if not isinstance(g, int) or g + 3 < NG:
                    eng.wait_ge(summed, g + 1)
                    gather(g + 3, (u + 3) % U)

            with eng.Fori(0, NG // U - 1) as j:
                for u in range(U):
                    body(U * j + u, u)
            for u in range(U):
                body(NG - U + u, u)

        @block.scalar
        def _(eng):
            eng.wait_ge(consts, 2)
            eng.activation(ident_r[:, :], ident[:, :], ACT.Copy).then_inc(consts, 1)

            def turn_out(g, k):
                eng.wait_ge(ready, 1)
                eng.wait_ge(turned, g + 1)
                turned_bank = bank_x[:, :].rearrange("p (c e) -> p c e", c=CH)
                eng.activation(hot_t[:, k, :, :], turned_bank, ACT.Copy).then_inc(turned_out, 1)
                eng.activation(bound[:, k, :, :], turned_bank, ACT.Copy, scale=BIG, bias=-BIG).then_inc(turned_out, 1)

            def relu(g):
                eng.wait_ge(msg_ready, 2 * g + 2)
                if not isinstance(g, int) or g > 0:
                    eng.wait_ge(score_ready, g)
                eng.activation(act_m, msg, ACT.Relu, scale=4.0).then_inc(relu_ready, 1)

            def parts(g, u, c):
                k, at = u % 2, g * CH + c
                eng.wait_ge(ready, 1)
                eng.wait_ge(local_hots, at + 1)
                eng.wait_ge(counted, at + 1)
                eng.activation(hot_b[:, k, c, 0, :], hot_f[:, u, c, :], ACT.Copy)
                for q in range(3):
                    a = eng.activation(hot_b[:, k, c, 1 + q, :], hot_f[:, u, c, :], ACT.Copy,
                                       scale=w_part[:, q, bass.ds(at, 1)])
                a.then_inc(parts_ready, 1)

            def body(g, u):
                if not isinstance(g, int) or g + 1 < NG:
                    relu(g + 1)
                    for c in range(3):
                        parts(g + 1, (u + 1) % U, c)
                eng.wait_ge(ready, 1)
                eng.wait_ge(shift_ready, g + 1)
                eng.activation(fade[:, :], shift[:, :], ACT.Exp).then_inc(fade_ready, 1)
                eng.wait_ge(ready, 1)
                eng.wait_ge(expo_ready, g + 1)
                eng.activation(prob[:, :], expo[:, :], ACT.Exp).then_inc(prob_ready, 1)
                if not isinstance(g, int) or g + 1 < NG:
                    parts(g + 1, (u + 1) % U, 3)
                if not isinstance(g, int) or g + 2 < NG:
                    turn_out(g + 2, u % 2)

            eng.wait_ge(ready, 1)
            eng.activation(self_prob[:, :], self_prob[:, :], ACT.Exp).then_inc(self_ready, 1)
            turn_out(0, 0)
            relu(0)
            for c in range(CH):
                parts(0, 0, c)
            turn_out(1, 1)
            with eng.Fori(0, NG // U - 1) as j:
                for u in range(U):
                    body(U * j + u, u)
            for u in range(U):
                body(NG - U + u, u)
            eng.wait_ge(deg_done, 4)
            eng.activation(droot[:, :], deg1[:, :], ACT.Sqrt).then_inc(root, 1)
            with eng.Fori(0, NT // 2) as j:
                for k in range(2):
                    i = 2 * j + k
                    eng.wait_ge(counts_added, NG + 1)
                    eng.wait_ge(adj_turned, i + 1)
                    eng.activation(adj_st[:, k, :], adj[:, bass.ds(i, 1), :].rearrange("p a n -> p (a n)"),
                                   ACT.Copy).then_inc(adj_st_ready, 1)

        @block.tensor
        def _(eng):
            eng.sem_inc(counted, 2 * CH)
            eng.sem_inc(adj_turned, 2)
            eng.sem_inc(summed, 1)

            def turn(g, u):
                eng.wait_ge(ready, 1)
                eng.wait_ge(local_hots, CH * g + CH)
                for c in range(CH):
                    mm = eng.transpose(bank_x[:, c * P:(c + 1) * P], hot_f[:, u, c, :], ident[:, :])
                mm.then_inc(turned, 1)

            def destinations(g, u):
                k = u % 2
                t = eng.value_load(tiles[0:1, bass.ds(g, 1)], min_val=0, max_val=NT - 1)
                eng.wait_ge(ready, 1)
                eng.wait_ge(turned_out, 2 * g + 1)
                if not isinstance(g, int) or g > 0:
                    eng.wait_ge(sums_added, g)
                for c in range(CH):
                    bank = (bank_y, bank_z)[c // 2]
                    for q, part in enumerate((xr_hi, xr_lo)):
                        mm = eng.matmul(bank[:, (c % 2) * HID:(c % 2 + 1) * HID], hot_t[:, k, c, :],
                                        part[:, bass.ds(t, 1), :].rearrange("p a n -> p (a n)"),
                                        start=(q == 0), stop=(q == 1))
                    if c % 2 == 1:
                        mm.then_inc(xr_done, 1)

            def counts(g, u, c):
                k = u % 2
                eng.wait_ge(ready, 1)
                if c == 0:
                    eng.wait_ge(counts_added, g + 1)
                eng.wait_ge(hots, CH * g + c + 1)
                eng.wait_ge(parts_ready, CH * g + c + 1)
                for n0, n1 in ((0, 512), (512, 1024), (1024, N_NODES)):
                    eng.matmul(p_adj[:, n0:n1], hot_b[:, k, c, 0, :], hot_s[:, k, c, n0:n1],
                               start=(c == 0), stop=(c == CH - 1))
                for q in range(3):
                    for n0 in (0, 512):
                        mm = eng.matmul(p_wt[:, n0:n0 + 512], hot_b[:, k, c, 1 + q, :], hot_s[:, k, c, n0:n0 + 512],
                                        start=(c == 0 and q == 0), stop=(c == CH - 1 and q == 2))
                mm.then_inc(counted, 1)

            def spread_head(g, u, h):
                bank = (bank_x, bank_y, bank_z, bank_x)[h]
                for c in range(CH):
                    mm = eng.matmul(bank[:, c * P:(c + 1) * P],
                                    score_r[:, u % 2, c * HEADS + h:c * HEADS + h + 1].broadcast_to([P, P]),
                                    ident_r[:, :], start=True, stop=True)
                mm.then_inc(spread, 1)

            def body(g, u):
                more = not isinstance(g, int) or g + 1 < NG
                if more:
                    destinations(g + 1, (u + 1) % U)
                    eng.wait_ge(ready, 1)
                    eng.wait_ge(turned_out, 2 * g + 4)
                eng.wait_ge(ready, 1)
                eng.wait_ge(score_ready, g + 1)
                spread_head(g, u, 0)
                counts(g, u, 0)
                if more:
                    eng.wait_ge(ready, 1)
                    eng.wait_ge(msg_ready, 2 * g + 4)
                else:
                    eng.wait_ge(sums_added, g + 1)
                for h in (1, 2):
                    spread_head(g, u, h)
                counts(g, u, 1)
                eng.wait_ge(ready, 1)
                eng.wait_ge(head_max, HEADS * g + 1)
                spread_head(g, u, 3)
                counts(g, u, 2)
                eng.wait_ge(ready, 1)
                eng.wait_ge(max_ready, g + 1)
                for c in range(CH):
                    mm = eng.matmul(bank_z[:, c * HEADS:(c + 1) * HEADS], hot_t[:, u % 2, c, :], max_r[:, :],
                                    start=True, stop=True)
                mm.then_inc(max_back, 1)
                counts(g, u, 3)
                if not isinstance(g, int) or g + 2 < NG:
                    turn(g + 2, (u + 2) % U)
                eng.wait_ge(ready, 1)
                eng.wait_ge(weighted, g + 1)
                for c in range(CH):
                    mm = eng.matmul(bank_y[:, 0:XW], hot_f[:, u, c, :], xlg[:, u, c, :],
                                    start=(c == 0), stop=(c == CH - 1))
                mm.then_inc(summed, 1)

            eng.wait_ge(consts, 3)
            eng.wait_ge(tiles_in, 16)
            turn(0, 0)
            eng.wait_ge(xr_ready, 1)
            destinations(0, 0)
            eng.wait_ge(turned_out, 2)
            turn(1, 1)
            with eng.Fori(0, NG // U - 1) as j:
                for u in range(U):
                    body(U * j + u, u)
            for u in range(U):
                body(NG - U + u, u)
            with eng.Fori(0, NT // 2) as j:
                for k in range(2):
                    i = 2 * j + k
                    eng.wait_ge(counts_added, NG + 1)
                    eng.wait_ge(adj_st_ready, i + 1)
                    eng.wait_ge(adj_t_ready, i + 1)
                    for s in range(NT):
                        mm = eng.transpose(p_adj[:, s * P:(s + 1) * P], adj_st[:, k, s * P:(s + 1) * P], ident[:, :])
                    mm.then_inc(adj_turned, 1)

        @block.vector
        def _(eng):
            eng.sem_inc(counts_added, 1)
            eng.sem_inc(sums_added, 1)
            n = 0

            def step(ins):
                nonlocal n
                n += 1
                ins.then_inc(dve, 1)
                eng.wait_ge(dve, n)

            eng.wait_ge(tabs_in, 80)
            eng.wait_ge(tiles_in, 16)
            eng.wait_ge(consts, 3)
            step(eng.tensor_copy(src_f[:, :], slots[:, :, 0]))
            step(eng.tensor_copy(src_i[:, :], slots[:, :, 0]))
            step(eng.tensor_copy(loc[:, :], slots[:, :, 1]))
            step(eng.tensor_copy(w_rest, slots[:, :, 2]))
            for q in range(3):
                step(eng.tensor_copy(w_b[:, :], w_rest))
                step(eng.tensor_copy(w_part[:, q, :], w_b[:, :]))
                step(eng.tensor_tensor(w_rest, w_rest, w_part[:, q, :], ALU.subtract))
            step(eng.tensor_scalar(att_b[:, :], att_b[:, :], 0.2, None, ALU.mult))
            step(eng.tensor_copy(seg_max_r[:, :], seg_max[:, :]))
            step(eng.tensor_tensor(self_prob[:, :], seg_max[:, :], seg_max_r[:, :].bitcast(F32), ALU.subtract))
            eng.sem_inc(ready, 1)
            step(eng.tensor_copy(seg_max[:, :], seg_max_r[:, :].bitcast(F32)))

            def hot_local(g, u):
                for c in range(CH):
                    eng.tensor_scalar(hot_f[:, u, c, :], iota_n[:, 0:P], loc[:, bass.ds(g * CH + c, 1)], None,
                                      ALU.is_equal).then_inc(local_hots, 1)

            def hot_source(g, u, c):
                at = g * CH + c
                eng.wait_ge(ready, 1)
                eng.wait_ge(counted, at + 1)
                eng.tensor_scalar(hot_s[:, u % 2, c, :], iota_n[:, :], src_f[:, bass.ds(at, 1)], None, ALU.is_equal)\
                   .then_inc(hots, 1)

            hot_local(0, 0)
            eng.wait_ge(self_ready, 1)
            for t in range(NT):
                rows = seg_sum[:, t, :].rearrange("p (h w) -> p h w", h=HEADS)
                step(eng.tensor_tensor(rows, rows, self_prob[:, t * HEADS:(t + 1) * HEADS].unsqueeze(2)
                                       .broadcast_to([P, HEADS, HW]), ALU.mult))
            landed = adj[:, 0:2, :].rearrange("p a n -> p (a n)").rearrange("p (t n) -> p t n", t=NT)
            step(eng.tensor_copy(xr_hi[:, :, :], landed))
            step(eng.tensor_tensor(xr_lo[:, :, :], landed, xr_hi[:, :, :].bitcast(F32), ALU.subtract))
            eng.sem_inc(xr_ready, 1)
            hot_local(1, 1)
            step(eng.memset(adj[:, :, :], 0.0))
            for c in range(CH):
                hot_source(0, 0, c)
            at0 = n + 1
            STEPS = 5

            def link(ins, done):
                ins.then_inc(dve, 1)
                eng.wait_ge(ready, 1)
                eng.wait_ge(dve, done)

            def messages(g, r, u):
                eng.wait_ge(gathered[u], 16 * CH * (r + 1))
                for b, bank in enumerate((bank_y, bank_z)):
                    eng.wait_ge(ready, 1)
                    eng.wait_ge(xr_done, 2 * g + b + 1)
                    eng.tensor_tensor(msg[:, 2 * b * HID:(2 * b + 2) * HID].rearrange("p (c d) -> p c d", d=HD),
                                      xlg[:, u, 2 * b:2 * b + 2, :].rearrange("p c (h w) -> p (c h) w", h=HEADS)[:, :, 0:HD],
                                      bank[:, :].rearrange("p (c d) -> p c d", d=HD), ALU.add).then_inc(msg_ready, 1)

            def scores(g, u, done):
                eng.wait_ge(ready, 1)
                eng.wait_ge(act_scaled, g + 1)
                link(eng.tensor_reduce(score[:, u % 2, :], act_m.rearrange("p (c d) -> p c d", d=HD), AX.X, ALU.add), done)
                eng.tensor_copy(score_r[:, u % 2, :], score[:, u % 2, :]).then_inc(score_ready, 1)

            def head_maximum(g, u, h):
                bank = (bank_x, bank_y, bank_z, bank_x)[h]
                here, before = g * HEADS + (h + 1), g * HEADS + h
                if not isinstance(g, int):
                    here, before = eng.to_reg(here), eng.to_reg(before) if h else None
                eng.wait_ge(ready, 1)
                eng.wait_ge(spread, here)
                if h:
                    eng.wait_ge(head_max, before)
                eng.tensor_tensor_reduce(masked[:, :], bank[:, :], bound[:, u % 2, :, :].rearrange("p c e -> p (c e)"),
                                         1.0, -BIG, ALU.add, ALU.max, group_max[:, h:h + 1]).then_inc(head_max, 1)

            def body(g, r, u):
                more = not isinstance(g, int) or g + 1 < NG
                t = eng.value_load(tiles[0:1, bass.ds(g, 1)], min_val=0, max_val=NT - 1)
                at = at0 + STEPS * g
                if more:
                    messages(g + 1, r if u < U - 1 else r + 1, (u + 1) % U)
                head_maximum(g, u, 0)
                if not isinstance(g, int) or g + 2 < NG:
                    hot_local(g + 2, (u + 2) % U)
                head_maximum(g, u, 1)
                head_maximum(g, u, 2)
                if more:
                    hot_source(g + 1, u + 1, 0)
                    hot_source(g + 1, u + 1, 1)
                head_maximum(g, u, 3)
                run_max = seg_max[:, bass.ds(t * HEADS, HEADS)]
                eng.wait_ge(ready, 1)
                eng.wait_ge(head_max, HEADS * g + HEADS)
                link(eng.tensor_tensor(new_max[:, :], run_max, group_max[:, :], ALU.max), at + 1)
                eng.tensor_copy(max_r[:, :], new_max[:, :]).then_inc(max_ready, 1)
                eng.tensor_tensor(shift[:, :], run_max, new_max[:, :], ALU.subtract).then_inc(shift_ready, 1)
                eng.wait_ge(ready, 1)
                eng.wait_ge(shift_ready, g + 1)
                eng.tensor_scalar(run_max, new_max[:, :], 1.0, None, ALU.mult).then_inc(dve, 1)
                if more:
                    scores(g + 1, u + 1, at + 3)
                else:
                    eng.wait_ge(dve, at + 2)
                eng.wait_ge(ready, 1)
                eng.wait_ge(max_back, g + 1)
                late = at + 4 if more else at + 3
                link(eng.tensor_tensor(expo[:, :], score[:, u % 2, :], bank_z[:, 0:CH * HEADS], ALU.subtract), late)
                eng.tensor_scalar(expo[:, :], expo[:, :], 80.0, None, ALU.min).then_inc(expo_ready, 1)
                if more:
                    hot_source(g + 1, u + 1, 2)
                    hot_source(g + 1, u + 1, 3)
                eng.wait_ge(ready, 1)
                eng.wait_ge(prob_ready, g + 1)
                rows = xlg[:, u, :, :].rearrange("p c (h w) -> p (c h) w", h=HEADS)
                eng.tensor_tensor(rows, rows, prob[:, :].unsqueeze(2).broadcast_to([P, CH * HEADS, HW]), ALU.mult)\
                   .then_inc(weighted, 1)
                run_adj = adj[:, bass.ds(t, 1), 0:N_NODES].rearrange("p a n -> p (a n)")
                run_wt = wt[:, bass.ds(t, 1), :].rearrange("p a n -> p (a n)")
                eng.wait_ge(ready, 1)
                eng.wait_ge(counted, CH * g + CH + 2 * CH)
                eng.wait_ge(counts_added, g + 1)
                eng.tensor_tensor(run_adj, run_adj, p_adj[:, 0:N_NODES], ALU.add)
                eng.tensor_tensor(run_wt, run_wt, p_wt[:, :], ALU.add).then_inc(counts_added, 1)
                run_sum = seg_sum[:, bass.ds(t, 1), :].rearrange("p a (h w) -> p (a h) w", h=HEADS)
                eng.wait_ge(ready, 1)
                eng.wait_ge(fade_ready, g + 1)
                eng.wait_ge(sums_added, g + 1)
                link(eng.tensor_tensor(run_sum, run_sum, fade[:, :].unsqueeze(2).broadcast_to([P, HEADS, HW]), ALU.mult),
                     late + 1)
                eng.wait_ge(ready, 1)
                eng.wait_ge(summed, g + 2)
                eng.tensor_tensor(run_sum, run_sum, bank_y[:, 0:XW].rearrange("p (h w) -> p h w", h=HEADS), ALU.add)\
                   .then_inc(sums_added, 1)

            messages(0, 0, 0)
            scores(0, 0, n + 1)
            eng.wait_ge(wt_cleared, 1)
            with eng.Fori(0, NG // U - 1) as j:
                for u in range(U):
                    body(U * j + u, j, u)
            for u in range(U):
                body(NG - U + u, NG // U - 1, u)

            n = at0 + STEPS * NG - 1
            eng.wait_ge(sums_added, NG + 1)
            eng.wait_ge(counts_added, NG + 1)
            sums = seg_sum[:, :, :].rearrange("p t (h w) -> p t h w", h=HEADS)
            step(eng.tensor_scalar(den[:, :, :], sums[:, :, :, HD], 1e-16, None, ALU.add))
            step(eng.reciprocal(den[:, :, :], den[:, :, :]))
            for t in range(NT):
                rows = seg_sum[:, t, :].rearrange("p (h w) -> p h w", h=HEADS)
                step(eng.tensor_tensor(rows, rows, den[:, t, :].unsqueeze(2).broadcast_to([P, HEADS, HW]), ALU.mult))
            eng.sem_inc(o_ready, 1)
            for t in range(NT):
                step(eng.tensor_reduce(deg[:, t:t + 1], adj[:, t, :], AX.X, ALU.add))
            step(eng.tensor_scalar(deg1[:, :], deg[:, :], 1.0, None, ALU.max))
            step(eng.reciprocal(deg_inv[:, :], deg1[:, :]))
            step(eng.tensor_scalar(deg1[:, :], deg[:, :], 1.0, None, ALU.add))
            eng.sem_inc(deg_done, 4)
            eng.wait_ge(root, 1)
            step(eng.reciprocal(deg_rsqrt[:, :], droot[:, :]))
            eng.sem_inc(adj_t_ready, 1)
            eng.sem_inc(adj_out[0], 16)
            eng.sem_inc(adj_out[1], 16)
            with eng.Fori(0, NT // 2) as j:
                for k in range(2):
                    i = 2 * j + k
                    eng.wait_ge(counts_added, NG + 1)
                    eng.wait_ge(adj_turned, i + 3)
                    eng.wait_ge(adj_out[k], 16 * j + 16)
                    eng.tensor_scalar(adj_t[:, k, :], p_adj[:, 0:NPAD], 1.0, None, ALU.mult).then_inc(adj_t_ready, 1)


def dense_phase(nc, sem, tag, sources, resident=None, scale=None, add_first=None, bias=None, relu=False,
                add=None, norm=False, out=None, add_after=None, out_after=None):
    S = len(sources)
    kts = [right.shape[0] // P for _, _, right in sources]
    KTS = sum(kts)
    KM = max(kts)
    rows = [r for r in (add_first, add, add_after) if r is not None]
    R = len(rows)

    with ExitStack() as ctx:
        def sb(name, shape, dt=F32):
            return ctx.enter_context(nc.sbuf_tensor(tag + name, shape, dt))

        right_hi = sb("right_hi", [P, KTS, D], F32R)
        right_lo = sb("right_lo", [P, KTS, D], F32R)
        right_in = sb("right_in", [P, 2, D])
        left_in = sb("left_in", [P, 2, KM * P]) if sources[0][0] != "held" else None
        left_hi = sb("left_hi", [P, 2, KM * P], F32R)
        left_lo = sb("left_lo", [P, 2, KM * P], F32R)
        ident = sb("ident", [P, P])
        y = sb("y", [P, 2, D])
        row_in = sb("row_in", [P, 2, R, D]) if R else None
        y2 = sb("y2", [P, 2, D]) if out_after is not None else None
        bias_b = sb("bias_b", [P, D]) if bias is not None else None
        stats = sb("stats", [P, 2, 6])
        mean_var = sb("mean_var", [P, 2])
        var_eps = sb("var_eps", [P, 1])
        std = sb("std", [P, 1])
        rstd = sb("rstd", [P, 1])
        turn = ctx.enter_context(nc.psum_tensor(tag + "turn", [P, 2, D], F32))
        acc = ctx.enter_context(nc.psum_tensor(tag + "acc", [P, 2, D], F32))

        started = sem(tag + "started")
        filled = sem(tag + "filled")
        ident_ready = sem(tag + "ident_ready")
        bias_in = sem(tag + "bias_in")
        right_landed = [sem(tag + f"right_landed{k}") for k in range(2)]
        right_hi_ready = sem(tag + "right_hi_ready")
        right_lo_ready = sem(tag + "right_lo_ready")
        left_landed = [sem(tag + f"left_landed{k}") for k in range(2)]
        turned = sem(tag + "turned")
        hi_ready = sem(tag + "hi_ready")
        lo_ready = sem(tag + "lo_ready")
        multiplied = sem(tag + "multiplied")
        row_landed = [sem(tag + f"row_landed{k}") for k in range(2)]
        chain = sem(tag + "chain")
        eps_added = sem(tag + "eps_added")
        rooted = sem(tag + "rooted")
        y_ready = sem(tag + "y_ready")
        y2_ready = sem(tag + "y2_ready")
        y_left = [sem(tag + f"y_left{k}") for k in range(2)]
        y2_left = [sem(tag + f"y2_left{k}") for k in range(2)]

        OPS = (add_first is not None) + (bias is not None or scale is not None) + relu + (add is not None)
        LINKS = OPS + 4 if norm else OPS - 1

        block = ctx.enter_context(nc.Block())

        @block.sync
        def _(eng):
            eng.sem_inc(started, 1)
            if bias is not None:
                eng.dma_start(bias_b[:, :], bias.partition_broadcast(P)).then_inc(bias_in, 16)
            n = 0

            def load_left(i, k, s, q):
                kind, left, _ = sources[s]
                kt = kts[s]
                eng.dma_start(left_in[:, q, 0:kt * P], left[bass.ds(i * P, P), :]).then_inc(left_landed[q], 16)

            for s, (_, _, right) in enumerate(sources):
                for t in range(kts[s]):
                    if n >= 2:
                        eng.wait_ge(right_lo_ready, n - 1)
                        eng.wait_ge(right_hi_ready, n - 1)
                    eng.dma_start(right_in[:, n % 2, :], right[t * P:(t + 1) * P, :]).then_inc(right_landed[n % 2], 16)
                    n += 1
            eng.wait_ge(started, 5)

            def store(i, k):
                n = N_NODES - (NT - 1) * P if out.shape[0] != NPAD and i is NT - 1 else P
                eng.dma_start(out[bass.ds(i * P, n), :], y[0:n, k, :]).then_inc(y_left[k], 16)
                if out_after is not None:
                    eng.dma_start(out_after[bass.ds(i * P, P), :], y2[:, k, :]).then_inc(y2_left[k], 16)

            def body(i, k, first=False):
                for s in range(S):
                    if sources[s][0] != "held":
                        q = (k * S + s) % 2
                        eng.wait_ge(started, 5)
                        if sources[s][0] == "rows":
                            eng.wait_ge(turned, S * i + s + 1)
                        else:
                            eng.wait_ge(lo_ready, S * i + s + 1)
                            eng.wait_ge(hi_ready, S * i + s + 1)
                        eng.dma_start(left_in[:, q, 0:kts[s] * P], sources[s][1][bass.ds(i * P, P), :])\
                           .then_inc(left_landed[q], 16)
                eng.wait_ge(started, 5)
                eng.wait_ge(y_ready, i + 1)
                if out_after is not None:
                    eng.wait_ge(y2_ready, i + 1)
                if not first:
                    store(i - 2, k)
                for r in range(R):
                    eng.dma_start(row_in[:, k, r, :], rows[r][bass.ds(i * P, P), :]).then_inc(row_landed[k], 16)

            for k in range(2):
                body(k, k, first=True)
            with eng.Fori(1, NT // 2) as j:
                for k in range(2):
                    body(2 * j + k, k)
            for i in (NT - 2, NT - 1):
                eng.wait_ge(y_ready, i + 3)
                if out_after is not None:
                    eng.wait_ge(y2_ready, i + 3)
                store(i, i % 2)
            for k in range(2):
                eng.wait_ge(y_left[k], 16 * (NT // 2) + 16)
                if out_after is not None:
                    eng.wait_ge(y2_left[k], 16 * (NT // 2) + 16)

        @block.gpsimd
        def _(eng):
            eng.sem_inc(started, 1)
            eng.memset(ident[:, :], 0.0).then_inc(filled, 1)
            eng.wait_ge(filled, 1)
            eng.affine_select(out=ident[:, :], in_=ident[:, :], compare_op=ALU.not_equal, fill=1.0, base=0,
                              pattern=[[-1, P]], channel_multiplier=1).then_inc(ident_ready, 1)

        @block.scalar
        def _(eng):
            eng.sem_inc(started, 1)
            eng.sem_inc(hi_ready, 2)
            for n in range(KTS):
                eng.wait_ge(right_landed[n % 2], 16 * (n // 2) + 16)
                eng.activation(right_hi[:, n, :], right_in[:, n % 2, :], ACT.Copy).then_inc(right_hi_ready, 1)

            def high(i, j, k, s):
                kind, kt, q = sources[s][0], kts[s], (k * S + s) % 2
                eng.wait_ge(started, 5)
                eng.wait_ge(multiplied, S * i + s + 1)
                if kind == "rows":
                    eng.wait_ge(turned, S * i + s + 3)
                    eng.activation(left_hi[:, q, 0:kt * P], turn[:, q, 0:kt * P], ACT.Copy).then_inc(hi_ready, 1)
                elif kind == "turned":
                    eng.wait_ge(left_landed[q], 16 * j + 16)
                    eng.activation(left_hi[:, q, 0:kt * P], left_in[:, q, 0:kt * P], ACT.Copy).then_inc(hi_ready, 1)
                else:
                    eng.activation(left_hi[:, q, :].rearrange("p (t n) -> p t n", t=kt),
                                   resident[:, :, bass.ds(i * P, P)], ACT.Copy).then_inc(hi_ready, 1)

            for s in range(S):
                high(0, 0, 0, s)
            with eng.Fori(0, NT // 2 - 1) as j:
                for k in range(2):
                    i = 2 * j + k
                    for s in range(S):
                        high(i + 1, (j, j + 1)[k], 1 - k, s)
                    if norm:
                        eng.wait_ge(started, 5)
                        eng.wait_ge(eps_added, i + 1)
                        eng.activation(std[:, :], var_eps[:, :], ACT.Sqrt).then_inc(rooted, 1)
            for i in (NT - 2, NT - 1):
                if i < NT - 1:
                    for s in range(S):
                        high(NT - 1, NT // 2 - 1, 1, s)
                if norm:
                    eng.wait_ge(eps_added, i + 1)
                    eng.activation(std[:, :], var_eps[:, :], ACT.Sqrt).then_inc(rooted, 1)

        @block.tensor
        def _(eng):
            eng.sem_inc(started, 1)
            eng.sem_inc(turned, 2)
            eng.sem_inc(multiplied, 2)
            eng.wait_ge(ident_ready, 1)

            def transposes(i, j, k, s):
                if sources[s][0] != "rows":
                    return
                q = (k * S + s) % 2
                eng.wait_ge(started, 5)
                eng.wait_ge(left_landed[q], 16 * (j + 1) if S == 1 else 16 * (i + 1))
                eng.wait_ge(hi_ready, S * i + s + 1)
                eng.wait_ge(lo_ready, S * i + s + 1)
                for t in range(kts[s]):
                    mm = eng.transpose(turn[:, q, t * P:(t + 1) * P], left_in[:, q, t * P:(t + 1) * P], ident[:, :])
                mm.then_inc(turned, 1)

            def products(i, k, s):
                q = (k * S + s) % 2
                first = sum(kts[:s])
                eng.wait_ge(started, 5)
                eng.wait_ge(hi_ready, S * i + s + 3)
                eng.wait_ge(lo_ready, S * i + s + 3)
                if s == 0:
                    eng.wait_ge(y_ready, i + 1)
                for n0 in (0, 512):
                    for t in range(kts[s]):
                        for a, b in ((left_hi, right_hi), (left_hi, right_lo), (left_lo, right_hi)):
                            mm = eng.matmul(acc[:, k, n0:n0 + 512], a[:, q, t * P:(t + 1) * P],
                                            b[:, first + t, n0:n0 + 512],
                                            start=(s == 0 and t == 0 and a is left_hi and b is right_hi),
                                            stop=(s == S - 1 and t == kts[s] - 1 and a is left_lo),
                                            skip_group_check=True)
                mm.then_inc(multiplied, 1)

            for s in range(S):
                transposes(0, 0, 0, s)
            eng.wait_ge(right_hi_ready, KTS)
            eng.wait_ge(right_lo_ready, KTS)
            with eng.Fori(0, NT // 2 - 1) as j:
                for k in range(2):
                    i = 2 * j + k
                    if S == 1:
                        transposes(i + 1, (j, j + 1)[k], 1 - k, 0)
                        products(i, k, 0)
                    else:
                        for s in range(S):
                            products(i, k, s)
                            transposes(i + 1, (j, j + 1)[k], 1 - k, s)
            if S == 1:
                transposes(NT - 1, NT // 2 - 1, 1, 0)
                products(NT - 2, 0, 0)
                products(NT - 1, 1, 0)
            else:
                for s in range(S):
                    products(NT - 2, 0, s)
                    transposes(NT - 1, NT // 2 - 1, 1, s)
                for s in range(S):
                    products(NT - 1, 1, s)

        @block.vector
        def _(eng):
            eng.sem_inc(started, 1)
            eng.sem_inc(lo_ready, 2)
            eng.sem_inc(y_ready, 2)
            eng.sem_inc(y_left[0], 16)
            eng.sem_inc(y_left[1], 16)
            if out_after is not None:
                eng.sem_inc(y2_ready, 2)
                eng.sem_inc(y2_left[0], 16)
                eng.sem_inc(y2_left[1], 16)
            for n in range(KTS):
                eng.wait_ge(right_hi_ready, n + 1)
                eng.tensor_tensor(right_lo[:, n, :], right_in[:, n % 2, :], right_hi[:, n, :].bitcast(F32), ALU.subtract)\
                   .then_inc(right_lo_ready, 1)

            def low(i, k, s):
                kind, kt, q = sources[s][0], kts[s], (k * S + s) % 2
                whole = {"rows": turn, "turned": left_in}.get(kind)
                eng.wait_ge(started, 5)
                eng.wait_ge(hi_ready, S * i + s + 3)
                if whole is not None:
                    eng.tensor_tensor(left_lo[:, q, 0:kt * P], whole[:, q, 0:kt * P],
                                      left_hi[:, q, 0:kt * P].bitcast(F32), ALU.subtract).then_inc(lo_ready, 1)
                else:
                    eng.tensor_tensor(left_lo[:, q, :].rearrange("p (t n) -> p t n", t=kt),
                                      resident[:, :, bass.ds(i * P, P)],
                                      left_hi[:, q, :].rearrange("p (t n) -> p t n", t=kt).bitcast(F32),
                                      ALU.subtract).then_inc(lo_ready, 1)

            def epilogue(i, j, k):
                m = 0
                yk = y[:, k, :]
                cur = acc[:, k, :]
                r = 0

                def link(ins):
                    nonlocal m
                    m += 1
                    if m > LINKS:
                        ins.then_inc(y_ready, 1)
                        return
                    ins.then_inc(chain, 1)
                    due = eng.to_reg(i * LINKS + m) if not isinstance(i, int) else i * LINKS + m
                    eng.wait_ge(started, 5)
                    eng.wait_ge(chain, due)

                eng.wait_ge(started, 5)
                eng.wait_ge(multiplied, S * i + S + 2)
                eng.wait_ge(y_left[k], 16 * j + 16)
                if R:
                    eng.wait_ge(row_landed[k], 16 * R * (j + 1))
                if bias is not None:
                    eng.wait_ge(bias_in, 16)
                if add_first is not None:
                    link(eng.tensor_tensor(yk, cur, row_in[:, k, r, :], ALU.add))
                    cur, r = yk, r + 1
                if scale is not None and bias is not None:
                    link(eng.scalar_tensor_tensor(out=yk, in0=cur, scalar=scale[:, bass.ds(i, 1)], in1=bias_b[:, :],
                                                  op0=ALU.mult, op1=ALU.add))
                    cur = yk
                elif scale is not None:
                    link(eng.tensor_scalar(yk, cur, scale[:, bass.ds(i, 1)], None, ALU.mult))
                    cur = yk
                elif bias is not None:
                    link(eng.tensor_tensor(yk, cur, bias_b[:, :], ALU.add))
                    cur = yk
                if relu:
                    link(eng.tensor_scalar(yk, cur, 0.0, None, ALU.max))
                if add is not None:
                    link(eng.tensor_tensor(yk, cur, row_in[:, k, r, :], ALU.add))
                    cur, r = yk, r + 1
                if norm:
                    eng.bn_stats(stats[:, 0, :], yk[:, 0:512]).then_inc(chain, 1)
                    link(eng.bn_stats(stats[:, 1, :], yk[:, 512:1024]))
                    m += 1
                    due = eng.to_reg(i * LINKS + m) if not isinstance(i, int) else i * LINKS + m
                    eng.wait_ge(started, 5)
                    eng.wait_ge(chain, due)
                    link(eng.bn_aggr(mean_var[:, :], stats[:, :, :].rearrange("p a b -> p (a b)")))
                    eng.tensor_scalar(var_eps[:, :], mean_var[:, 1:2], LN_EPS, None, ALU.add).then_inc(eps_added, 1)
                    eng.wait_ge(started, 5)
                    eng.wait_ge(rooted, i + 1)
                    link(eng.reciprocal(rstd[:, :], std[:, :]))
                    eng.tensor_scalar(yk, yk, mean_var[:, 0:1], rstd[:, 0:1], ALU.subtract, ALU.mult).then_inc(y_ready, 1)
                assert m == OPS + 4 * norm
                if out_after is not None:
                    eng.wait_ge(started, 5)
                    eng.wait_ge(y_ready, i + 3)
                    eng.wait_ge(y2_left[k], 16 * j + 16)
                    eng.tensor_tensor(y2[:, k, :], yk, row_in[:, k, r, :], ALU.add).then_inc(y2_ready, 1)

            for s in range(S):
                low(0, 0, s)
            with eng.Fori(0, NT // 2 - 1) as j:
                for k in range(2):
                    i = 2 * j + k
                    for s in range(S):
                        low(i + 1, 1 - k, s)
                    epilogue(i, j, k)
            for s in range(S):
                low(NT - 1, 1, s)
            epilogue(NT - 2, NT // 2 - 1, 0)
            epilogue(NT - 1, NT // 2 - 1, 1)


def batch_norm_phase(nc, sem, g_tab, gamma, beta, held):
    with ExitStack() as ctx:
        def sb(name, shape):
            return ctx.enter_context(nc.sbuf_tensor("bn_" + name, shape, F32))

        g_in = sb("g_in", [P, NT, D])
        ident = sb("ident", [P, P])
        gam = sb("gam", [P, KT])
        bet = sb("bet", [P, KT])
        PIECE = -(-N_NODES // 3)
        stats = sb("stats", [P, KT, 3, 6])
        mean_var = sb("mean_var", [P, KT, 2])
        var_eps = sb("var_eps", [P, KT])
        std = sb("std", [P, KT])
        factor = sb("factor", [P, KT])
        offset = sb("offset", [P, KT])
        turn = ctx.enter_context(nc.psum_tensor("bn_turn", [P, 2, 3 * 512], F32))

        loaded = [sem(f"bn_loaded{i}") for i in range(NT)]
        consts_in = sem("bn_consts_in")
        filled = sem("bn_filled")
        ident_ready = sem("bn_ident_ready")
        turned = sem("bn_turned")
        copied = sem("bn_copied")
        stated = sem("bn_stated")
        var_ready = sem("bn_var_ready")
        rooted = sem("bn_rooted")
        chain = sem("bn_chain")
        affine_ready = sem("bn_affine_ready")
        normed = sem("bn_normed")

        block = ctx.enter_context(nc.Block())

        @block.sync
        def _(eng):
            for i in range(NT):
                eng.dma_start(g_in[:, i, :], g_tab[i * P:(i + 1) * P, :]).then_inc(loaded[i], 16)
            eng.dma_start(gam[:, :], gamma.rearrange("(k p) -> p k", p=P),
                          allow_slow_non_contiguous=True).then_inc(consts_in, 16)
            eng.dma_start(bet[:, :], beta.rearrange("(k p) -> p k", p=P),
                          allow_slow_non_contiguous=True).then_inc(consts_in, 16)

        @block.gpsimd
        def _(eng):
            eng.memset(ident[:, :], 0.0).then_inc(filled, 1)
            eng.wait_ge(filled, 1)
            eng.affine_select(out=ident[:, :], in_=ident[:, :], compare_op=ALU.not_equal, fill=1.0, base=0,
                              pattern=[[-1, P]], channel_multiplier=1).then_inc(ident_ready, 1)

        @block.tensor
        def _(eng):
            eng.wait_ge(ident_ready, 1)
            for i in range(NT):
                eng.wait_ge(loaded[i], 16)
            for t in range(KT):
                if t >= 2:
                    eng.wait_ge(copied, t - 1)
                for i in range(NT):
                    mm = eng.transpose(turn[:, t % 2, i * P:(i + 1) * P], g_in[:, i, t * P:(t + 1) * P], ident[:, :])
                mm.then_inc(turned, 1)

        @block.scalar
        def _(eng):
            for t in range(KT):
                eng.wait_ge(turned, t + 1)
                eng.activation(held[:, t, :], turn[:, t % 2, 0:NPAD], ACT.Copy).then_inc(copied, 1)
            eng.wait_ge(var_ready, 1)
            eng.activation(std[:, :], var_eps[:, :], ACT.Sqrt).then_inc(rooted, 1)
            eng.wait_ge(affine_ready, 1)
            for t in range(KT):
                eng.activation(held[:, t, :], held[:, t, :], ACT.Relu, scale=factor[:, t:t + 1],
                               bias=offset[:, t:t + 1]).then_inc(normed, 1)
            eng.wait_ge(normed, KT)

        @block.vector
        def _(eng):
            for t in range(KT):
                eng.wait_ge(copied, t + 1)
                for q in range(3):
                    eng.bn_stats(stats[:, t, q, :], held[:, t, q * PIECE:min((q + 1) * PIECE, N_NODES)])\
                       .then_inc(stated, 1)
                eng.wait_ge(stated, 3 * t + 3)
                eng.bn_aggr(mean_var[:, t, :], stats[:, t, :, :].rearrange("p q s -> p (q s)")).then_inc(chain, 1)
            eng.wait_ge(chain, KT)
            eng.tensor_scalar(var_eps[:, :], mean_var[:, :, 1], LN_EPS, None, ALU.add).then_inc(var_ready, 1)
            eng.wait_ge(rooted, 1)
            eng.reciprocal(factor[:, :], std[:, :]).then_inc(chain, 1)
            eng.wait_ge(consts_in, 32)
            eng.wait_ge(chain, KT + 1)
            eng.tensor_tensor(factor[:, :], factor[:, :], gam[:, :], ALU.mult).then_inc(chain, 1)
            eng.wait_ge(chain, KT + 2)
            eng.tensor_tensor(offset[:, :], mean_var[:, :, 0], factor[:, :], ALU.mult).then_inc(chain, 1)
            eng.wait_ge(chain, KT + 3)
            eng.tensor_tensor(offset[:, :], bet[:, :], offset[:, :], ALU.subtract).then_inc(affine_ready, 1)


def build(nc, stop, x, src, dst, edge_weight, positions, rms_w, w_down, wl, wr, att, w_up,
          w_self0, w_neigh0, b0, w_self1, w_neigh1, b1, sparse_bias, w1, c1, gamma, beta, w2, c2, out):
    taken = []

    def sem(name):
        taken.append(nc.alloc_semaphore(name=name))
        return taken[-1]

    def phase(f, *args, **kwargs):
        f(nc, sem, *args, **kwargs)
        nc.clear_and_free_semaphores(taken)
        nc.all_engine_barrier()
        taken.clear()

    with ExitStack() as ctx:
        def scratch(name, shape, dt=F32):
            return nc.dram_tensor(name, shape, dt, kind="Internal").ap()

        edge_tab = scratch("edge_tab", [NC * P, 4])
        xl_tab = scratch("xl_tab", [NPAD, XW])
        xr_tab = scratch("xr_tab", [NPAD, HID])
        self_tab = scratch("self_tab", [P, NT, HEADS])
        tile_tab = scratch("tile_tab", [1, NG], I32)
        adj_tab = scratch("adj_tab", [NPAD, NPAD])
        wt_tab = scratch("wt_tab", [D, D])
        o_tab = scratch("o_tab", [NPAD, HID])
        rows = {n: scratch(n, [NPAD, D]) for n in ("x1", "mean1", "h1", "mean2", "x2", "x3", "x3p", "s1", "g1", "s2")}
        deg_inv = ctx.enter_context(nc.sbuf_tensor("deg_inv", [P, NT], F32))
        deg_rsqrt = ctx.enter_context(nc.sbuf_tensor("deg_rsqrt", [P, NT], F32))

        phase(prepare_phase, x, src, dst, edge_weight, rms_w, w_down, wl, wr, att,
                      edge_tab, xl_tab, self_tab, xr_tab, tile_tab)
        phase(edge_phase, edge_tab, xl_tab, self_tab, xr_tab, tile_tab, att, adj_tab, wt_tab, o_tab,
                   deg_inv, deg_rsqrt)

        phase(dense_phase, "up_", [("rows", o_tab, w_up)], add=x, norm=True, out=out if stop == 1 else rows["x1"])
        if stop == 1:
            return
        phase(dense_phase, "m1_", [("turned", adj_tab, rows["x1"])], scale=deg_inv, out=rows["mean1"])
        phase(dense_phase, "h1_", [("rows", rows["x1"], w_self0), ("rows", rows["mean1"], w_neigh0)],
                    bias=b0, relu=True, out=rows["h1"])
        phase(dense_phase, "m2_", [("turned", adj_tab, rows["h1"])], scale=deg_inv, out=rows["mean2"])
        phase(dense_phase, "x2_", [("rows", rows["h1"], w_self1), ("rows", rows["mean2"], w_neigh1)],
                    bias=b1, add=rows["x1"], norm=True, out=out if stop == 2 else rows["x2"])
        if stop == 2:
            return
        phase(dense_phase, "x3_", [("rows", rows["x2"], wt_tab)], bias=sparse_bias, add=rows["x2"], norm=True,
                    out=out if stop == 3 else rows["x3"], add_after=positions, out_after=rows["x3p"])
        if stop == 3:
            return
        phase(dense_phase, "s1_", [("rows", rows["x3p"], w1)], scale=deg_rsqrt, out=rows["s1"])
        phase(dense_phase, "g1_", [("turned", adj_tab, rows["s1"])], add_first=rows["s1"], scale=deg_rsqrt,
                    bias=c1, out=rows["g1"])
        with nc.sbuf_tensor("held", [P, KT, NPAD], F32) as held:
            phase(batch_norm_phase, rows["g1"], gamma, beta, held)
            phase(dense_phase, "s2_", [("held", None, w2)], resident=held, scale=deg_rsqrt, out=rows["s2"])
        phase(dense_phase, "g2_", [("turned", adj_tab, rows["s2"])], add_first=rows["s2"], scale=deg_rsqrt,
                    bias=c2, relu=True, add=rows["x3"], norm=True, out=out)


_INS = ["x", "src", "dst", "edge_weight", "positions", "L0_gnn_rms_w", "L0_gnn_W_down", "L0_gnn_Wl", "L0_gnn_Wr",
        "L0_gnn_att", "L0_gnn_W_up", "L1_gnn_W_self0", "L1_gnn_W_neigh0", "L1_gnn_b0", "L1_gnn_W_self1",
        "L1_gnn_W_neigh1", "L1_gnn_b1", "L2_gnn_bias", "L3_gnn_W1", "L3_gnn_b1", "L3_gnn_gamma", "L3_gnn_beta",
        "L3_gnn_W2", "L3_gnn_b2"]
STOP = 4


def kernel(**inputs):
    import numpy as _np
    import concourse.bacc as _bacc
    from concourse import mybir as _mybir
    from concourse.bass_utils import run_bass_kernel_spmd as _run

    pos = _np.arange(N_NODES, dtype=_np.float32)[:, None]
    div = _np.exp(_np.arange(0, D, 2, dtype=_np.float32) * _np.float32(-_np.log(10000.0) / D))
    ang = (pos * div).astype(_np.float32)
    positions = _np.zeros((NPAD, D), _np.float32)
    positions[:N_NODES] = _np.stack([_np.sin(ang), _np.cos(ang)], axis=-1).reshape(N_NODES, D)

    nc = _bacc.Bacc("TRN2", target_bir_lowering=False, num_devices=1)
    arrays, args = {}, []
    for name in _INS:
        if name == "positions":
            a = positions
        else:
            a = _np.ascontiguousarray(inputs[name])
        if name == "x":
            a = _np.pad(a, ((0, NPAD - N_NODES), (0, 0)))
        arrays[f"in_{name}_dram"] = a
        args.append(nc.dram_tensor(f"in_{name}_dram", a.shape, _mybir.dt.from_np(a.dtype), kind="ExternalInput").ap())
    args.append(nc.dram_tensor("out_0_dram", (N_NODES, D), _mybir.dt.float32, kind="ExternalOutput").ap())
    build(nc, STOP, *args)
    r = _run(nc, [arrays], core_ids=[0])
    return r.results[0]["out_0_dram"]
```

```python
from contextlib import ExitStack

import concourse.bass as bass
from concourse import mybir

F32 = mybir.dt.float32
F32R = mybir.dt.float32r
BF16 = mybir.dt.bfloat16
F16 = mybir.dt.float16
I32 = mybir.dt.int32
ALU = mybir.AluOpType
ACT = mybir.ActivationFunctionType
AX = mybir.AxisListType

P = 128
N_NODES = 1250
N_EDGES = 40000
D = 1024
HID = 256
HEADS = 4
HD = HID // HEADS
HW = HD + 1
XW = HEADS * HW
NT = -(-N_NODES // P)
NPAD = NT * P
KT = D // P

EP = 125
EC = N_EDGES // EP
CH = 4
GE = CH * P
NG = (N_EDGES + NT * (GE - 1)) // GE
U = 4
NG += -NG % U
NC = NG * CH
NO_DST = 200.0

COUNT_EXACT = 2048.0
LN_EPS = 1e-5
BIG = 1e38


def prepare_phase(nc, sem, x, src, dst, edge_weight, rms_w, w_down, wl, wr, att,
                  edge_tab, xl_tab, self_tab, xr_tab, tile_tab):
    with ExitStack() as ctx:
        def sb(name, shape, dt):
            return ctx.enter_context(nc.sbuf_tensor("pr_" + name, shape, dt))

        def ps(name, shape):
            return ctx.enter_context(nc.psum_tensor("pr_" + name, shape, F32))

        src_i = sb("src_i", [EP, EC], I32)
        dst_i = sb("dst_i", [EP, EC], I32)
        wgt = sb("wgt", [EP, EC], F32)
        bucket_i = sb("bucket_i", [EP, EC], I32)
        local_i = sb("local_i", [EP, EC], I32)
        bucket = sb("bucket", [EP, EC], F32)
        mask = sb("mask", [EP, NT, EC], F32)
        rank = sb("rank", [EP, NT, EC], F32)
        zeros = sb("zeros", [EP, EC], F32)
        total = sb("total", [EP, NT], F32)
        before = sb("before", [EP, P], F32)
        ones = sb("ones", [P, P], F32)
        count_f = sb("count_f", [P, NT], F32)
        count_i = sb("count_i", [P, NT], I32)
        groups = sb("groups", [P, NT], F32)
        zeros10 = sb("zeros10", [P, NT], F32)
        group_end = sb("group_end", [P, NT], F32)
        base = sb("base", [EP, NT], F32)
        slot = sb("slot", [EP, EC], F32)
        part = sb("part", [EP, EC], F32)
        slot_i = sb("slot_i", [EP, EC], I32)
        record = sb("record", [EP, EC, 4], F32)
        unused = sb("unused", [P, NC, 4], F32)
        iota_g = sb("iota_g", [1, NG], F32)
        tile_f = sb("tile_f", [1, NG], F32)
        tile_i = sb("tile_i", [1, NG], I32)
        SC = 8
        slot_st = sb("slot_st", [EP, 2, SC], I32)
        rec_st = sb("rec_st", [EP, 2, SC * 4], F32)
        ident = sb("ident", [P, P], F32)
        xin = sb("xin", [P, 2, D], F32)
        sq = sb("sq", [P, D], F32)
        ssq = sb("ssq", [P, 2], F32)
        ms = sb("ms", [P, 1], F32)
        rms = sb("rms", [P, 1], F32)
        rinv = sb("rinv", [P, 1], F32)
        xT = sb("xT", [P, D], F32)
        wd = sb("wd", [P, KT, HID], F32)
        rw = sb("rw", [P, KT], F32)
        wlr = sb("wlr", [P, 2, 2 * HID], F32)
        xd = sb("xd", [P, HID], F32)
        xdT = sb("xdT", [P, HID], F32)
        xl = sb("xl", [P, 2, XW], F32)
        xr = sb("xr", [P, 2, HID], F32)
        att_b = sb("att_b", [P, HID], F32)
        msg = sb("msg", [P, HID], F32)
        act_s = sb("act_s", [P, HID], F32)
        prod = sb("prod", [P, HID], F32)
        e_self = sb("e_self", [P, NT, HEADS], F32)

        tp = ps("tp", [P, D])
        pd = ps("pd", [P, HID])
        pt = ps("pt", [P, HID])
        plr = ps("plr", [P, 2 * HID])
        pe = ps("pe", [P, 2 * 16])

        started = sem("pr_started")
        edges_in = sem("pr_edges_in")
        consts_in = sem("pr_consts_in")
        filled = sem("pr_filled")
        idents = sem("pr_idents")
        dve = sem("pr_dve")
        totals = sem("pr_totals")
        prefixes = sem("pr_prefixes")
        slots_ready = sem("pr_slots_ready")
        unused_ready = sem("pr_unused_ready")
        unused_out = sem("pr_unused_out")
        tiles_ready = sem("pr_tiles_ready")
        staged = sem("pr_staged")
        scattered = [sem(f"pr_scattered{k}") for k in range(2)]
        x_in = [sem(f"pr_x_in{k}") for k in range(2)]
        x_used = sem("pr_x_used")
        squared = sem("pr_squared")
        x_turned = sem("pr_x_turned")
        xT_ready = sem("pr_xT_ready")
        wd_ready = sem("pr_wd_ready")
        down = sem("pr_down")
        ms_ready = sem("pr_ms_ready")
        rms_ready = sem("pr_rms_ready")
        xd_ready = sem("pr_xd_ready")
        xd_turned = sem("pr_xd_turned")
        xdT_ready = sem("pr_xdT_ready")
        lr = sem("pr_lr")
        xr_ready = sem("pr_xr_ready")
        self_msg = sem("pr_self_msg")
        self_act = sem("pr_self_act")
        self_ready = sem("pr_self_ready")
        xl_ones = sem("pr_xl_ones")
        tabs_out = [sem(f"pr_tabs_out{k}") for k in range(2)]
        last_out = sem("pr_last_out")

        block = ctx.enter_context(nc.Block())

        @block.sync
        def _(eng):
            eng.dma_start(dst_i[:, :], dst.rearrange("(p c) -> p c", p=EP)).then_inc(edges_in, 16)
            eng.dma_start(src_i[:, :], src.rearrange("(p c) -> p c", p=EP)).then_inc(edges_in, 16)
            eng.dma_start(wgt[:, :], edge_weight.rearrange("(p c) -> p c", p=EP)).then_inc(edges_in, 16)
            eng.dma_start(wd[:, :, :], w_down.rearrange("(k p) n -> p k n", p=P)).then_inc(consts_in, 16)
            eng.dma_start(rw[:, :], rms_w.rearrange("(k p) -> p k", p=P),
                          allow_slow_non_contiguous=True).then_inc(consts_in, 16)
            eng.dma_start(wlr[:, :, 0:HID], wl.rearrange("(k p) n -> p k n", p=P)).then_inc(consts_in, 16)
            eng.dma_start(wlr[:, :, HID:2 * HID], wr.rearrange("(k p) n -> p k n", p=P)).then_inc(consts_in, 16)
            eng.dma_start(att_b[:, :], att.rearrange("h d -> (h d)").partition_broadcast(P)).then_inc(consts_in, 16)
            eng.wait_ge(unused_ready, 1)
            eng.dma_start(edge_tab.rearrange("(p c) w -> p c w", p=P), unused[:, :, :]).then_inc(unused_out, 16)
            eng.wait_ge(started, 3)
            with eng.Fori(0, NT // 2) as j:
                for k in range(2):
                    i = 2 * j + k
                    eng.wait_ge(started, 3)
                    eng.wait_ge(x_used, i + 1)
                    eng.dma_start(xin[:, k, :], x[bass.ds(i * P, P), :]).then_inc(x_in[k], 16)
            eng.wait_ge(tiles_ready, 1)
            eng.dma_start(tile_tab, tile_i[:, :]).then_inc(last_out, 16)
            eng.wait_ge(self_ready, NT)
            eng.dma_start(self_tab, e_self[:, :, :]).then_inc(last_out, 16)
            eng.wait_ge(last_out, 32)

        @block.gpsimd
        def _(eng):
            eng.sem_inc(x_used, 2)
            eng.sem_inc(started, 1)
            eng.memset(unused[:, :, :], 0.0).then_inc(filled, 1)
            eng.memset(ident[:, :], 0.0).then_inc(filled, 1)
            eng.memset(before[:, :], 1.0).then_inc(filled, 1)
            eng.memset(ones[:, :], 1.0).then_inc(filled, 1)
            eng.wait_ge(filled, 4)
            eng.memset(unused[:, :, 1], NO_DST).then_inc(unused_ready, 1)
            eng.affine_select(out=ident[:, :], in_=ident[:, :], compare_op=ALU.not_equal, fill=1.0, base=0,
                              pattern=[[-1, P]], channel_multiplier=1).then_inc(idents, 1)
            eng.affine_select(out=before[:, :], in_=before[:, :], compare_op=ALU.is_gt, fill=0.0, base=0,
                              pattern=[[1, P]], channel_multiplier=-1).then_inc(idents, 1)
            eng.iota(iota_g[:, :], [[1, NG]], base=0, channel_multiplier=0,
                     allow_small_or_imprecise_dtypes=True).then_inc(idents, 1)
            eng.memset(xl[:, :, :], 1.0).then_inc(xl_ones, 1)
            eng.wait_ge(slots_ready, 1)
            eng.wait_ge(unused_out, 16)
            for k in range(2):
                eng.tensor_copy(slot_st[:, k, :], slot_i[:, k * SC:(k + 1) * SC]).then_inc(staged, 1)
                eng.tensor_copy(rec_st[:, k, :], record[:, k * SC:(k + 1) * SC, :].rearrange("p c w -> p (c w)"))\
                   .then_inc(staged, 1)
                eng.wait_ge(staged, 2 * k + 2)
                for s in range(SC):
                    eng.indirect_dma_start(edge_tab, bass.IndirectOffsetOnAxis(ap=slot_st[:, k, s:s + 1], axis=0),
                                           rec_st[:, k, s * 4:s * 4 + 4], None).then_inc(scattered[k], 16)
            with eng.Fori(1, EC // (2 * SC)) as j:
                for k in range(2):
                    i = 2 * j + k
                    eng.wait_ge(unused_out, 16)
                    eng.wait_ge(scattered[k], 16 * SC * j)
                    eng.tensor_copy(slot_st[:, k, :], slot_i[:, bass.ds(i * SC, SC)]).then_inc(staged, 1)
                    eng.tensor_copy(rec_st[:, k, :], record[:, bass.ds(i * SC, SC), :].rearrange("p c w -> p (c w)"))\
                       .then_inc(staged, 1)
                    due = eng.to_reg(i * 2 + 2)
                    eng.wait_ge(unused_out, 16)
                    eng.wait_ge(staged, due)
                    for s in range(SC):
                        eng.indirect_dma_start(edge_tab, bass.IndirectOffsetOnAxis(ap=slot_st[:, k, s:s + 1], axis=0),
                                               rec_st[:, k, s * 4:s * 4 + 4], None).then_inc(scattered[k], 16)
            for k in range(2):
                eng.wait_ge(scattered[k], 16 * EC // 2)

        @block.scalar
        def _(eng):
            eng.sem_inc(started, 1)
            eng.sem_inc(rms_ready, 1)
            eng.wait_ge(started, 3)
            with eng.Fori(0, NT // 2) as j:
                for k in range(2):
                    i = 2 * j + k
                    eng.wait_ge(started, 3)
                    eng.wait_ge(x_in[k], 16 * j + 16)
                    eng.wait_ge(ms_ready, i + 1)
                    eng.activation(sq[:, :], xin[:, k, :], ACT.Square, accum_out=ssq[:, 0:1]).then_inc(squared, 1)
                    eng.wait_ge(started, 3)
                    eng.wait_ge(x_turned, i + 1)
                    eng.activation(xT[:, :], tp[:, :], ACT.Copy).then_inc(xT_ready, 1)
                    eng.wait_ge(started, 3)
                    eng.wait_ge(ms_ready, i + 2)
                    eng.activation(rms[:, :], ms[:, :], ACT.Sqrt).then_inc(rms_ready, 1)
                    eng.wait_ge(started, 3)
                    eng.wait_ge(xr_ready, i + 1)
                    eng.dma_start(xl_tab[bass.ds(i * P, P), :], xl[:, k, :]).then_inc(tabs_out[k], 16)
                    eng.dma_start(xr_tab[bass.ds(i * P, P), :], xr[:, k, :]).then_inc(tabs_out[k], 16)
            for k in range(2):
                eng.wait_ge(tabs_out[k], 32 * (NT // 2) + 32)

        @block.tensor
        def _(eng):
            eng.sem_inc(started, 1)
            eng.wait_ge(idents, 3)
            eng.wait_ge(totals, 1)
            eng.matmul(pe[:, 0:NT], before[:, :], total[:, :], start=True, stop=True).then_inc(prefixes, 1)
            eng.matmul(pe[:, 16:16 + NT], ones[0:EP, :], total[:, :], start=True, stop=True).then_inc(prefixes, 1)
            eng.wait_ge(wd_ready, KT)
            with eng.Fori(0, NT // 2) as j:
                for k in range(2):
                    i = 2 * j + k
                    eng.wait_ge(started, 3)
                    eng.wait_ge(squared, i + 1)
                    for t in range(KT):
                        mm = eng.transpose(tp[:, t * P:(t + 1) * P], xin[:, k, t * P:(t + 1) * P], ident[:, :])
                    mm.then_inc(x_turned, 1)
                    eng.wait_ge(started, 3)
                    eng.wait_ge(xT_ready, i + 1)
                    for t in range(KT):
                        mm = eng.matmul(pd[:, :], xT[:, t * P:(t + 1) * P], wd[:, t, :],
                                        start=(t == 0), stop=(t == KT - 1))
                        if t == 0:
                            mm.then_inc(x_used, 1)
                    mm.then_inc(down, 1)
                    eng.wait_ge(started, 3)
                    eng.wait_ge(xd_ready, i + 1)
                    for t in range(2):
                        mm = eng.transpose(pt[:, t * P:(t + 1) * P], xd[:, t * P:(t + 1) * P], ident[:, :])
                    mm.then_inc(xd_turned, 1)
                    eng.wait_ge(started, 3)
                    eng.wait_ge(xdT_ready, i + 1)
                    for t in range(2):
                        mm = eng.matmul(plr[:, :], xdT[:, t * P:(t + 1) * P], wlr[:, t, :],
                                        start=(t == 0), stop=(t == 1))
                    mm.then_inc(lr, 1)

        @block.vector
        def _(eng):
            eng.sem_inc(ms_ready, 1)
            eng.sem_inc(tabs_out[0], 32)
            eng.sem_inc(tabs_out[1], 32)
            n = 0

            def step(ins):
                nonlocal n
                n += 1
                ins.then_inc(dve, 1)
                eng.wait_ge(dve, n)

            eng.wait_ge(edges_in, 48)
            step(eng.tensor_scalar(bucket_i[:, :], dst_i[:, :], 7, None, ALU.logical_shift_right))
            step(eng.tensor_scalar(local_i[:, :], dst_i[:, :], P - 1, None, ALU.bitwise_and))
            step(eng.tensor_copy(bucket[:, :], bucket_i[:, :]))
            step(eng.tensor_copy(record[:, :, 0], src_i[:, :]))
            step(eng.tensor_copy(record[:, :, 1], local_i[:, :]))
            step(eng.tensor_copy(record[:, :, 2], wgt[:, :]))
            step(eng.memset(record[:, :, 3], 0.0))
            step(eng.memset(zeros[:, :], 0.0))
            step(eng.memset(zeros10[:, :], 0.0))
            for b in range(NT):
                step(eng.tensor_scalar(mask[:, b, :], bucket[:, :], float(b), None, ALU.is_equal))
                step(eng.tensor_tensor_scan(rank[:, b, :], mask[:, b, :], zeros[:, :], 0.0, ALU.add, ALU.add))
            eng.tensor_copy(total[:, :], rank[:, :, EC - 1]).then_inc(totals, 1)
            eng.wait_ge(prefixes, 2)
            step(eng.tensor_scalar(count_f[:, :], pe[:, 16:16 + NT], float(GE - 1), None, ALU.add))
            step(eng.tensor_copy(count_i[:, :], count_f[:, :]))
            step(eng.tensor_scalar(count_i[:, :], count_i[:, :], GE.bit_length() - 1, None, ALU.logical_shift_right))
            step(eng.tensor_copy(groups[:, :], count_i[:, :]))
            step(eng.tensor_tensor_scan(group_end[:, :], groups[:, :], zeros10[:, :], 0.0, ALU.add, ALU.add))
            step(eng.tensor_tensor(groups[:, :], group_end[:, :], groups[:, :], ALU.subtract))
            step(eng.tensor_scalar(base[:, :], groups[0:EP, :], float(GE), -1.0, ALU.mult, ALU.add))
            step(eng.tensor_tensor(base[:, :], base[:, :], pe[0:EP, 0:NT], ALU.add))
            for b in range(NT):
                o = slot if b == 0 else part
                step(eng.scalar_tensor_tensor(out=o[:, :], in0=rank[:, b, :], scalar=base[:, b:b + 1],
                                              in1=mask[:, b, :], op0=ALU.add, op1=ALU.mult))
                if b:
                    step(eng.tensor_tensor(slot[:, :], slot[:, :], part[:, :], ALU.add))
            eng.tensor_copy(slot_i[:, :], slot[:, :]).then_inc(slots_ready, 1)
            step(eng.memset(tile_f[:, :], 0.0))
            eng.wait_ge(idents, 3)
            for b in range(NT - 1):
                step(eng.scalar_tensor_tensor(out=tile_f[:, :], in0=iota_g[:, :], scalar=group_end[0:1, b:b + 1],
                                              in1=tile_f[:, :], op0=ALU.is_ge, op1=ALU.add))
            eng.tensor_copy(tile_i[:, :], tile_f[:, :]).then_inc(tiles_ready, 1)

            eng.wait_ge(consts_in, 80)
            for t in range(KT):
                eng.tensor_scalar(wd[:, t, :], wd[:, t, :], rw[:, t:t + 1], None, ALU.mult).then_inc(wd_ready, 1)
            eng.wait_ge(xl_ones, 1)
            with eng.Fori(0, NT // 2) as j:
                for k in range(2):
                    i = 2 * j + k
                    eng.wait_ge(xl_ones, 1)
                    eng.wait_ge(squared, i + 1)
                    eng.wait_ge(rms_ready, i + 1)
                    eng.tensor_scalar(ms[:, :], ssq[:, 0:1], 1.0 / D, 1e-6, ALU.mult, ALU.add).then_inc(ms_ready, 1)
                    eng.wait_ge(xl_ones, 1)
                    eng.wait_ge(rms_ready, i + 2)
                    eng.reciprocal(rinv[:, :], rms[:, :]).then_inc(dve, 1)
                    eng.wait_ge(dve, n + 3 * i + 1)
                    eng.wait_ge(down, i + 1)
                    eng.tensor_scalar(xd[:, :], pd[:, :], rinv[:, 0:1], None, ALU.mult).then_inc(xd_ready, 1)
                    eng.wait_ge(xl_ones, 1)
                    eng.wait_ge(xd_turned, i + 1)
                    eng.tensor_copy(xdT[:, :], pt[:, :]).then_inc(xdT_ready, 1)
                    eng.wait_ge(xl_ones, 1)
                    eng.wait_ge(lr, i + 1)
                    eng.wait_ge(tabs_out[k], 32 * j + 32)
                    eng.tensor_copy(xl[:, k, :].rearrange("p (h w) -> p h w", h=HEADS)[:, :, 0:HD],
                                    plr[:, 0:HID].rearrange("p (h d) -> p h d", h=HEADS)).then_inc(dve, 1)
                    eng.tensor_copy(xr[:, k, :], plr[:, HID:2 * HID]).then_inc(xr_ready, 1)
                    eng.wait_ge(xl_ones, 1)
                    eng.wait_ge(dve, n + 3 * i + 2)
                    eng.wait_ge(xr_ready, i + 1)
                    eng.tensor_tensor(msg[:, :].rearrange("p (h d) -> p h d", h=HEADS),
                                      xl[:, k, :].rearrange("p (h w) -> p h w", h=HEADS)[:, :, 0:HD],
                                      xr[:, k, :].rearrange("p (h d) -> p h d", h=HEADS), ALU.add)\
                       .then_inc(self_msg, 1)
                    eng.wait_ge(xl_ones, 1)
                    eng.wait_ge(self_msg, i + 1)
                    eng.scalar_tensor_tensor(out=act_s[:, :], in0=msg[:, :], scalar=0.2, in1=msg[:, :],
                                             op0=ALU.mult, op1=ALU.max).then_inc(self_act, 1)
                    eng.wait_ge(xl_ones, 1)
                    eng.wait_ge(self_act, i + 1)
                    eng.tensor_tensor(prod[:, :], act_s[:, :], att_b[:, :], ALU.mult).then_inc(dve, 1)
                    eng.wait_ge(xl_ones, 1)
                    eng.wait_ge(dve, n + 3 * i + 3)
                    eng.tensor_reduce(e_self[:, bass.ds(i, 1), :].rearrange("p a h -> p (a h)"),
                                      prod[:, :].rearrange("p (h d) -> p h d", h=HEADS), AX.X, ALU.add)\
                       .then_inc(self_ready, 1)


def edge_phase(nc, sem, edge_tab, xl_tab, self_tab, xr_tab, tile_tab, att, adj_tab, wt_tab, o_tab,
               deg_inv, deg_rsqrt, wide):
    COLS = N_NODES + 1

    with ExitStack() as ctx:
        def sb(name, shape, dt):
            return ctx.enter_context(nc.sbuf_tensor("ed_" + name, shape, dt))

        def ps(name, shape):
            return ctx.enter_context(nc.psum_tensor("ed_" + name, shape, F32))

        src_f = sb("src_f", [P, NC], F32)
        src_i = sb("src_i", [P, NC], I32)
        loc = sb("loc", [P, NC], F32)
        w_b = sb("w_b", [P, NC], BF16)
        w_part = sb("w_part", [P, 3, NC], F32)
        tiles = sb("tiles", [1, NG + 2], I32)
        zero_b = sb("zero_b", [P, 1], BF16)
        iota_n = sb("iota_n", [P, N_NODES], F16)
        ident = sb("ident", [P, P], F32)
        ident_r = sb("ident_r", [P, P], F32R)
        att_b = sb("att_b", [P, HID], F32)
        src_st = sb("src_st", [P, U, CH], I32)
        gat = sb("gat", [P, U * CH * XW], F32)
        hot_s = sb("hot_s", [P, 2, CH, NPAD], BF16)
        hot_b = sb("hot_b", [P, 2, CH, 4, P], BF16)
        hot_f = sb("hot_f", [P, U, CH, P], F32)
        hot_t = sb("hot_t", [P, 2, CH, P], F32R)
        bound = sb("bound", [P, 2, CH, P], F32)
        xr_hi = sb("xr_hi", [P, NT, HID], F32R)
        xr_lo = sb("xr_lo", [P, NT, HID], F32R)
        work = sb("work", [P, 2, NPAD], F32)
        score = sb("score", [P, 2, CH * HEADS], F32)
        score_r = sb("score_r", [P, 2, CH * HEADS], F32R)
        masked = sb("masked", [P, CH * P], F32)
        group_max = sb("group_max", [P, HEADS], F32)
        new_max = sb("new_max", [P, HEADS], F32)
        shift = sb("shift", [P, HEADS], F32)
        fade = sb("fade", [P, HEADS], F32)
        max_r = sb("max_r", [P, HEADS], F32R)
        expo = sb("expo", [P, CH * HEADS], F32)
        prob = sb("prob", [P, CH * HEADS], F32)
        seg_max = sb("seg_max", [P, NT * HEADS], F32)
        seg_max_r = sb("seg_max_r", [P, NT * HEADS], F32R)
        self_prob = sb("self_prob", [P, NT * HEADS], F32)
        seg_sum = sb("seg_sum", [P, NT, XW], F32)
        adj = sb("adj", [P, NT, NPAD], F32)
        wt = sb("wt", [P, NT, D], F32)

        p_adj = ps("p_adj", [P, 3 * 512])
        p_wt = ps("p_wt", [P, D])
        banks = ps("banks", [P, 3 * 512])
        bank_x, bank_y, bank_z = (banks[:, b * 512:(b + 1) * 512] for b in range(3))

        tabs_in = sem("ed_tabs_in")
        filled = sem("ed_filled")
        consts = sem("ed_consts")
        dve = sem("ed_dve")
        ready = sem("ed_ready")
        tiles_in = sem("ed_tiles_in")
        staged = sem("ed_staged")
        gathered = [sem(f"ed_gathered{u}") for u in range(U)]
        hots = sem("ed_hots")
        turned = sem("ed_turned")
        turned_out = sem("ed_turned_out")
        self_ready = sem("ed_self_ready")
        ones_set = sem("ed_ones_set")
        ends_set = sem("ed_ends_set")
        flushed = sem("ed_flushed")
        xr_done = sem("ed_xr_done")
        xr_ready = sem("ed_xr_ready")
        msg_ready = sem("ed_msg_ready")
        relu_ready = sem("ed_relu_ready")
        act_added = sem("ed_act_added")
        act_scaled = sem("ed_act_scaled")
        local_hots = sem("ed_local_hots")
        parts_ready = sem("ed_parts_ready")
        wt_cleared = sem("ed_wt_cleared")
        score_ready = sem("ed_score_ready")
        spread = sem("ed_spread")
        head_max = sem("ed_head_max")
        shift_ready = sem("ed_shift_ready")
        fade_ready = sem("ed_fade_ready")
        max_ready = sem("ed_max_ready")
        max_back = sem("ed_max_back")
        expo_ready = sem("ed_expo_ready")
        prob_ready = sem("ed_prob_ready")
        weighted = sem("ed_weighted")
        summed = sem("ed_summed")
        sums_added = sem("ed_sums_added")
        counted = sem("ed_counted")
        adj_st_ready = sem("ed_adj_st_ready")
        adj_turned = sem("ed_adj_turned")
        adj_t_ready = sem("ed_adj_t_ready")
        adj_out = [sem(f"ed_adj_out{k}") for k in range(2)]
        deg_out = sem("ed_deg_out")
        deg_max_ready = sem("ed_deg_max_ready")
        deg_max_turned = sem("ed_deg_max_turned")
        deg_done = sem("ed_deg_done")
        root = sem("ed_root")
        o_ready = sem("ed_o_ready")
        last_out = sem("ed_last_out")

        deg = sb("deg", [P, NT], F32)
        deg1 = sb("deg1", [P, NT], F32)
        deg_max = sb("deg_max", [P, 1], F32)
        deg_top = sb("deg_top", [1, 1], F32)
        droot = sb("droot", [P, NT], F32)
        den = masked[:, 0:NT * HEADS].rearrange("p (t h) -> p t h", h=HEADS)
        xlg = gat[:, :].rearrange("p (u c w) -> p u c w", u=U, c=CH)
        msg = work[:, 0, 0:CH * HID]
        act_m = work[:, 1, 0:CH * HID]
        w_rest = masked[:, 0:NC]
        slots = wt[:, :, :].rearrange("p t n -> p (t n)")[:, 0:NC * 4].rearrange("p (c w) -> p c w", w=4)
        adj_st = work
        adj_t = gat[:, 0:2 * NPAD].rearrange("p (k n) -> p k n", k=2)

        block = ctx.enter_context(nc.Block())

        @block.sync
        def _(eng):
            eng.dma_start(wt[:, :, :].rearrange("p t n -> p (t n)")[:, 0:NC * 4].rearrange("p (g w) -> p g w", w=4 * CH),
                          edge_tab.rearrange("(g p c) w -> p g (c w)", p=P, c=CH)).then_inc(tabs_in, 16)
            eng.dma_start(seg_max[:, :], self_tab.rearrange("p t h -> p (t h)")).then_inc(tabs_in, 16)
            eng.dma_start(seg_sum[:, :, :], xl_tab.rearrange("(t p) w -> p t w", p=P)).then_inc(tabs_in, 16)
            eng.dma_start(adj[:, 0:2, :].rearrange("p a n -> p (a n)").rearrange("p (t n) -> p t n", t=NT),
                          xr_tab.rearrange("(t p) n -> p t n", p=P)).then_inc(tabs_in, 16)
            eng.dma_start(att_b[:, :], att.rearrange("h d -> (h d)").partition_broadcast(P)).then_inc(tabs_in, 16)
            eng.dma_start(tiles[:, 1:NG + 1], tile_tab).then_inc(tiles_in, 16)
            eng.wait_ge(deg_out, 1)
            for t in range(D // P):
                eng.dma_start(wt_tab[t * P:(t + 1) * P, :], wt[:, t, :]).then_inc(last_out, 16)
            eng.wait_ge(o_ready, 1)
            for h in range(HEADS):
                eng.dma_start(o_tab.rearrange("(t p) (h d) -> p t h d", p=P, h=HEADS)[:, :, h, :],
                              seg_sum[:, :, h * HW:h * HW + HD]).then_inc(last_out, 16)
            with eng.Fori(0, NT // 2) as j:
                for k in range(2):
                    i = 2 * j + k
                    eng.wait_ge(tiles_in, 16)
                    eng.wait_ge(adj_t_ready, i + 3)
                    eng.dma_start(adj_tab[bass.ds(i * P, P), :], adj_t[:, k, :]).then_inc(adj_out[k], 16)
            for k in range(2):
                eng.wait_ge(adj_out[k], 16 * (NT // 2) + 16)
            eng.wait_ge(last_out, 16 * (D // P + HEADS))

        @block.gpsimd
        def _(eng):
            eng.memset(ident[:, :], 0.0).then_inc(filled, 1)
            eng.iota(iota_n[:, :], [[1, N_NODES]], base=0, channel_multiplier=0,
                     allow_small_or_imprecise_dtypes=True).then_inc(consts, 1)
            eng.memset(tiles[:, 0:1], NT).then_inc(ends_set, 1)
            eng.memset(tiles[:, NG + 1:NG + 2], NT).then_inc(ends_set, 1)
            eng.memset(zero_b[:, :], 0.0).then_inc(ones_set, 1)
            eng.memset(hot_s[:, :, :, N_NODES], 1.0).then_inc(ones_set, 1)
            eng.wait_ge(filled, 1)
            eng.affine_select(out=ident[:, :], in_=ident[:, :], compare_op=ALU.not_equal, fill=1.0, base=0,
                              pattern=[[-1, P]], channel_multiplier=1).then_inc(consts, 1)
            eng.wait_ge(ready, 1)
            eng.memset(wt[:, :, :], 0.0).then_inc(wt_cleared, 1)

            def gather(g, u):
                eng.wait_ge(ready, 1)
                eng.tensor_copy(src_st[:, u, :], src_i[:, bass.ds(g * CH, CH)]).then_inc(staged, 1)
                due = eng.to_reg(g + 1) if not isinstance(g, int) else g + 1
                eng.wait_ge(ready, 1)
                eng.wait_ge(staged, due)
                for c in range(CH):
                    eng.indirect_dma_start(xlg[:, u, c, :], None, xl_tab,
                                           bass.IndirectOffsetOnAxis(ap=src_st[:, u, c:c + 1], axis=0))\
                       .then_inc(gathered[u], 16)

            def weigh(g):
                eng.wait_ge(ready, 1)
                eng.wait_ge(relu_ready, g + 1)
                eng.tensor_tensor(act_m, msg, act_m, ALU.add).then_inc(act_added, 1)
                eng.wait_ge(ready, 1)
                eng.wait_ge(act_added, g + 1)
                eng.tensor_tensor(act_m.rearrange("p (c d) -> p c d", c=CH), act_m.rearrange("p (c d) -> p c d", c=CH),
                                  att_b[:, :].unsqueeze(1).broadcast_to([P, CH, HID]), ALU.mult).then_inc(act_scaled, 1)

            for g in range(3):
                gather(g, g)
            weigh(0)

            def body(g, u):
                if not isinstance(g, int) or g + 1 < NG:
                    weigh(g + 1)
                if not isinstance(g, int) or g + 3 < NG:
                    eng.wait_ge(summed, g + 1)
                    gather(g + 3, (u + 3) % U)

            with eng.Fori(0, NG // U - 1) as j:
                for u in range(U):
                    body(U * j + u, u)
            for u in range(U):
                body(NG - U + u, u)

        @block.scalar
        def _(eng):
            eng.wait_ge(consts, 2)
            eng.activation(ident_r[:, :], ident[:, :], ACT.Copy).then_inc(consts, 1)

            def turn_out(g, k):
                eng.wait_ge(ready, 1)
                eng.wait_ge(turned, g + 1)
                turned_bank = bank_x[:, :].rearrange("p (c e) -> p c e", c=CH)
                eng.activation(hot_t[:, k, :, :], turned_bank, ACT.Copy).then_inc(turned_out, 1)
                eng.activation(bound[:, k, :, :], turned_bank, ACT.Copy, scale=BIG, bias=-BIG).then_inc(turned_out, 1)

            def relu(g):
                eng.wait_ge(msg_ready, 2 * g + 2)
                if not isinstance(g, int) or g > 0:
                    eng.wait_ge(score_ready, g)
                eng.activation(act_m, msg, ACT.Relu, scale=4.0).then_inc(relu_ready, 1)

            def parts(g, u, c):
                k, at = u % 2, g * CH + c
                eng.wait_ge(ready, 1)
                eng.wait_ge(local_hots, at + 1)
                eng.wait_ge(counted, at + 1)
                eng.activation(hot_b[:, k, c, 0, :], hot_f[:, u, c, :], ACT.Copy)
                for q in range(3):
                    a = eng.activation(hot_b[:, k, c, 1 + q, :], hot_f[:, u, c, :], ACT.Copy,
                                       scale=w_part[:, q, bass.ds(at, 1)])
                a.then_inc(parts_ready, 1)

            def body(g, u):
                if not isinstance(g, int) or g + 1 < NG:
                    relu(g + 1)
                    for c in range(2):
                        parts(g + 1, (u + 1) % U, c)
                eng.wait_ge(ready, 1)
                eng.wait_ge(shift_ready, g + 1)
                eng.activation(fade[:, :], shift[:, :], ACT.Exp).then_inc(fade_ready, 1)
                eng.wait_ge(ready, 1)
                eng.wait_ge(expo_ready, g + 1)
                eng.activation(prob[:, :], expo[:, :], ACT.Exp).then_inc(prob_ready, 1)
                if not isinstance(g, int) or g + 1 < NG:
                    for c in (2, 3):
                        parts(g + 1, (u + 1) % U, c)
                if not isinstance(g, int) or g + 2 < NG:
                    turn_out(g + 2, u % 2)

            eng.wait_ge(ready, 1)
            eng.activation(self_prob[:, :], self_prob[:, :], ACT.Exp).then_inc(self_ready, 1)
            turn_out(0, 0)
            relu(0)
            for c in range(CH):
                parts(0, 0, c)
            turn_out(1, 1)
            with eng.Fori(0, NG // U - 1) as j:
                for u in range(U):
                    body(U * j + u, u)
            for u in range(U):
                body(NG - U + u, u)
            eng.wait_ge(deg_out, 1)
            with eng.Fori(0, NT // 2) as j:
                for k in range(2):
                    i = 2 * j + k
                    eng.wait_ge(sums_added, NG + 1)
                    eng.wait_ge(adj_turned, i + 1)
                    eng.activation(adj_st[:, k, :], adj[:, bass.ds(i, 1), :].rearrange("p a n -> p (a n)"),
                                   ACT.Copy).then_inc(adj_st_ready, 1)
            eng.wait_ge(deg_done, 1)
            eng.activation(droot[:, :], deg1[:, :], ACT.Sqrt).then_inc(root, 1)

        @block.tensor
        def _(eng):
            eng.sem_inc(counted, 2 * CH)
            eng.sem_inc(adj_turned, 2)
            eng.sem_inc(summed, 1)

            PIECES = ((p_adj, 0, 512), (p_adj, 512, 1024), (p_adj, 1024, COLS), (p_wt, 0, 512), (p_wt, 512, 1024))

            def turn(g, u):
                eng.wait_ge(ready, 1)
                eng.wait_ge(local_hots, CH * g + CH)
                for c in range(CH):
                    mm = eng.transpose(bank_x[:, c * P:(c + 1) * P], hot_f[:, u, c, :], ident[:, :])
                mm.then_inc(turned, 1)

            def destinations(g, u):
                k = u % 2
                t = eng.value_load(tiles[0:1, bass.ds(g + 1, 1)], min_val=0, max_val=NT - 1)
                eng.wait_ge(ready, 1)
                eng.wait_ge(turned_out, 2 * g + 1)
                if not isinstance(g, int) or g > 0:
                    eng.wait_ge(sums_added, g)
                for c in range(CH):
                    bank = (bank_y, bank_z)[c // 2]
                    for q, part in enumerate((xr_hi, xr_lo)):
                        mm = eng.matmul(bank[:, (c % 2) * HID:(c % 2 + 1) * HID], hot_t[:, k, c, :],
                                        part[:, bass.ds(t, 1), :].rearrange("p a n -> p (a n)"),
                                        start=(q == 0), stop=(q == 1))
                    if c % 2 == 1:
                        mm.then_inc(xr_done, 1)

            def counts(g, u, c, before=None, here=None):
                k = u % 2
                if c == 0:
                    with eng.If(here != before):
                        eng.wait_ge(ready, 1)
                        eng.wait_ge(hots, CH * g + 1)
                        if not isinstance(g, int) or g + 1 < NG:
                            eng.wait_ge(msg_ready, 2 * g + 3)
                        else:
                            eng.wait_ge(head_max, HEADS * g + 1)
                        for bank, n0, n1 in PIECES:
                            eng.matmul(bank[:, n0:n1], zero_b[:, :].broadcast_to([P, P]), hot_s[:, k, 0, n0:n1], start=True, stop=False,
                                       skip_group_check=True)
                eng.wait_ge(ready, 1)
                eng.wait_ge(hots, CH * g + c + 1)
                eng.wait_ge(parts_ready, CH * g + c + 1)
                for bank, n0, n1 in PIECES:
                    for q in ((0,) if bank is p_adj else (1, 2, 3)):
                        mm = eng.matmul(bank[:, n0:n1], hot_b[:, k, c, q, :], hot_s[:, k, c, n0:n1],
                                        start=False, stop=False, skip_group_check=True)
                mm.then_inc(counted, 1)

            def spread_head(g, u, h):
                bank = (bank_x, bank_y, bank_z, bank_x)[h]
                for c in range(CH):
                    mm = eng.matmul(bank[:, c * P:(c + 1) * P],
                                    score_r[:, u % 2, c * HEADS + h:c * HEADS + h + 1].broadcast_to([P, P]),
                                    ident_r[:, :], start=True, stop=True)
                mm.then_inc(spread, 1)

            def body(g, u):
                more = not isinstance(g, int) or g + 1 < NG
                before = eng.value_load(tiles[0:1, bass.ds(g, 1)], min_val=0, max_val=NT)
                here = eng.value_load(tiles[0:1, bass.ds(g + 1, 1)], min_val=0, max_val=NT)
                if more:
                    destinations(g + 1, (u + 1) % U)
                    eng.wait_ge(ready, 1)
                    eng.wait_ge(turned_out, 2 * g + 4)
                eng.wait_ge(ready, 1)
                eng.wait_ge(score_ready, g + 1)
                spread_head(g, u, 0)
                counts(g, u, 0, before, here)
                if more:
                    eng.wait_ge(ready, 1)
                    eng.wait_ge(msg_ready, 2 * g + 4)
                else:
                    eng.wait_ge(sums_added, g + 1)
                for h in (1, 2):
                    spread_head(g, u, h)
                eng.wait_ge(ready, 1)
                eng.wait_ge(head_max, HEADS * g + 1)
                spread_head(g, u, 3)
                counts(g, u, 1)
                eng.wait_ge(ready, 1)
                eng.wait_ge(max_ready, g + 1)
                for c in range(CH):
                    mm = eng.matmul(bank_z[:, c * HEADS:(c + 1) * HEADS], hot_t[:, u % 2, c, :], max_r[:, :],
                                    start=True, stop=True)
                mm.then_inc(max_back, 1)
                counts(g, u, 2)
                eng.wait_ge(ready, 1)
                eng.wait_ge(weighted, g + 1)
                for c in range(CH):
                    mm = eng.matmul(bank_y[:, 0:XW], hot_f[:, u, c, :], xlg[:, u, c, :],
                                    start=(c == 0), stop=(c == CH - 1))
                mm.then_inc(summed, 1)
                if not isinstance(g, int) or g + 2 < NG:
                    turn(g + 2, (u + 2) % U)
                counts(g, u, 3)

            eng.wait_ge(consts, 3)
            eng.wait_ge(ones_set, 2)
            eng.wait_ge(ends_set, 2)
            eng.wait_ge(tiles_in, 16)
            turn(0, 0)
            eng.wait_ge(xr_ready, 1)
            destinations(0, 0)
            eng.wait_ge(turned_out, 2)
            turn(1, 1)
            with eng.Fori(0, NG // U - 1) as j:
                for u in range(U):
                    body(U * j + u, u)
            for u in range(U):
                body(NG - U + u, u)
            eng.wait_ge(deg_max_ready, 1)
            eng.transpose(p_wt[0:1, 0:P], deg_max[:, :], ident[:, :]).then_inc(deg_max_turned, 1)
            with eng.Fori(0, NT // 2) as j:
                for k in range(2):
                    i = 2 * j + k
                    eng.wait_ge(sums_added, NG + 1)
                    eng.wait_ge(adj_st_ready, i + 1)
                    eng.wait_ge(adj_t_ready, i + 1)
                    for s in range(NT):
                        mm = eng.transpose((p_adj, banks)[k][:, s * P:(s + 1) * P], adj_st[:, k, s * P:(s + 1) * P], ident[:, :])
                    mm.then_inc(adj_turned, 1)

        @block.vector
        def _(eng):
            eng.sem_inc(sums_added, 1)
            n = 0

            def step(ins):
                nonlocal n
                n += 1
                ins.then_inc(dve, 1)
                eng.wait_ge(dve, n)

            eng.wait_ge(tabs_in, 80)
            eng.wait_ge(ends_set, 2)
            eng.wait_ge(tiles_in, 16)
            eng.wait_ge(consts, 3)
            step(eng.tensor_copy(src_f[:, :], slots[:, :, 0]))
            step(eng.tensor_copy(src_i[:, :], slots[:, :, 0]))
            step(eng.tensor_copy(loc[:, :], slots[:, :, 1]))
            step(eng.tensor_copy(w_rest, slots[:, :, 2]))
            for q in range(3):
                step(eng.tensor_copy(w_b[:, :], w_rest))
                step(eng.tensor_copy(w_part[:, q, :], w_b[:, :]))
                step(eng.tensor_tensor(w_rest, w_rest, w_part[:, q, :], ALU.subtract))
            step(eng.tensor_scalar(att_b[:, :], att_b[:, :], 0.2, None, ALU.mult))
            step(eng.tensor_copy(seg_max_r[:, :], seg_max[:, :]))
            step(eng.tensor_tensor(self_prob[:, :], seg_max[:, :], seg_max_r[:, :].bitcast(F32), ALU.subtract))
            eng.sem_inc(ready, 1)
            step(eng.tensor_copy(seg_max[:, :], seg_max_r[:, :].bitcast(F32)))

            def hot_local(g, u):
                for c in range(CH):
                    eng.tensor_scalar(hot_f[:, u, c, :], iota_n[:, 0:P], loc[:, bass.ds(g * CH + c, 1)], None,
                                      ALU.is_equal).then_inc(local_hots, 1)

            def hot_source(g, u, c):
                at = g * CH + c
                eng.wait_ge(ready, 1)
                eng.wait_ge(counted, at + 1)
                eng.tensor_scalar(hot_s[:, u % 2, c, 0:N_NODES], iota_n[:, 0:N_NODES], src_f[:, bass.ds(at, 1)], None, ALU.is_equal)\
                   .then_inc(hots, 1)

            hot_local(0, 0)
            eng.wait_ge(self_ready, 1)
            for t in range(NT):
                rows = seg_sum[:, t, :].rearrange("p (h w) -> p h w", h=HEADS)
                step(eng.tensor_tensor(rows, rows, self_prob[:, t * HEADS:(t + 1) * HEADS].unsqueeze(2)
                                       .broadcast_to([P, HEADS, HW]), ALU.mult))
            landed = adj[:, 0:2, :].rearrange("p a n -> p (a n)").rearrange("p (t n) -> p t n", t=NT)
            step(eng.tensor_copy(xr_hi[:, :, :], landed))
            step(eng.tensor_tensor(xr_lo[:, :, :], landed, xr_hi[:, :, :].bitcast(F32), ALU.subtract))
            eng.sem_inc(xr_ready, 1)
            hot_local(1, 1)
            step(eng.memset(adj[:, :, :], 0.0))
            for c in range(CH):
                hot_source(0, 0, c)
            at0 = n + 1
            STEPS = 5

            def link(ins, done):
                ins.then_inc(dve, 1)
                eng.wait_ge(ready, 1)
                eng.wait_ge(dve, done)

            def messages(g, r, u):
                eng.wait_ge(gathered[u], 16 * CH * (r + 1))
                for b, bank in enumerate((bank_y, bank_z)):
                    eng.wait_ge(ready, 1)
                    eng.wait_ge(xr_done, 2 * g + b + 1)
                    eng.tensor_tensor(msg[:, 2 * b * HID:(2 * b + 2) * HID].rearrange("p (c d) -> p c d", d=HD),
                                      xlg[:, u, 2 * b:2 * b + 2, :].rearrange("p c (h w) -> p (c h) w", h=HEADS)[:, :, 0:HD],
                                      bank[:, :].rearrange("p (c d) -> p c d", d=HD), ALU.add).then_inc(msg_ready, 1)

            def scores(g, u, done):
                eng.wait_ge(ready, 1)
                eng.wait_ge(act_scaled, g + 1)
                link(eng.tensor_reduce(score[:, u % 2, :], act_m.rearrange("p (c d) -> p c d", d=HD), AX.X, ALU.add), done)
                eng.tensor_copy(score_r[:, u % 2, :], score[:, u % 2, :]).then_inc(score_ready, 1)

            def head_maximum(g, u, h):
                bank = (bank_x, bank_y, bank_z, bank_x)[h]
                here, before = g * HEADS + (h + 1), g * HEADS + h
                if not isinstance(g, int):
                    here, before = eng.to_reg(here), eng.to_reg(before) if h else None
                eng.wait_ge(ready, 1)
                eng.wait_ge(spread, here)
                if h:
                    eng.wait_ge(head_max, before)
                eng.tensor_tensor_reduce(masked[:, :], bank[:, :], bound[:, u % 2, :, :].rearrange("p c e -> p (c e)"),
                                         1.0, -BIG, ALU.add, ALU.max, group_max[:, h:h + 1]).then_inc(head_max, 1)

            def leave(g, t):
                run_adj = adj[:, bass.ds(t, 1), 0:COLS].rearrange("p a n -> p (a n)")
                run_wt = wt[:, bass.ds(t, 1), :].rearrange("p a n -> p (a n)")
                eng.wait_ge(ready, 1)
                eng.wait_ge(counted, CH * g + CH + 2 * CH)
                eng.tensor_tensor(run_adj, run_adj, p_adj[:, 0:COLS], ALU.add)
                return eng.tensor_tensor(run_wt, run_wt, p_wt[:, :], ALU.add)

            def body(g, r, u):
                more = not isinstance(g, int) or g + 1 < NG
                t = eng.value_load(tiles[0:1, bass.ds(g + 1, 1)], min_val=0, max_val=NT - 1)
                at = at0 + STEPS * g
                if more:
                    messages(g + 1, r if u < U - 1 else r + 1, (u + 1) % U)
                for h in range(HEADS):
                    head_maximum(g, u, h)
                run_max = seg_max[:, bass.ds(t * HEADS, HEADS)]
                eng.wait_ge(ready, 1)
                eng.wait_ge(head_max, HEADS * g + HEADS)
                link(eng.tensor_tensor(new_max[:, :], run_max, group_max[:, :], ALU.max), at + 1)
                eng.tensor_copy(max_r[:, :], new_max[:, :]).then_inc(max_ready, 1)
                eng.tensor_tensor(shift[:, :], run_max, new_max[:, :], ALU.subtract).then_inc(shift_ready, 1)
                eng.wait_ge(ready, 1)
                eng.wait_ge(shift_ready, g + 1)
                eng.tensor_scalar(run_max, new_max[:, :], 1.0, None, ALU.mult).then_inc(dve, 1)
                eng.wait_ge(ready, 1)
                eng.wait_ge(max_back, g + 1)
                link(eng.tensor_tensor(expo[:, :], score[:, u % 2, :], bank_z[:, 0:CH * HEADS], ALU.subtract), at + 3)
                eng.tensor_scalar(expo[:, :], expo[:, :], 80.0, None, ALU.min).then_inc(expo_ready, 1)
                run_sum = seg_sum[:, bass.ds(t, 1), :].rearrange("p a (h w) -> p (a h) w", h=HEADS)
                eng.wait_ge(ready, 1)
                eng.wait_ge(fade_ready, g + 1)
                eng.wait_ge(sums_added, g + 1)
                eng.tensor_tensor(run_sum, run_sum, fade[:, :].unsqueeze(2).broadcast_to([P, HEADS, HW]), ALU.mult)\
                   .then_inc(dve, 1)
                eng.wait_ge(ready, 1)
                eng.wait_ge(prob_ready, g + 1)
                rows = xlg[:, u, :, :].rearrange("p c (h w) -> p (c h) w", h=HEADS)
                eng.tensor_tensor(rows, rows, prob[:, :].unsqueeze(2).broadcast_to([P, CH * HEADS, HW]), ALU.mult)\
                   .then_inc(weighted, 1)
                if not isinstance(g, int) or g + 2 < NG:
                    hot_local(g + 2, (u + 2) % U)
                if more:
                    for c in range(CH):
                        hot_source(g + 1, u + 1, c)
                eng.wait_ge(ready, 1)
                eng.wait_ge(dve, at + 4)
                eng.wait_ge(summed, g + 2)
                eng.tensor_tensor(run_sum, run_sum, bank_y[:, 0:XW].rearrange("p (h w) -> p h w", h=HEADS), ALU.add)\
                   .then_inc(sums_added, 1)
                following = eng.value_load(tiles[0:1, bass.ds(g + 2, 1)], min_val=0, max_val=NT)
                if more:
                    scores(g + 1, u + 1, at + 5)
                    with eng.If(following != t):
                        leave(g, t)
                else:
                    leave(g, t).then_inc(flushed, 1)

            messages(0, 0, 0)
            scores(0, 0, n + 1)
            eng.wait_ge(wt_cleared, 1)
            with eng.Fori(0, NG // U - 1) as j:
                for u in range(U):
                    body(U * j + u, j, u)
            for u in range(U):
                body(NG - U + u, NG // U - 1, u)

            n = at0 + STEPS * NG - 1
            eng.wait_ge(sums_added, NG + 1)
            eng.wait_ge(flushed, 1)
            step(eng.tensor_copy(deg[:, :], adj[:, :, N_NODES]))
            step(eng.memset(adj[:, :, N_NODES], 0.0))
            eng.sem_inc(deg_out, 1)
            step(eng.tensor_reduce(deg_max[:, :], deg[:, :], AX.X, ALU.max))
            eng.sem_inc(deg_max_ready, 1)
            step(eng.tensor_scalar(deg1[:, :], deg[:, :], 1.0, None, ALU.max))
            step(eng.reciprocal(deg_inv[:, :], deg1[:, :]))
            step(eng.tensor_scalar(deg1[:, :], deg[:, :], 1.0, None, ALU.add))
            eng.sem_inc(deg_done, 1)
            eng.wait_ge(deg_max_turned, 1)
            step(eng.tensor_reduce(deg_top[:, :], p_wt[0:1, 0:P], AX.X, ALU.max))
            step(eng.tensor_scalar(deg_top[:, :], deg_top[:, :], COUNT_EXACT, None, ALU.is_gt))
            step(eng.tensor_copy(wide[:, :], deg_top[:, :]))
            sums = seg_sum[:, :, :].rearrange("p t (h w) -> p t h w", h=HEADS)
            step(eng.tensor_scalar(den, sums[:, :, :, HD], 1e-16, None, ALU.add))
            step(eng.reciprocal(den, den))
            for t in range(NT):
                rows = seg_sum[:, t, :].rearrange("p (h w) -> p h w", h=HEADS)
                divided = eng.tensor_tensor(rows, rows, den[:, t, :].unsqueeze(2).broadcast_to([P, HEADS, HW]), ALU.mult)
            divided.then_inc(o_ready, 1)
            eng.sem_inc(adj_t_ready, 2)
            eng.sem_inc(adj_out[0], 16)
            eng.sem_inc(adj_out[1], 16)
            with eng.Fori(0, NT // 2) as j:
                for k in range(2):
                    i = 2 * j + k
                    eng.wait_ge(sums_added, NG + 1)
                    eng.wait_ge(adj_turned, i + 3)
                    eng.wait_ge(adj_out[k], 16 * j + 16)
                    eng.tensor_scalar(adj_t[:, k, :], (p_adj, banks)[k][:, 0:NPAD], 1.0, None, ALU.mult)\
                       .then_inc(adj_t_ready, 1)
            eng.wait_ge(root, 1)
            step(eng.reciprocal(deg_rsqrt[:, :], droot[:, :]))


def dense_phase(nc, sem, tag, sources, resident=None, scale=None, add_first=None, bias=None, relu=False,
                add=None, norm=False, out=None, add_after=None, out_after=None, wide=None):
    S = len(sources)
    kts = [right.shape[0] // P for _, _, right in sources]
    KTS = sum(kts)
    KM = max(kts)
    right_tiles = [(right, t) for (_, _, right), kt in zip(sources, kts) for t in range(kt)]
    rows = [r for r in (add_first, add, add_after) if r is not None]
    R = len(rows)
    RB = 4 if S == 1 else 3
    EARLY = min(3, KTS)
    LAG = 4

    with ExitStack() as ctx:
        def sb(name, shape, dt=F32):
            return ctx.enter_context(nc.sbuf_tensor(tag + name, shape, dt))

        right_hi = sb("right_hi", [P, KTS, D], F32R)
        right_lo = sb("right_lo", [P, KTS, D], F32R)
        right_in = sb("right_in", [P, RB, D])
        left_in = sb("left_in", [P, 2, KM * P]) if sources[0][0] != "held" else None
        left_hi = sb("left_hi", [P, 2 * S, KM * P], F32R)
        left_lo = sb("left_lo", [P, 2 * S, KM * P], F32R)
        ident = sb("ident", [P, P])
        y = sb("y", [P, 2, D])
        row_in = sb("row_in", [P, 2, R, D]) if R else None
        y2 = sb("y2", [P, 2, D]) if out_after is not None else None
        bias_b = sb("bias_b", [P, D]) if bias is not None else None
        stats = sb("stats", [P, 2, 6])
        mean_var = sb("mean_var", [P, 2])
        var_eps = sb("var_eps", [P, 1])
        std = sb("std", [P, 1])
        rstd = sb("rstd", [P, 1])
        turn = ctx.enter_context(nc.psum_tensor(tag + "turn", [P, 2, D], F32))
        acc = ctx.enter_context(nc.psum_tensor(tag + "acc", [P, 2, D], F32))

        started = sem(tag + "started")
        filled = sem(tag + "filled")
        ident_ready = sem(tag + "ident_ready")
        bias_in = sem(tag + "bias_in")
        right_landed = [sem(tag + f"right_landed{k}") for k in range(RB)]
        right_hi_ready = sem(tag + "right_hi_ready")
        right_lo_ready = sem(tag + "right_lo_ready")
        left_landed = [sem(tag + f"left_landed{k}") for k in range(2)]
        turned = sem(tag + "turned")
        hi_ready = sem(tag + "hi_ready")
        lo_ready = sem(tag + "lo_ready")
        multiplied = sem(tag + "multiplied")
        row_landed = [sem(tag + f"row_landed{k}") for k in range(2)]
        chain = sem(tag + "chain")
        eps_added = sem(tag + "eps_added")
        rooted = sem(tag + "rooted")
        y_ready = sem(tag + "y_ready")
        y2_ready = sem(tag + "y2_ready")
        y_left = [sem(tag + f"y_left{k}") for k in range(2)]
        y2_left = [sem(tag + f"y2_left{k}") for k in range(2)]

        OPS = (add_first is not None) + (bias is not None or scale is not None) + relu + (add is not None)
        LINKS = OPS + 4 if norm else OPS - 1

        block = ctx.enter_context(nc.Block())

        @block.sync
        def _(eng):
            eng.sem_inc(started, 1)

            def load_left(i, k):
                for s in range(S):
                    if sources[s][0] == "held":
                        continue
                    q = (k * S + s) % 2
                    eng.wait_ge(started, 5)
                    if sources[s][0] == "rows":
                        eng.wait_ge(turned, S * i + s + 1)
                    else:
                        eng.wait_ge(lo_ready, S * i + s + 1)
                        eng.wait_ge(hi_ready, S * i + s + 1)
                    eng.dma_start(left_in[:, q, 0:kts[s] * P], sources[s][1][bass.ds(i * P, P), :])\
                       .then_inc(left_landed[q], 16)

            def load_right(n):
                right, t = right_tiles[n]
                if n >= RB:
                    eng.wait_ge(right_lo_ready, n - RB + 1)
                    eng.wait_ge(right_hi_ready, n - RB + 1)
                eng.dma_start(right_in[:, n % RB, :], right[t * P:(t + 1) * P, :]).then_inc(right_landed[n % RB], 16)

            def load_rows(i, k):
                for r in range(R):
                    eng.dma_start(row_in[:, k, r, :], rows[r][bass.ds(i * P, P), :]).then_inc(row_landed[k], 16)

            load_left(0, 0)
            load_right(0)
            load_right(1)
            load_left(1, 1)
            for n in range(2, KTS):
                load_right(n)
            if bias is not None:
                eng.dma_start(bias_b[:, :], bias.partition_broadcast(P)).then_inc(bias_in, 16)
            for k in range(2):
                load_rows(k, k)
            load_left(2, 0)

            def store(i, k):
                n = N_NODES - (NT - 1) * P if out.shape[0] != NPAD and i is NT - 1 else P
                eng.dma_start(out[bass.ds(i * P, n), :], y[0:n, k, :]).then_inc(y_left[k], 16)
                if out_after is not None:
                    eng.dma_start(out_after[bass.ds(i * P, P), :], y2[:, k, :]).then_inc(y2_left[k], 16)

            def body(i, k, last=False):
                if not last:
                    load_left(i + 1, 1 - k)
                eng.wait_ge(started, 5)
                eng.wait_ge(y_ready, i + 1)
                if out_after is not None:
                    eng.wait_ge(y2_ready, i + 1)
                store(i - 2, k)
                load_rows(i, k)

            with eng.Fori(1, NT // 2 - 1) as j:
                for k in range(2):
                    body(2 * j + k, k)
            body(NT - 2, 0)
            body(NT - 1, 1, last=True)
            for i in (NT - 2, NT - 1):
                eng.wait_ge(y_ready, i + 3)
                if out_after is not None:
                    eng.wait_ge(y2_ready, i + 3)
                store(i, i % 2)
            for k in range(2):
                eng.wait_ge(y_left[k], 16 * (NT // 2) + 16)
                if out_after is not None:
                    eng.wait_ge(y2_left[k], 16 * (NT // 2) + 16)

        @block.gpsimd
        def _(eng):
            eng.sem_inc(started, 1)
            eng.memset(ident[:, :], 0.0).then_inc(filled, 1)
            eng.wait_ge(filled, 1)
            eng.affine_select(out=ident[:, :], in_=ident[:, :], compare_op=ALU.not_equal, fill=1.0, base=0,
                              pattern=[[-1, P]], channel_multiplier=1).then_inc(ident_ready, 1)

        @block.scalar
        def _(eng):
            eng.sem_inc(started, 1)
            eng.sem_inc(hi_ready, 2)

            def right_high(n):
                eng.wait_ge(right_landed[n % RB], 16 * (n // RB) + 16)
                eng.activation(right_hi[:, n, :], right_in[:, n % RB, :], ACT.Copy).then_inc(right_hi_ready, 1)

            def high(i, j, k, s):
                kind, kt, q, b = sources[s][0], kts[s], (k * S + s) % 2, k * S + s
                eng.wait_ge(started, 5)
                eng.wait_ge(multiplied, S * i + s + 1)
                if kind == "rows":
                    eng.wait_ge(turned, S * i + s + 3)
                    eng.activation(left_hi[:, b, 0:kt * P], turn[:, q, 0:kt * P], ACT.Copy).then_inc(hi_ready, 1)
                elif kind == "turned":
                    eng.wait_ge(left_landed[q], 16 * j + 16)
                    eng.activation(left_hi[:, b, 0:kt * P], left_in[:, q, 0:kt * P], ACT.Copy).then_inc(hi_ready, 1)
                else:
                    eng.activation(left_hi[:, b, :].rearrange("p (t n) -> p t n", t=kt),
                                   resident[:, :, bass.ds(i * P, P)], ACT.Copy).then_inc(hi_ready, 1)

            for s in range(S):
                high(0, 0, 0, s)
            for n in range(EARLY):
                right_high(n)
            for s in range(S):
                high(1, 0, 1, s)
            for n in range(EARLY, KTS):
                right_high(n)
            with eng.Fori(0, NT // 2 - 1) as j:
                for k in range(2):
                    i = 2 * j + k
                    for s in range(S):
                        high(i + 2, j + 1, k, s)
                    if norm:
                        eng.wait_ge(started, 5)
                        eng.wait_ge(eps_added, i + 1)
                        eng.activation(std[:, :], var_eps[:, :], ACT.Sqrt).then_inc(rooted, 1)
            if norm:
                for i in (NT - 2, NT - 1):
                    eng.wait_ge(eps_added, i + 1)
                    eng.activation(std[:, :], var_eps[:, :], ACT.Sqrt).then_inc(rooted, 1)

        @block.tensor
        def _(eng):
            eng.sem_inc(started, 1)
            eng.sem_inc(turned, 2)
            eng.sem_inc(multiplied, 2 * S)
            eng.wait_ge(ident_ready, 1)

            def transposes(i, j, k, s):
                if sources[s][0] != "rows":
                    return
                q = (k * S + s) % 2
                eng.wait_ge(started, 5)
                eng.wait_ge(left_landed[q], 16 * (j + 1) if S == 1 else 16 * (i + 1))
                eng.wait_ge(hi_ready, S * i + s + 1)
                eng.wait_ge(lo_ready, S * i + s + 1)
                for t in range(kts[s]):
                    mm = eng.transpose(turn[:, q, t * P:(t + 1) * P], left_in[:, q, t * P:(t + 1) * P], ident[:, :])
                mm.then_inc(turned, 1)

            if wide is not None:
                low_counts = eng.value_load(wide[0:1, 0:1], min_val=0, max_val=1)

            def product(k, s, t, n0, parts):
                at = sum(kts[:s]) + t
                for a, b in parts:
                    mm = eng.matmul(acc[:, k, n0:n0 + 512], a[:, k * S + s, t * P:(t + 1) * P], b[:, at, n0:n0 + 512],
                                    start=(at == 0 and a is left_hi and b is right_hi),
                                    stop=(at == KTS - 1 and b is right_lo), skip_group_check=True)
                return mm

            HIGHS, LOW_HIGH, HIGH_LOW = (left_hi, right_hi), (left_lo, right_hi), (left_hi, right_lo)
            PARTS = (HIGHS, HIGH_LOW) if wide is not None else (HIGHS, LOW_HIGH, HIGH_LOW)

            def low_products(k):
                with eng.If(low_counts > 0):
                    for n0 in (0, 512):
                        for t in range(KTS):
                            product(k, 0, t, n0, (LOW_HIGH,))

            def products(i, k, s):
                eng.wait_ge(started, 5)
                eng.wait_ge(hi_ready, S * i + s + 3)
                eng.wait_ge(lo_ready, S * i + s + 3)
                if s == 0:
                    eng.wait_ge(y_ready, i + 1)
                for n0 in (0, 512):
                    for t in range(kts[s]):
                        if wide is not None and n0 == 512 and t == kts[s] - 1:
                            low_products(k)
                        mm = product(k, s, t, n0, PARTS)
                mm.then_inc(multiplied, 1)

            for s in range(S):
                transposes(0, 0, 0, s)
            places = [(s, t) for s in range(S) for t in range(kts[s])]
            for n in range(KTS + LAG):
                if n == 1:
                    for s in range(S):
                        transposes(1, 0, 1, s)
                for k, m in ((0, n), (1, n - LAG)):
                    if not 0 <= m < KTS:
                        continue
                    s, t = places[m]
                    if t == 0:
                        eng.wait_ge(started, 5)
                        eng.wait_ge(hi_ready, S * k + s + 3)
                        eng.wait_ge(lo_ready, S * k + s + 3)
                    eng.wait_ge(right_hi_ready, m + 1)
                    eng.wait_ge(right_lo_ready, m + 1)
                    product(k, s, t, 0, PARTS)
                    if wide is not None and m == KTS - 1:
                        low_products(k)
                    mm = product(k, s, t, 512, PARTS)
                    if k == 0 and t == kts[s] - 1:
                        mm.then_inc(multiplied, 1)
                    if k == 1 and m == KTS - 1:
                        mm.then_inc(multiplied, S)
                if n == KTS - 1:
                    for s in range(S):
                        transposes(2, 1, 0, s)

            with eng.Fori(1, NT // 2 - 1) as j:
                for k in range(2):
                    i = 2 * j + k
                    for s in range(S):
                        transposes(i + 1, (j, j + 1)[k], 1 - k, s)
                    for s in range(S):
                        products(i, k, s)
            for s in range(S):
                transposes(NT - 1, NT // 2 - 1, 1, s)
            for k in range(2):
                for s in range(S):
                    products(NT - 2 + k, k, s)

        @block.vector
        def _(eng):
            eng.sem_inc(started, 1)
            eng.sem_inc(lo_ready, 2)
            eng.sem_inc(y_ready, 2)
            eng.sem_inc(y_left[0], 16)
            eng.sem_inc(y_left[1], 16)
            if out_after is not None:
                eng.sem_inc(y2_ready, 2)
                eng.sem_inc(y2_left[0], 16)
                eng.sem_inc(y2_left[1], 16)

            def right_low(n):
                eng.wait_ge(right_hi_ready, n + 1)
                eng.tensor_tensor(right_lo[:, n, :], right_in[:, n % RB, :], right_hi[:, n, :].bitcast(F32), ALU.subtract)\
                   .then_inc(right_lo_ready, 1)

            def low(i, k, s):
                kind, kt, q, b = sources[s][0], kts[s], (k * S + s) % 2, k * S + s
                whole = {"rows": turn, "turned": left_in}.get(kind)
                eng.wait_ge(started, 5)
                eng.wait_ge(hi_ready, S * i + s + 3)
                if whole is not None:
                    eng.tensor_tensor(left_lo[:, b, 0:kt * P], whole[:, q, 0:kt * P],
                                      left_hi[:, b, 0:kt * P].bitcast(F32), ALU.subtract).then_inc(lo_ready, 1)
                else:
                    eng.tensor_tensor(left_lo[:, b, :].rearrange("p (t n) -> p t n", t=kt),
                                      resident[:, :, bass.ds(i * P, P)],
                                      left_hi[:, b, :].rearrange("p (t n) -> p t n", t=kt).bitcast(F32),
                                      ALU.subtract).then_inc(lo_ready, 1)

            def epilogue(i, j, k):
                m = 0
                yk = y[:, k, :]
                cur = acc[:, k, :]
                r = 0

                def link(ins):
                    nonlocal m
                    m += 1
                    if m > LINKS:
                        ins.then_inc(y_ready, 1)
                        return
                    ins.then_inc(chain, 1)
                    due = eng.to_reg(i * LINKS + m) if not isinstance(i, int) else i * LINKS + m
                    eng.wait_ge(started, 5)
                    eng.wait_ge(chain, due)

                eng.wait_ge(started, 5)
                eng.wait_ge(multiplied, S * i + 3 * S)
                eng.wait_ge(y_left[k], 16 * j + 16)
                if R:
                    eng.wait_ge(row_landed[k], 16 * R * (j + 1))
                if bias is not None:
                    eng.wait_ge(bias_in, 16)
                if add_first is not None:
                    link(eng.tensor_tensor(yk, cur, row_in[:, k, r, :], ALU.add))
                    cur, r = yk, r + 1
                if scale is not None and bias is not None:
                    link(eng.scalar_tensor_tensor(out=yk, in0=cur, scalar=scale[:, bass.ds(i, 1)], in1=bias_b[:, :],
                                                  op0=ALU.mult, op1=ALU.add))
                    cur = yk
                elif scale is not None:
                    link(eng.tensor_scalar(yk, cur, scale[:, bass.ds(i, 1)], None, ALU.mult))
                    cur = yk
                elif bias is not None:
                    link(eng.tensor_tensor(yk, cur, bias_b[:, :], ALU.add))
                    cur = yk
                if relu:
                    link(eng.tensor_scalar(yk, cur, 0.0, None, ALU.max))
                if add is not None:
                    link(eng.tensor_tensor(yk, cur, row_in[:, k, r, :], ALU.add))
                    cur, r = yk, r + 1
                if norm:
                    eng.bn_stats(stats[:, 0, :], yk[:, 0:512]).then_inc(chain, 1)
                    link(eng.bn_stats(stats[:, 1, :], yk[:, 512:1024]))
                    m += 1
                    due = eng.to_reg(i * LINKS + m) if not isinstance(i, int) else i * LINKS + m
                    eng.wait_ge(started, 5)
                    eng.wait_ge(chain, due)
                    link(eng.bn_aggr(mean_var[:, :], stats[:, :, :].rearrange("p a b -> p (a b)")))
                    eng.tensor_scalar(var_eps[:, :], mean_var[:, 1:2], LN_EPS, None, ALU.add).then_inc(eps_added, 1)
                    eng.wait_ge(started, 5)
                    eng.wait_ge(rooted, i + 1)
                    link(eng.reciprocal(rstd[:, :], std[:, :]))
                    eng.tensor_scalar(yk, yk, mean_var[:, 0:1], rstd[:, 0:1], ALU.subtract, ALU.mult).then_inc(y_ready, 1)
                assert m == OPS + 4 * norm
                if out_after is not None:
                    eng.wait_ge(started, 5)
                    eng.wait_ge(y_ready, i + 3)
                    eng.wait_ge(y2_left[k], 16 * j + 16)
                    eng.tensor_tensor(y2[:, k, :], yk, row_in[:, k, r, :], ALU.add).then_inc(y2_ready, 1)

            for s in range(S):
                low(0, 0, s)
            for n in range(EARLY):
                right_low(n)
            for s in range(S):
                low(1, 1, s)
            for n in range(EARLY, KTS):
                right_low(n)
            with eng.Fori(0, NT // 2 - 1) as j:
                for k in range(2):
                    i = 2 * j + k
                    for s in range(S):
                        low(i + 2, k, s)
                    epilogue(i, j, k)
            epilogue(NT - 2, NT // 2 - 1, 0)
            epilogue(NT - 1, NT // 2 - 1, 1)


def batch_norm_phase(nc, sem, g_tab, gamma, beta, held):
    with ExitStack() as ctx:
        def sb(name, shape):
            return ctx.enter_context(nc.sbuf_tensor("bn_" + name, shape, F32))

        g_in = sb("g_in", [P, NT, D])
        ident = sb("ident", [P, P])
        gam = sb("gam", [P, KT])
        bet = sb("bet", [P, KT])
        PIECE = -(-N_NODES // 3)
        stats = sb("stats", [P, KT, 3, 6])
        mean_var = sb("mean_var", [P, KT, 2])
        var_eps = sb("var_eps", [P, KT])
        std = sb("std", [P, KT])
        factor = sb("factor", [P, KT])
        offset = sb("offset", [P, KT])
        turn = ctx.enter_context(nc.psum_tensor("bn_turn", [P, 2, 3 * 512], F32))

        loaded = [sem(f"bn_loaded{i}") for i in range(NT)]
        consts_in = sem("bn_consts_in")
        filled = sem("bn_filled")
        ident_ready = sem("bn_ident_ready")
        turned = sem("bn_turned")
        copied = sem("bn_copied")
        stated = sem("bn_stated")
        var_ready = sem("bn_var_ready")
        rooted = sem("bn_rooted")
        chain = sem("bn_chain")
        affine_ready = sem("bn_affine_ready")
        normed = sem("bn_normed")

        block = ctx.enter_context(nc.Block())

        @block.sync
        def _(eng):
            for i in range(NT):
                eng.dma_start(g_in[:, i, :], g_tab[i * P:(i + 1) * P, :]).then_inc(loaded[i], 16)
            eng.dma_start(gam[:, :], gamma.rearrange("(k p) -> p k", p=P),
                          allow_slow_non_contiguous=True).then_inc(consts_in, 16)
            eng.dma_start(bet[:, :], beta.rearrange("(k p) -> p k", p=P),
                          allow_slow_non_contiguous=True).then_inc(consts_in, 16)

        @block.gpsimd
        def _(eng):
            eng.memset(ident[:, :], 0.0).then_inc(filled, 1)
            eng.wait_ge(filled, 1)
            eng.affine_select(out=ident[:, :], in_=ident[:, :], compare_op=ALU.not_equal, fill=1.0, base=0,
                              pattern=[[-1, P]], channel_multiplier=1).then_inc(ident_ready, 1)

        @block.tensor
        def _(eng):
            eng.wait_ge(ident_ready, 1)
            for i in range(NT):
                eng.wait_ge(loaded[i], 16)
            for t in range(KT):
                if t >= 2:
                    eng.wait_ge(copied, t - 1)
                for i in range(NT):
                    mm = eng.transpose(turn[:, t % 2, i * P:(i + 1) * P], g_in[:, i, t * P:(t + 1) * P], ident[:, :])
                mm.then_inc(turned, 1)

        @block.scalar
        def _(eng):
            for t in range(KT):
                eng.wait_ge(turned, t + 1)
                eng.activation(held[:, t, :], turn[:, t % 2, 0:NPAD], ACT.Copy).then_inc(copied, 1)
            eng.wait_ge(var_ready, 1)
            eng.activation(std[:, :], var_eps[:, :], ACT.Sqrt).then_inc(rooted, 1)
            eng.wait_ge(affine_ready, 1)
            for t in range(KT):
                eng.activation(held[:, t, :], held[:, t, :], ACT.Relu, scale=factor[:, t:t + 1],
                               bias=offset[:, t:t + 1]).then_inc(normed, 1)
            eng.wait_ge(normed, KT)

        @block.vector
        def _(eng):
            for t in range(KT):
                eng.wait_ge(copied, t + 1)
                for q in range(3):
                    eng.bn_stats(stats[:, t, q, :], held[:, t, q * PIECE:min((q + 1) * PIECE, N_NODES)])\
                       .then_inc(stated, 1)
                eng.wait_ge(stated, 3 * t + 3)
                eng.bn_aggr(mean_var[:, t, :], stats[:, t, :, :].rearrange("p q s -> p (q s)")).then_inc(chain, 1)
            eng.wait_ge(chain, KT)
            eng.tensor_scalar(var_eps[:, :], mean_var[:, :, 1], LN_EPS, None, ALU.add).then_inc(var_ready, 1)
            eng.wait_ge(rooted, 1)
            eng.reciprocal(factor[:, :], std[:, :]).then_inc(chain, 1)
            eng.wait_ge(consts_in, 32)
            eng.wait_ge(chain, KT + 1)
            eng.tensor_tensor(factor[:, :], factor[:, :], gam[:, :], ALU.mult).then_inc(chain, 1)
            eng.wait_ge(chain, KT + 2)
            eng.tensor_tensor(offset[:, :], mean_var[:, :, 0], factor[:, :], ALU.mult).then_inc(chain, 1)
            eng.wait_ge(chain, KT + 3)
            eng.tensor_tensor(offset[:, :], bet[:, :], offset[:, :], ALU.subtract).then_inc(affine_ready, 1)


def build(nc, stop, x, src, dst, edge_weight, positions, rms_w, w_down, wl, wr, att, w_up,
          w_self0, w_neigh0, b0, w_self1, w_neigh1, b1, sparse_bias, w1, c1, gamma, beta, w2, c2, out):
    taken = []

    def sem(name):
        taken.append(nc.alloc_semaphore(name=name))
        return taken[-1]

    def phase(f, *args, **kwargs):
        f(nc, sem, *args, **kwargs)
        nc.clear_and_free_semaphores(taken)
        nc.all_engine_barrier()
        taken.clear()

    with ExitStack() as ctx:
        def scratch(name, shape, dt=F32):
            return nc.dram_tensor(name, shape, dt, kind="Internal").ap()

        edge_tab = scratch("edge_tab", [NC * P, 4])
        xl_tab = scratch("xl_tab", [NPAD, XW])
        xr_tab = scratch("xr_tab", [NPAD, HID])
        self_tab = scratch("self_tab", [P, NT, HEADS])
        tile_tab = scratch("tile_tab", [1, NG], I32)
        adj_tab = scratch("adj_tab", [NPAD, NPAD])
        wt_tab = scratch("wt_tab", [D, D])
        o_tab = scratch("o_tab", [NPAD, HID])
        rows = {n: scratch(n, [NPAD, D]) for n in ("x1", "mean1", "h1", "mean2", "x2", "x3", "x3p", "s1", "g1", "s2")}
        deg_inv = ctx.enter_context(nc.sbuf_tensor("deg_inv", [P, NT], F32))
        wide = ctx.enter_context(nc.sbuf_tensor("wide", [1, 1], I32))
        deg_rsqrt = ctx.enter_context(nc.sbuf_tensor("deg_rsqrt", [P, NT], F32))

        phase(prepare_phase, x, src, dst, edge_weight, rms_w, w_down, wl, wr, att,
                      edge_tab, xl_tab, self_tab, xr_tab, tile_tab)
        phase(edge_phase, edge_tab, xl_tab, self_tab, xr_tab, tile_tab, att, adj_tab, wt_tab, o_tab,
                   deg_inv, deg_rsqrt, wide)

        phase(dense_phase, "up_", [("rows", o_tab, w_up)], add=x, norm=True, out=out if stop == 1 else rows["x1"])
        if stop == 1:
            return
        phase(dense_phase, "m1_", [("turned", adj_tab, rows["x1"])], wide=wide, scale=deg_inv, out=rows["mean1"])
        phase(dense_phase, "h1_", [("rows", rows["x1"], w_self0), ("rows", rows["mean1"], w_neigh0)],
                    bias=b0, relu=True, out=rows["h1"])
        phase(dense_phase, "m2_", [("turned", adj_tab, rows["h1"])], wide=wide, scale=deg_inv, out=rows["mean2"])
        phase(dense_phase, "x2_", [("rows", rows["h1"], w_self1), ("rows", rows["mean2"], w_neigh1)],
                    bias=b1, add=rows["x1"], norm=True, out=out if stop == 2 else rows["x2"])
        if stop == 2:
            return
        phase(dense_phase, "x3_", [("rows", rows["x2"], wt_tab)], bias=sparse_bias, add=rows["x2"], norm=True,
                    out=out if stop == 3 else rows["x3"], add_after=positions, out_after=rows["x3p"])
        if stop == 3:
            return
        phase(dense_phase, "s1_", [("rows", rows["x3p"], w1)], scale=deg_rsqrt, out=rows["s1"])
        phase(dense_phase, "g1_", [("turned", adj_tab, rows["s1"])], add_first=rows["s1"], wide=wide, scale=deg_rsqrt,
                    bias=c1, out=rows["g1"])
        with nc.sbuf_tensor("held", [P, KT, NPAD], F32) as held:
            phase(batch_norm_phase, rows["g1"], gamma, beta, held)
            phase(dense_phase, "s2_", [("held", None, w2)], resident=held, scale=deg_rsqrt, out=rows["s2"])
        phase(dense_phase, "g2_", [("turned", adj_tab, rows["s2"])], add_first=rows["s2"], wide=wide, scale=deg_rsqrt,
                    bias=c2, relu=True, add=rows["x3"], norm=True, out=out)


_INS = ["x", "src", "dst", "edge_weight", "positions", "L0_gnn_rms_w", "L0_gnn_W_down", "L0_gnn_Wl", "L0_gnn_Wr",
        "L0_gnn_att", "L0_gnn_W_up", "L1_gnn_W_self0", "L1_gnn_W_neigh0", "L1_gnn_b0", "L1_gnn_W_self1",
        "L1_gnn_W_neigh1", "L1_gnn_b1", "L2_gnn_bias", "L3_gnn_W1", "L3_gnn_b1", "L3_gnn_gamma", "L3_gnn_beta",
        "L3_gnn_W2", "L3_gnn_b2"]
STOP = 4


def kernel(**inputs):
    import numpy as _np
    import concourse.bacc as _bacc
    from concourse import mybir as _mybir
    from concourse.bass_utils import run_bass_kernel_spmd as _run

    pos = _np.arange(N_NODES, dtype=_np.float32)[:, None]
    div = _np.exp(_np.arange(0, D, 2, dtype=_np.float32) * _np.float32(-_np.log(10000.0) / D))
    ang = (pos * div).astype(_np.float32)
    positions = _np.zeros((NPAD, D), _np.float32)
    positions[:N_NODES] = _np.stack([_np.sin(ang), _np.cos(ang)], axis=-1).reshape(N_NODES, D)

    nc = _bacc.Bacc("TRN2", target_bir_lowering=False, num_devices=1)
    arrays, args = {}, []
    for name in _INS:
        if name == "positions":
            a = positions
        else:
            a = _np.ascontiguousarray(inputs[name])
        if name == "x":
            a = _np.pad(a, ((0, NPAD - N_NODES), (0, 0)))
        arrays[f"in_{name}_dram"] = a
        args.append(nc.dram_tensor(f"in_{name}_dram", a.shape, _mybir.dt.from_np(a.dtype), kind="ExternalInput").ap())
    args.append(nc.dram_tensor("out_0_dram", (N_NODES, D), _mybir.dt.float32, kind="ExternalOutput").ap())
    build(nc, STOP, *args)
    r = _run(nc, [arrays], core_ids=[0])
    return r.results[0]["out_0_dram"]
```
